# Optimizing a Trainium2 kernel written in Bass

```python
import numpy as np
import jax
import jax.numpy as jnp

def _softmax(x, axis=-1):
    return jax.nn.softmax(x, axis=axis)

def _gelu(x):
    return jax.nn.gelu(x, approximate=True)

def _silu(x):
    return jax.nn.silu(x)

def _sigmoid(x):
    return jax.nn.sigmoid(x)

def _layernorm(x, axis=-1, eps=1e-05):
    m = jnp.mean(x, axis=axis, keepdims=True)
    v = jnp.var(x, axis=axis, keepdims=True)
    return (x - m) / jnp.sqrt(v + eps)

def _scatter_add(tgt, idx, src, axis=0):
    return tgt.at[idx].add(src)

def _segment_sum(src, seg, n):
    return jax.ops.segment_sum(src, seg, n)
kernel_name = 'mk_gnn_preln_d2_gnn_r8_57db95'

def setup_inputs(seed: int=0):
    np.random.seed(seed)
    _w = jnp.asarray

    def _rec_inputs():
        import jax
        import jax.numpy as jnp
        _gk = jax.random.key(seed)
        x = -0.000202 + 1 * jax.random.normal(jax.random.fold_in(_gk, 1), (12500, 64), jnp.float32)
        src = jax.random.randint(jax.random.fold_in(_gk, 2), (200000,), 0, 12500, jnp.int32)
        dst = jax.random.randint(jax.random.fold_in(_gk, 3), (200000,), 0, 12500, jnp.int32)
        _o = jnp.argsort(dst, stable=True)
        src = src[_o]
        dst = dst[_o]
        edge_attr_2 = -0.000414295 + 0.999828 * jax.random.normal(jax.random.fold_in(_gk, 13), (200000, 2), jnp.float32)
        edge_attr_64 = -5.16925e-05 + 1.00005 * jax.random.normal(jax.random.fold_in(_gk, 14), (200000, 64), jnp.float32)
        return (x, src, dst, edge_attr_2, edge_attr_64)
    x, src, dst, edge_attr_2, edge_attr_64 = _rec_inputs()

    def _L0_gnn_setup():
        import jax, jax.numpy as jnp
        import numpy as np
        N_NODES = 12500
        N_EDGES = 200000
        D = 64
        HIDDEN = 128
        D_OUT = 64
        key = jax.random.key(seed)
        ks = jax.random.split(key, 8)
        x = jax.random.normal(ks[0], (N_NODES, D), dtype=jnp.float32)
        edge_index = jax.random.randint(ks[1], (2, N_EDGES), 0, N_NODES, dtype=jnp.int64)
        edge_attr = jax.random.normal(ks[2], (N_EDGES, D), dtype=jnp.float32)
        u = jax.random.normal(ks[3], (1, D), dtype=jnp.float32)
        batch = jnp.zeros((N_NODES,), dtype=jnp.int64)
        s1 = 1.0 / np.sqrt(2 * D)
        s2 = 1.0 / np.sqrt(HIDDEN)
        W1 = jax.random.uniform(ks[4], (2 * D, HIDDEN), jnp.float32, -s1, s1)
        b1 = jax.random.uniform(ks[5], (HIDDEN,), jnp.float32, -s1, s1)
        W2 = jax.random.uniform(ks[6], (HIDDEN, D_OUT), jnp.float32, -s2, s2)
        b2 = jax.random.uniform(ks[7], (D_OUT,), jnp.float32, -s2, s2)
        return {'x': x, 'edge_index': edge_index, 'edge_attr': edge_attr, 'u': u, 'batch': batch, 'W1': W1, 'b1': b1, 'W2': W2, 'b2': b2}
    _L0_gnn_all = _L0_gnn_setup()
    _L0_gnn_in = {k: v for k, v in _L0_gnn_all.items() if k in ('u', 'W1', 'b1', 'W2', 'b2')}
    del _L0_gnn_all

    def _L1_gnn_setup():
        import jax, jax.numpy as jnp
        import numpy as np
        K = 3
        SLOPE = 0.01
        N_NODES = 6250
        N_EDGES = 100000
        D_IN = 64
        D_OUT = 64
        E_DIM = 2

        def _moments(z_e, Wm_list):
            moms = [z_e]
            mu = z_e.mean(axis=0, keepdims=True)
            for k in range(2, K + 1):
                mk = jnp.mean((z_e - mu) ** k, axis=0)
                mk = jnp.sign(mk) * jnp.abs(mk) ** (1.0 / k)
                moms.append(mk @ Wm_list[k - 2].T)
            return moms
        key = jax.random.key(seed)
        ks = jax.random.split(key, 10)
        s = 0.1
        return {'h': jax.random.normal(ks[0], (N_NODES, D_IN), dtype=jnp.float32), 'e': jax.random.normal(ks[1], (N_EDGES, E_DIM), dtype=jnp.float32), 'src': jax.random.randint(ks[2], (N_EDGES,), 0, N_NODES), 'dst': jax.random.randint(ks[3], (N_EDGES,), 0, N_NODES), 'W_fc': jax.random.normal(ks[4], (D_OUT, D_IN), dtype=jnp.float32) * s, 'W_attn': jax.random.normal(ks[5], (1, 2 * D_OUT * K + E_DIM), dtype=jnp.float32) * s, 'W_edge': jax.random.normal(ks[6], (E_DIM, E_DIM), dtype=jnp.float32) * s, 'W_e2n': jax.random.normal(ks[7], (D_OUT, E_DIM), dtype=jnp.float32) * s, 'W_m1': jax.random.normal(ks[8], (D_OUT, D_OUT), dtype=jnp.float32) * s, 'W_m2': jax.random.normal(ks[9], (D_OUT, D_OUT), dtype=jnp.float32) * s}
    _L1_gnn_all = _L1_gnn_setup()
    _L1_gnn_in = {k: v for k, v in _L1_gnn_all.items() if k in ('W_fc', 'W_attn', 'W_edge', 'W_e2n', 'W_m1', 'W_m2')}
    del _L1_gnn_all
    return {'x': x, 'src': src, 'dst': dst, 'edge_attr_2': edge_attr_2, 'edge_attr_64': edge_attr_64, 'L0_gnn_u': _L0_gnn_in['u'], 'L0_gnn_W1': _L0_gnn_in['W1'], 'L0_gnn_b1': _L0_gnn_in['b1'], 'L0_gnn_W2': _L0_gnn_in['W2'], 'L0_gnn_b2': _L0_gnn_in['b2'], 'L1_gnn_W_fc': _L1_gnn_in['W_fc'], 'L1_gnn_W_attn': _L1_gnn_in['W_attn'], 'L1_gnn_W_edge': _L1_gnn_in['W_edge'], 'L1_gnn_W_e2n': _L1_gnn_in['W_e2n'], 'L1_gnn_W_m1': _L1_gnn_in['W_m1'], 'L1_gnn_W_m2': _L1_gnn_in['W_m2']}

def reference(x, src, dst, edge_attr_2, edge_attr_64, L0_gnn_u, L0_gnn_W1, L0_gnn_b1, L0_gnn_W2, L0_gnn_b2, L1_gnn_W_fc, L1_gnn_W_attn, L1_gnn_W_edge, L1_gnn_W_e2n, L1_gnn_W_m1, L1_gnn_W_m2):
    import jax
    import jax.numpy as jnp

    def _L0_gnn_ref(x, edge_index, edge_attr, u, batch, W1, b1, W2, b2):
        import jax, jax.numpy as jnp
        import numpy as np
        N_NODES = 12500
        N_EDGES = 200000
        D = 64
        HIDDEN = 128
        D_OUT = 64
        row = edge_index[0]
        aggr_msg = jax.ops.segment_sum(edge_attr, row, num_segments=x.shape[0])
        h = jnp.concatenate([x, aggr_msg], axis=-1)
        h = jax.nn.relu(h @ W1 + b1)
        out = h @ W2 + b2
        return out

    def _L1_gnn_ref(h, e, src, dst, W_fc, W_attn, W_edge, W_e2n, W_m1, W_m2):
        import jax, jax.numpy as jnp
        import numpy as np
        K = 3
        SLOPE = 0.01
        N_NODES = 6250
        N_EDGES = 100000
        D_IN = 64
        D_OUT = 64
        E_DIM = 2

        def _moments(z_e, Wm_list):
            moms = [z_e]
            mu = z_e.mean(axis=0, keepdims=True)
            for k in range(2, K + 1):
                mk = jnp.mean((z_e - mu) ** k, axis=0)
                mk = jnp.sign(mk) * jnp.abs(mk) ** (1.0 / k)
                moms.append(mk @ Wm_list[k - 2].T)
            return moms
        N = h.shape[0]
        D = W_fc.shape[0]
        z = h @ W_fc.T
        z_src = z[src]
        z_dst = z[dst]
        ex = e @ W_edge.T
        wm = [W_m1, W_m2]
        src_m = _moments(z_src, wm)
        dst_m = _moments(z_dst, wm)
        wa = W_attn[0]
        blk = [wa[i * D:(i + 1) * D] for i in range(2 * K)]
        w_e = wa[2 * K * D:]
        a = z_src @ blk[0] + z_dst @ blk[K] + ex @ w_e
        for k in range(1, K):
            a = a + src_m[k] @ blk[k] + dst_m[k] @ blk[K + k]
        att = jnp.where(a > 0, a, SLOPE * a)
        m = jax.ops.segment_max(att, dst, num_segments=N)
        expv = jnp.exp(att - m[dst])
        denom = jax.ops.segment_sum(expv, dst, num_segments=N)
        w = expv / denom[dst]
        ez = ex @ W_e2n.T
        msg = w[:, None] * (z_src + ez)
        return jax.ops.segment_sum(msg, dst, num_segments=N)
    edge_index = jnp.stack([src, dst])
    batch0 = jnp.zeros((12500,), jnp.int32)
    h = jnp.maximum(_layernorm(x, axis=-1), 0.0)
    x = x + _L0_gnn_ref(h, edge_index, edge_attr_64, L0_gnn_u, batch0, L0_gnn_W1, L0_gnn_b1, L0_gnn_W2, L0_gnn_b2)
    h = jnp.maximum(_layernorm(x, axis=-1), 0.0)
    x = x + _L1_gnn_ref(h, edge_attr_2, src, dst, L1_gnn_W_fc, L1_gnn_W_attn, L1_gnn_W_edge, L1_gnn_W_e2n, L1_gnn_W_m1, L1_gnn_W_m2)
    return x

_drawn_inputs = setup_inputs


def setup_inputs(seed=0):
    import zlib

    import numpy as np

    out = dict(_drawn_inputs(seed))
    spreads = {}
    factors = {'edge_attr_2': 8.0,
     'L0_gnn_b1': 2.902,
     'L1_gnn_W_attn': 3.521,
     'L1_gnn_W_edge': 8.0,
     'L1_gnn_W_e2n': 8.0,
     'L1_gnn_W_m1': 5.141,
     'L1_gnn_W_m2': 7.962}
    for name, (base, spread) in spreads.items():
        noise = np.random.default_rng([zlib.crc32(name.encode()), seed]).standard_normal(out[name].shape)
        drawn = base * np.exp(spread * noise) if base else spread * noise
        out[name] = jnp.asarray(drawn.astype(out[name].dtype))
    for name, factor in factors.items():
        out[name] = (out[name] * factor).astype(out[name].dtype)
    return out
```

```python
import concourse.bass as bass
from concourse import mybir
from contextlib import ExitStack

ALU = mybir.AluOpType
ACT = mybir.ActivationFunctionType
X_AXIS = mybir.AxisListType.X
F32 = mybir.dt.float32
BF16 = mybir.dt.bfloat16
I32 = mybir.dt.int32

P = 128
NODES, EDGES, D, HID = 12500, 200000, 64, 128
G = 8
ME = P * G
NM = -(-EDGES // ME)
LAST0 = EDGES - ME
DUP = (NM * ME - EDGES) // G
NT = NM * G
NB = -(-NODES // P)
NPAD = P * NB
NROWS = NPAD + P
FULL = NODES // NB
REST = NODES - FULL * NB
AW = D + 1
ZW = D + 1
RW = D + 4
TW = RW + 1
CH = 7
NC = NB // CH
EPS = 1e-5
SLOPE = 0.01
OFF = -1e30
FLOOR = -1e20
assert NM % 2 == 0 and (NM * ME - EDGES) % G == 0 and NB % CH == 0 and 0 < REST < NB


class Chain:

    def __init__(self, eng, sem, base=0):
        self.eng, self.sem, self.base, self.k = eng, sem, base, 0

    def __call__(self, ins):
        self.k += 1
        ins.then_inc(self.sem, 1)
        self.eng.wait_ge(self.sem, self.base + self.k)


def gnn_kernel(nc, x, src, dst, e2, e64, W1, b1, W2, b2, W_fc, W_attn, W_edge, W_e2n, W_m1, W_m2, out):
    with ExitStack() as ctx:
        def sb(name, shape, dt=F32):
            return ctx.enter_context(nc.sbuf_tensor(name, shape, dt))

        def pb(name, shape, dt=F32):
            return ctx.enter_context(nc.psum_tensor(name, shape, dt))

        def sem(name):
            return ctx.enter_context(nc.semaphore(name))

        acc_dram = [nc.dram_tensor(f"acc_dram{k}", (NROWS, AW), F32, kind="Internal").ap() for k in range(G)]
        z_dram = nc.dram_tensor("z_dram", (NPAD, ZW), F32, kind="Internal").ap()
        t_dram = nc.dram_tensor("t_dram", (1, NROWS), F32, kind="Internal").ap()
        tab_dram = nc.dram_tensor("tab_dram", (NROWS, TW), F32, kind="Internal").ap()

        ident = sb("ident", [P, P])
        iota_f = sb("iota_f", [P, P])
        tri = sb("tri", [P, P])
        ones_f = sb("ones_f", [P, P])
        zeros_b = sb("zeros_b", [P, P], BF16)
        dummy_row = sb("dummy_row", [P, 1])
        w1_sb = sb("w1_sb", [P, HID])
        b1_sb = sb("b1_sb", [P, 1])
        w2_sb = sb("w2_sb", [P, D])
        b2_sb = sb("b2_sb", [P, D])
        wfc_sb = sb("wfc_sb", [D, D])
        blk_sb = sb("blk_sb", [D, 6])
        we_sb = sb("we_sb", [2, 1])
        wedge_sb = sb("wedge_sb", [2, 2])
        we2nT_sb = sb("we2nT_sb", [2, D])
        wm_sb = sb("wm_sb", [D, 2, D])
        wz_sb = sb("wz_sb", [D, D + 2])
        q_sb = sb("q_sb", [P, 2])
        r_sb = sb("r_sb", [P, 2, D])
        v_sb = sb("v_sb", [P, 4, D])
        src_i = sb("src_i", [P, NT + 2 * G], I32)
        dst_i = sb("dst_i", [P, NT], I32)
        dst_f = sb("dst_f", [P, NT])
        dst_p = sb("dst_p", [P, NT])
        dst_j = sb("dst_j", [P, NT])
        e2_sb = sb("e2_sb", [P, NT, 2])
        ee_sb = sb("ee_sb", [P, NT])
        x_sb = sb("x_sb", [P, NB, D])
        d_sb = sb("d_sb", [P, NB, D])
        z_sb = sb("z_sb", [P, NB, D + 2])
        work = sb("work", [P, max((NB + 1) * TW, 2 * G * CH * AW)])
        cnt_sb = sb("cnt_sb", [P, 2, NB])
        mean_sb = sb("mean_sb", [P, NB])
        var_sb = sb("var_sb", [P, NB])
        rstd_sb = sb("rstd_sb", [P, NB])
        t_sb = sb("t_sb", [P, NB])
        ea_sb = sb("ea_sb", [P, 2, G * D])
        one_sb = sb("one_sb", [P, 2])
        srcf = sb("srcf", [P, 2, G])
        ohp = sb("ohp", [P, 2, 4, P], BF16)
        ohj = sb("ohj", [P, 2, 4, NB], BF16)
        same = sb("same", [P, 2, 4, P])
        junk = sb("junk", [P, P])
        before = sb("before", [P, 2, G])
        todummy = sb("todummy", [P, 2, G])
        idx = sb("idx", [P, 2, G], I32)
        y_sb = sb("y_sb", [P, 2, G * AW])
        zg = sb("zg", [P, 2, G, RW])
        s_sb = sb("s_sb", [P, G])
        dloc = sb("dloc", [P, G])
        big_a = sb("big_a", [P, G, P])
        big_b = sb("big_b", [P, G, P])
        gmax = sb("gmax", [P, P])
        trow = sb("trow", [P, P])
        tab = sb("tab", [P, TW])
        mloc = sb("mloc", [P, 1])
        mnew = sb("mnew", [P, 1])
        rescale = sb("rescale", [P, 1])
        lo_all = sb("lo_all", [P, NM])
        hi_all = sb("hi_all", [P, NM])
        cum_f = sb("cum_f", [P, NM + 1])
        cum_i = sb("cum_i", [P, NM + 1], I32)
        base_i = sb("base_i", [P, NM], I32)
        tmp_m = sb("tmp_m", [P, NM])
        tmp_i = sb("tmp_i", [P, NM], I32)
        sums = sb("sums", [P, 2, D])
        mom = sb("mom", [P, 4, D])
        mabs = sb("mabs", [P, 4, D])
        msign = sb("msign", [P, 4, D])
        c_sb = sb("c_sb", [P, 1])

        banks = [pb(f"bank{i}", [P, 512]) for i in range(8)]

        s_const = sem("s_const")
        s_work = sem("s_work")
        s_tab = [sem(f"s_tab{k}") for k in range(G)]
        s_zero = [sem(f"s_zero{k}") for k in range(G)]
        s_room = sem("s_room")
        s_w = sem("s_w")
        s_src = sem("s_src")
        s_dst = sem("s_dst")
        s_e2 = sem("s_e2")
        s_x = sem("s_x")
        s_ea = [sem(f"s_ea{k}") for k in range(2)]
        s_pad = sem("s_pad")
        s_stage = sem("s_stage")
        s_srcb = sem("s_srcb")
        s_oh = sem("s_oh")
        s_oh_used = sem("s_oh_used")
        s_same = sem("s_same")
        s_y = sem("s_y")
        s_ysb = sem("s_ysb")
        s_idx = sem("s_idx")
        s_held = [sem(f"s_held{k}") for k in range(4)]
        s_pool = sem("s_pool")
        s_dve = sem("s_dve")
        s_dve1 = sem("s_dve1")
        s_dve2 = sem("s_dve2")
        s_dve3 = sem("s_dve3")
        s_dve4 = sem("s_dve4")
        s_dve5 = sem("s_dve5")
        s_act = sem("s_act")
        s_prep = sem("s_prep")
        s_prep_sb = sem("s_prep_sb")
        s_cnt = sem("s_cnt")
        s_dsub = sem("s_dsub")
        s_sq = sem("s_sq")
        s_std = sem("s_std")
        s_vv = sem("s_vv")
        s_rstd = sem("s_rstd")
        s_acc = [sem(f"s_acc{k}") for k in range(2)]
        s_cat = sem("s_cat")
        s_agg = sem("s_agg")
        s_tr = sem("s_tr")
        s_trs = sem("s_trs")
        s_hid = sem("s_hid")
        s_hids = sem("s_hids")
        s_o = sem("s_o")
        s_x1 = sem("s_x1")
        s_zp = sem("s_zp")
        s_z = sem("s_z")
        s_zst = sem("s_zst")
        s_part = sem("s_part")
        s_psum = sem("s_psum")
        s_mom = sem("s_mom")
        s_root = sem("s_root")
        s_t = sem("s_t")
        s_tst = sem("s_tst")
        s_tabi = sem("s_tabi")
        s_neg = sem("s_neg")
        s_range = sem("s_range")
        s_win = sem("s_win")
        s_zg = [sem(f"s_zg{k}") for k in range(2)]
        s_zg_used = sem("s_zg_used")
        s_rows = sem("s_rows")
        s_row_free = sem("s_row_free")
        s_mask = sem("s_mask")
        s_lin = sem("s_lin")
        s_gmax = sem("s_gmax")
        s_gT = sem("s_gT")
        s_mnew = sem("s_mnew")
        s_mrow = sem("s_mrow")
        s_sub = sem("s_sub")
        s_exp = sem("s_exp")
        s_agg1 = sem("s_agg1")
        s_tabn = sem("s_tabn")
        s_tabs = sem("s_tabs")
        s_fin = sem("s_fin")
        s_res = sem("s_res")
        s_out = sem("s_out")

        NEDGE_MAIN = (NM - 1) * ME
        NPARTS = 4
        zero_w = (NB + 1) * AW // 3

        def nodes_dma(eng, tile, dram, load, s):
            pairs = [(tile[0:FULL, :, :], dram[0:FULL * NB, :].rearrange("(p b) w -> p b w", p=FULL)),
                     (tile[FULL:FULL + 1, 0:REST, :], dram[FULL * NB:NODES, :].rearrange("(p b) w -> p b w", p=1))]
            for a, b in pairs:
                eng.dma_start(*((a, b) if load else (b, a))).then_inc(s, 16)

        block = ctx.enter_context(nc.Block())

        @block.sync
        def _(sp):
            nc_ = nc.sync
            sp.dma_start(src_i[:, 0:(NM - 1) * G].rearrange("p (m g) -> p m g", g=G),
                         src[0:NEDGE_MAIN].rearrange("(m p g) -> p m g", p=P, g=G)).then_inc(s_src, 16)
            sp.dma_start(src_i[:, (NM - 1) * G:NT], src[LAST0:EDGES].rearrange("(p g) -> p g", g=G)).then_inc(s_src, 16)
            sp.wait_ge(s_work, 1)
            for k in range(G):
                for h in range(3):
                    view = acc_dram[k].rearrange("(p r) c -> p (r c)", p=P)
                    sp.dma_start(view[:, h * zero_w:(h + 1) * zero_w], work[:, 0:zero_w]).then_inc(s_zero[k], 16)
                if k == 1:
                    sp.wait_ge(s_work, 2)
                    nodes_dma(sp, x_sb, x, True, s_x)
                    sp.dma_start(dst_i[:, 0:(NM - 1) * G].rearrange("p (m g) -> p m g", g=G),
                                 dst[0:NEDGE_MAIN].rearrange("(m p g) -> p m g", p=P, g=G)).then_inc(s_dst, 16)
                    sp.dma_start(dst_i[:, (NM - 1) * G:NT],
                                 dst[LAST0:EDGES].rearrange("(p g) -> p g", g=G)).then_inc(s_dst, 16)
            wa = W_attn.rearrange("a n -> n a")
            with nc.allow_non_contiguous_dma(reason="small transposed weights"):
                sp.dma_start(blk_sb[:, :], W_attn[0:1, 0:6 * D].rearrange("a (k d) -> d (a k)", k=6)).then_inc(s_w, 16)
                sp.dma_start(we_sb[:, :], wa[6 * D:6 * D + 2, :]).then_inc(s_w, 16)
                sp.dma_start(we2nT_sb[:, :], W_e2n.rearrange("f i -> i f")).then_inc(s_w, 16)
                sp.dma_start(b1_sb[:, :], b1.rearrange("(p a) -> p a", a=1)).then_inc(s_w, 16)
            sp.dma_start(w1_sb[:, :], W1).then_inc(s_w, 16)
            sp.dma_start(w2_sb[:, :], W2).then_inc(s_w, 16)
            sp.dma_start(b2_sb[:, :], b2.rearrange("(a d) -> a d", a=1).to_broadcast([P, D])).then_inc(s_w, 16)
            sp.dma_start(wfc_sb[:, :], W_fc).then_inc(s_w, 16)
            sp.dma_start(wedge_sb[:, :], W_edge).then_inc(s_w, 16)
            sp.dma_start(wm_sb[:, 0, :], W_m1).then_inc(s_w, 16)
            sp.dma_start(wm_sb[:, 1, :], W_m2).then_inc(s_w, 16)
            sp.dma_start(e2_sb[:, 0:(NM - 1) * G, :].rearrange("p (m g) c -> p m (g c)", g=G),
                         e2[0:NEDGE_MAIN, :].rearrange("(m p g) c -> p m (g c)", p=P, g=G)).then_inc(s_e2, 16)
            sp.dma_start(e2_sb[:, (NM - 1) * G:NT, :],
                         e2[LAST0:EDGES, :].rearrange("(p g) c -> p g c", g=G)).then_inc(s_e2, 16)

            def load_ea(s, m):
                rows = e64[bass.ds(m * ME, ME), :] if not isinstance(m, int) else e64[m * ME:(m + 1) * ME, :]
                sp.dma_start(ea_sb[:, s, :], rows.rearrange("(p g) c -> p (g c)", g=G)).then_inc(s_ea[s], 16)

            sp.wait_ge(s_const, 1)
            load_ea(0, 0)
            load_ea(1, 1)
            with sp.Fori(1, NM // 2 - 1) as it:
                for s in range(2):
                    sp.wait_ge(s_y, it * 4 + 2 * s)
                    load_ea(s, it * 2 + s)
            sp.wait_ge(s_y, 2 * (NM - 2))
            load_ea(0, NM - 2)
            sp.wait_ge(s_y, 2 * (NM - 1))
            sp.dma_start(ea_sb[0:DUP, 1, :], work[0:DUP, 0:G * D]).then_inc(s_pad, 16)
            sp.dma_start(one_sb[0:DUP, 1:2], work[0:DUP, 0:1]).then_inc(s_pad, 16)
            sp.wait_ge(s_pad, 32)
            sp.dma_start(ea_sb[DUP:P, 1, :],
                         e64[LAST0 + DUP * G:EDGES, :].rearrange("(p g) c -> p (g c)", g=G)).then_inc(s_ea[1], 16)

            for k in range(G):
                sp.wait_ge(s_tab[k], 16 * NM)
            with sp.Fori(0, NC // 2) as it:
                for s in range(2):
                    sp.wait_ge(s_agg, it * 2 + s + 1)
                    for k in range(G):
                        view = acc_dram[k][0:NPAD, :].rearrange("(p b) c -> p b c", p=P)
                        sp.dma_start(
                            work[:, s * G * CH * AW:(s + 1) * G * CH * AW].rearrange(
                                "p (k b c) -> p k b c", k=G, b=CH)[:, k, :, :],
                            view[:, bass.ds((it * 2 + s) * CH, CH), :]).then_inc(s_acc[s], 16)
            sp.wait_ge(s_z, NC)
            sp.dma_start(z_dram.rearrange("(p b) c -> p b c", p=P), z_sb[:, :, 0:ZW]).then_inc(s_zst, 16)
            sp.wait_ge(s_tabi, 1)
            sp.dma_start(tab_dram.rearrange("(p b) c -> p (b c)", p=P), work[:, 0:(NB + 1) * TW]).then_inc(s_tst, 16)
            sp.wait_ge(s_t, 1)
            sp.dma_start(t_dram[0:1, 0:NPAD].rearrange("a (p b) -> (a p) b", p=P), t_sb[:, :]).then_inc(s_tst, 16)
            sp.dma_start(t_dram[0:1, NPAD:NROWS].rearrange("a (p b) -> (a p) b", p=P), t_sb[:, 0:1]).then_inc(s_tst, 16)
            sp.wait_ge(s_tst, 48)
            sp.wait_ge(s_win, 1)
            with sp.Fori(0, NM) as m:
                c0 = sp.snap(sp.value_load(cum_i[0:1, bass.ds(m, 1)], min_val=0, max_val=NM * NB))
                c1 = sp.snap(sp.value_load(cum_i[0:1, bass.ds(m + 1, 1)], min_val=1, max_val=NM * NB))
                first = sp.snap(sp.value_load(base_i[0:1, bass.ds(m, 1)], min_val=0, max_val=NODES - 1))
                with sp.Fori(c0, c1) as i:
                    row = sp.snap(nc.s_assert_within(
                        first + (i - c0) * P, 0, NROWS - P,
                        skip_runtime_bounds_check_because="a window starts at or below the last destination"))
                    sp.dma_start(tab[:, :], tab_dram[bass.ds(row, P), :]).then_inc(s_rows, 16)
                    sp.dma_start(trow[:, :], t_dram[0:1, bass.ds(row, P)].to_broadcast([P, P])
                                 ).then_inc(s_rows, 16)
                    sp.wait_ge(s_tabn, i + 1)
                    sp.dma_start(tab_dram[bass.ds(row, P), :], tab[:, :]).then_inc(s_tabs, 16)
                    sp.wait_ge(s_tabs, i * 16 + 16)
                    sp.sem_inc(s_held[1], 1)
            sp.dma_start(work[:, 0:NB * TW], tab_dram[0:NPAD, :].rearrange("(p b) c -> p (b c)", p=P)).then_inc(s_fin, 16)
            sp.wait_ge(s_res, 1)
            nodes_dma(sp, x_sb, out, False, s_out)
            sp.wait_ge(s_out, 32)

        @block.gpsimd
        def _(pool):
            g_ = nc.gpsimd
            chain = Chain(pool, s_pool)
            chain(g_.memset(ones_f[:, :], 1.0))
            chain(g_.memset(ident[:, :], 0.0))
            chain(g_.affine_select(out=ident[:, :], in_=ident[:, :], compare_op=ALU.not_equal, fill=1.0, base=0,
                                   pattern=[[-1, P]], channel_multiplier=1))
            chain(g_.iota(src_iota := idx[:, 0, 0:1], pattern=[[0, 1]], base=NPAD, channel_multiplier=1))
            chain(g_.tensor_copy(dummy_row[:, :], src_iota))
            chain(g_.iota(cum_i[:, 0:P], pattern=[[1, P]], base=0, channel_multiplier=0))
            chain(g_.tensor_copy(iota_f[:, :], cum_i[:, 0:P]))
            chain(g_.affine_select(out=tri[:, :], in_=ones_f[:, :], compare_op=ALU.is_gt, fill=0.0, base=0,
                                   pattern=[[-1, P]], channel_multiplier=1))
            chain(g_.memset(one_sb[:, :], 1.0))
            chain(g_.memset(zeros_b[:, :], 0.0))
            for s in range(2):
                chain(g_.memset(zg[:, s, :, ZW:ZW + 1], 1.0))
            g_.sem_inc(s_const, 1)
            def scatter_half(s, h, n, before):
                pool.wait_ge(s_ysb, n + 3)
                pool.wait_ge(s_idx, n + 1)
                for g in range(4 * h, 4 * h + 4):
                    if before is None:
                        pool.wait_ge(s_zero[g], 48)
                    else:
                        pool.wait_ge(s_tab[g], before)
                g_.sem_inc(s_room, 1)
                for g in range(4 * h, 4 * h + 4):
                    g_.indirect_dma_start(
                        out=acc_dram[g][:, :],
                        out_offset=bass.IndirectOffsetOnAxis(ap=idx[:, s, g:g + 1], axis=0),
                        in_=y_sb[:, s, g * AW:(g + 1) * AW], in_offset=None,
                        compute_op=ALU.add).then_inc(s_tab[g], 16)

            for n in range(4):
                scatter_half(n // 2, n % 2, n, 16 if n >= 2 else None)
            with pool.Fori(1, NM // 2) as it:
                for s in range(2):
                    for h in range(2):
                        scatter_half(s, h, it * 4 + (2 * s + h), it * 32 + 16 * s)
            pool.wait_ge(s_neg, 1)
            g_.partition_all_reduce(lo_all[:, :], lo_all[:, :], P, bass.bass_isa.ReduceOp.max).then_inc(s_range, 1)
            g_.partition_all_reduce(hi_all[:, :], hi_all[:, :], P, bass.bass_isa.ReduceOp.max).then_inc(s_range, 1)
            pool.wait_ge(s_zst, 16)
            with pool.Fori(0, NM // 2) as it:
                for s in range(2):
                    pool.wait_ge(s_zg_used, it * 2 + s + 1)
                    g_.sem_inc(s_held[0], 1)
                    for g in range(G):
                        g_.indirect_dma_start(
                            out=zg[:, s, g, 0:ZW], out_offset=None, in_=z_dram[:, :],
                            in_offset=bass.IndirectOffsetOnAxis(ap=idx[:, s, g:g + 1], axis=0)).then_inc(s_zg[s], 16)

        @block.scalar
        def _(act):
            a_ = nc.scalar
            act.wait_ge(s_dsub, 1)
            a_.activation(z_sb[:, :, 0:D], d_sb[:, :, :], ACT.Square).then_inc(s_sq, 1)
            act.wait_ge(s_vv, 1)
            a_.activation(var_sb[:, :], var_sb[:, :], ACT.Sqrt).then_inc(s_std, 1)
            with act.Fori(0, NM // 2) as it:
                for s in range(2):
                    for h in range(2):
                        act.wait_ge(s_y, it * 4 + 2 * s + h + 3)
                        act.wait_ge(s_room, it * 4 + 2 * s + h + 1)
                        a_.activation(y_sb[:, s, 4 * h * AW:4 * (h + 1) * AW], banks[4 + h][:, 0:4 * AW],
                                      ACT.Copy).then_inc(s_ysb, 1)
            with act.Fori(0, NC) as c:
                act.wait_ge(s_hid, c + 1)
                for h in range(2):
                    w = 512 if h == 0 else CH * P - 512
                    ins = a_.activation(big_b.rearrange("p g n -> p (g n)")[:, h * 512:h * 512 + w], banks[2 + h][:, 0:w],
                                        ACT.Relu, bias=b1_sb[:, 0:1])
                ins.then_inc(s_hids, 1)
            act.wait_ge(s_dsub, 2)
            a_.activation(work[:, 0:NB * D], d_sb.rearrange("p b d -> p (b d)"), ACT.Square).then_inc(s_sq, 1)
            act.wait_ge(s_vv, 2)
            a_.activation(var_sb[:, :], var_sb[:, :], ACT.Sqrt).then_inc(s_std, 1)
            with act.Fori(0, NC) as c:
                act.wait_ge(s_tr, c + (NC + 1))
                for h in range(2):
                    w = 512 if h == 0 else CH * P - 512
                    ins = a_.activation(big_b.rearrange("p g n -> p (g n)")[0:D, h * 512:h * 512 + w], banks[h][0:D, 0:w],
                                        ACT.Copy)
                ins.then_inc(s_trs, 1)
            act.wait_ge(s_mom, 1)
            ch = Chain(act, s_act)
            ch(a_.activation(mabs[:, :, :], mabs[:, :, :], ACT.Ln))
            ch(a_.activation(mabs[:, 0:2, :], mabs[:, 0:2, :], ACT.Exp, scale=0.5))
            a_.activation(mabs[:, 2:4, :], mabs[:, 2:4, :], ACT.Exp, scale=1.0 / 3.0).then_inc(s_root, 1)
            act.wait_ge(s_win, 1)
            with act.Fori(0, NM) as m:
                c0 = act.snap(act.value_load(cum_i[0:1, bass.ds(m, 1)], min_val=0, max_val=NM * NB))
                c1 = act.snap(act.value_load(cum_i[0:1, bass.ds(m + 1, 1)], min_val=1, max_val=NM * NB))
                with act.Fori(c0, c1) as i:
                    act.wait_ge(s_mask, i + 1)
                    for g in range(G):
                        ins = a_.activation(big_b[:, g, :], big_a[:, g, :], ACT.Identity, bias=s_sb[:, g:g + 1])
                    ins.then_inc(s_lin, 1)
                    act.wait_ge(s_sub, i + 1)
                    a_.activation(rescale[:, :], mloc[:, :], ACT.Exp)
                    a_.activation(big_a[:, :, :], big_b[:, :, :], ACT.Exp).then_inc(s_exp, 1)

        @block.tensor
        def _(pe):
            t_ = nc.tensor
            pe.wait_ge(s_const, 1)
            pe.wait_ge(s_w, 16 * 11)
            t_.transpose(banks[0][0:D, 0:D], wfc_sb[:, :], ident[0:D, 0:D])
            t_.matmul(banks[0][0:D, D:D + 1], wfc_sb[:, :], blk_sb[:, 0:1], start=True, stop=True)
            t_.matmul(banks[0][0:D, D + 1:D + 2], wfc_sb[:, :], blk_sb[:, 3:4], start=True, stop=True)
            t_.matmul(banks[1][:, 0:2], we_sb[:, 0:1].to_broadcast([2, P]), wedge_sb[:, :], start=True, stop=True)
            for j in range(2):
                t_.matmul(banks[2][:, j * D:(j + 1) * D], wedge_sb[:, j:j + 1].to_broadcast([2, P]), we2nT_sb[:, :],
                          start=True, stop=True)
            for k, b in enumerate((1, 4, 2, 5)):
                ins = t_.matmul(banks[3][:, k * D:(k + 1) * D], blk_sb[:, b:b + 1].to_broadcast([D, P]),
                                wm_sb[:, k // 2, :], start=True, stop=True)
            ins.then_inc(s_prep, 1)
            t_.matmul(banks[6][:, 0:NB], zeros_b[:, :], zeros_b[:, 0:NB], start=True, stop=False)
            pe.wait_ge(s_prep_sb, 1)
            with pe.Fori(0, NM // 2) as it:
                for s in range(2):
                    for h in range(2):
                        n = it * 4 + (2 * s + h)
                        pe.wait_ge(s_stage, it * 2 + s + 1)
                        pe.wait_ge(s_same, n + 1)
                        for j in range(4):
                            ins = t_.matmul(banks[2 * s + h][:, j * P:(j + 1) * P],
                                            srcf[:, s, 4 * h + j:4 * h + j + 1].to_broadcast([P, P]), ident[:, :],
                                            start=True, stop=True)
                        ins.then_inc(s_srcb, 1)
                        pe.wait_ge(s_oh, n + 1)
                        for j in range(4):
                            ins = t_.matmul(banks[6][:, 0:NB], ohp[:, h, j, :], ohj[:, h, j, :], start=False, stop=False)
                        ins.then_inc(s_oh_used, 1)
                        pe.wait_ge(s_same, n + 5)
                        if h == 0:
                            pe.wait_ge(s_ea[s], it * 16 + 16)
                        pe.wait_ge(s_ysb, n + 1)
                        for j in range(4):
                            g = 4 * h + j
                            t_.matmul(banks[4 + h][:, j * AW:j * AW + D], same[:, h, j, :],
                                      ea_sb[:, s, g * D:(g + 1) * D], start=True, stop=True)
                            ins = t_.matmul(banks[4 + h][:, j * AW + D:(j + 1) * AW], same[:, h, j, :],
                                            one_sb[:, s:s + 1], start=True, stop=True)
                        ins.then_inc(s_y, 1)
            t_.matmul(banks[6][:, 0:NB], zeros_b[:, :], zeros_b[:, 0:NB], start=False, stop=True).then_inc(s_cnt, 1)
            catT = big_a.rearrange("p g n -> p (g n)")
            hidT = big_b.rearrange("p g n -> p (g n)")
            cat = y_sb.rearrange("p s w -> p (s w)")
            with pe.Fori(0, NC) as c:
                pe.wait_ge(s_cat, c + 1)
                for b in range(CH):
                    ins = t_.transpose(banks[b // 4][:, (b % 4) * P:(b % 4 + 1) * P], cat[:, b * P:(b + 1) * P], ident[:, :])
                ins.then_inc(s_tr, 1)
                pe.wait_ge(s_trs, c + 1)
                t_.matmul(banks[2][:, 0:512], w1_sb[:, :], catT[:, 0:512], start=True, stop=True)
                t_.matmul(banks[3][:, 0:CH * P - 512], w1_sb[:, :], catT[:, 512:CH * P], start=True, stop=True
                          ).then_inc(s_hid, 1)
                pe.wait_ge(s_hids, c + 1)
                for b in range(CH):
                    ins = t_.matmul(banks[4][:, b * D:(b + 1) * D], hidT[:, b * P:(b + 1) * P], w2_sb[:, :],
                                    start=True, stop=True)
                ins.then_inc(s_o, 1)
            with pe.Fori(0, NC) as c:
                pe.wait_ge(s_cat, c + (NC + 1))
                pe.sem_inc(s_held[3], 1)
                for b in range(CH):
                    ins = t_.transpose(banks[b // 4][0:D, (b % 4) * P:(b % 4 + 1) * P], cat[:, b * D:(b + 1) * D],
                                       ident[:, :])
                ins.then_inc(s_tr, 1)
                pe.wait_ge(s_trs, c + (NC + 1))
                for b in range(CH):
                    ins = t_.matmul(banks[2][:, b * (D + 2):(b + 1) * (D + 2)], hidT[0:D, b * P:(b + 1) * P], wz_sb[:, :],
                                    start=True, stop=True)
                ins.then_inc(s_zp, 1)
            pe.wait_ge(s_part, 1)
            t_.matmul(banks[5][:, 0:2 * D], ones_f[:, :], sums.rearrange("p a d -> p (a d)"), start=True, stop=True
                      ).then_inc(s_psum, 1)
            pe.wait_ge(s_part, 2)
            t_.matmul(banks[5][:, 0:4 * D], ones_f[:, :], mom.rearrange("p a d -> p (a d)"), start=True, stop=True
                      ).then_inc(s_psum, 1)
            pe.wait_ge(s_win, 1)
            with pe.Fori(0, NM // 2) as it:
                for s in range(2):
                    c0 = pe.snap(pe.value_load(cum_i[0:1, bass.ds(it * 2 + s, 1)], min_val=0, max_val=NM * NB))
                    c1 = pe.snap(pe.value_load(cum_i[0:1, bass.ds(it * 2 + s + 1, 1)], min_val=1, max_val=NM * NB))
                    with pe.Fori(c0, c1) as i:
                        pe.wait_ge(s_gmax, i + 1)
                        t_.transpose(banks[0][:, 0:P], gmax[:, :], ident[:, :]).then_inc(s_gT, 1)
                        pe.wait_ge(s_mnew, i + 1)
                        t_.matmul(banks[1][:, 0:P], mnew[:, 0:1].to_broadcast([P, P]), ident[:, :], start=True, stop=True
                                  ).then_inc(s_mrow, 1)
                        pe.wait_ge(s_exp, i + 1)
                        for g in range(G):
                            ins = t_.matmul(banks[2][:, 0:RW], big_a[:, g, :], zg[:, s, g, :], start=(g == 0),
                                            stop=(g == G - 1))
                        ins.then_inc(s_agg1, 1)

        @block.vector
        def _(dve):
            v_ = nc.vector
            ch = Chain(dve, s_dve)
            v_.memset(work[:, :], 0.0).then_inc(s_work, 1)
            v_.memset(x_sb[:, :, :], 0.0).then_inc(s_work, 1)
            dve.sem_inc(s_same, 4)
            dve.sem_inc(s_ysb, 2)
            dve.sem_inc(s_room, 2)
            dve.sem_inc(s_y, 2)
            dve.sem_inc(s_oh_used, 2)
            dve.wait_ge(s_prep, 1)
            v_.tensor_copy(wz_sb[:, :], banks[0][0:D, 0:D + 2])
            v_.tensor_copy(q_sb[:, :], banks[1][:, 0:2])
            v_.tensor_copy(r_sb.rearrange("p a d -> p (a d)"), banks[2][:, 0:2 * D])
            v_.tensor_copy(v_sb.rearrange("p a d -> p (a d)"), banks[3][:, 0:4 * D]).then_inc(s_prep_sb, 1)
            dve.wait_ge(s_prep_sb, 1)

            def wide(a, n):
                return a.unsqueeze(2).to_broadcast([P, NB, n])

            def layernorm_stats(n, xs, sq):
                ch(v_.tensor_reduce(mean_sb[:, :], xs, X_AXIS, ALU.add))
                ch(v_.tensor_scalar(mean_sb[:, :], mean_sb[:, :], 1.0 / D, None, ALU.mult))
                v_.tensor_tensor(d_sb[:, :, :], xs, wide(mean_sb[:, :], D), ALU.subtract).then_inc(s_dsub, 1)
                dve.wait_ge(s_sq, n)
                ch(v_.tensor_reduce(var_sb[:, :], sq, X_AXIS, ALU.add))
                v_.tensor_scalar(var_sb[:, :], var_sb[:, :], 1.0 / D, EPS, ALU.mult, ALU.add).then_inc(s_vv, 1)
                dve.wait_ge(s_std, n)
                v_.reciprocal(rstd_sb[:, :], var_sb[:, :]).then_inc(s_rstd, 1)
                dve.wait_ge(s_rstd, n)
                dve.wait_ge(s_dsub, n)

            dve.wait_ge(s_dst, 32)
            ch(v_.tensor_copy(dst_f[:, :], dst_i[:, :]))
            ch(v_.tensor_scalar(dst_i[:, :], dst_f[:, :], 1.0 / NB, None, ALU.mult))
            ch(v_.tensor_copy(dst_p[:, :], dst_i[:, :]))
            ch(v_.scalar_tensor_tensor(out=dst_j[:, :], in0=dst_p[:, :], scalar=-float(NB), in1=dst_f[:, :],
                                       op0=ALU.mult, op1=ALU.add))
            ch(v_.tensor_scalar(ee_sb[:, :], dst_j[:, :], 0.0, None, ALU.is_lt))
            ch(v_.tensor_tensor(dst_p[:, :], dst_p[:, :], ee_sb[:, :], ALU.subtract))
            ch(v_.scalar_tensor_tensor(out=dst_j[:, :], in0=ee_sb[:, :], scalar=float(NB), in1=dst_j[:, :],
                                       op0=ALU.mult, op1=ALU.add))
            ch(v_.memset(dst_p[0:DUP, (NM - 1) * G:NT], -1.0))
            ch(v_.tensor_reduce(hi_all[:, :], dst_f.rearrange("p (m g) -> p m g", g=G), X_AXIS, ALU.max))
            ch(v_.tensor_reduce(lo_all[:, :], dst_f.rearrange("p (m g) -> p m g", g=G), X_AXIS, ALU.min))
            v_.tensor_scalar(lo_all[:, :], lo_all[:, :], -1.0, None, ALU.mult).then_inc(s_neg, 1)
            dve.wait_ge(s_x, 32)
            layernorm_stats(1, x_sb[:, :, :], z_sb[:, :, 0:D])
            ch(v_.tensor_tensor(x_sb[:, :, :], x_sb[:, :, :], b2_sb[:, :].unsqueeze(1).to_broadcast([P, NB, D]), ALU.add))
            dve.wait_ge(s_src, 32)

            with dve.Fori(0, NM // 2) as it:
                c1 = Chain(dve, s_dve1, it * 28)
                for s in range(2):
                    col = it * (2 * G) + s * G
                    v_.tensor_scalar(srcf[:, s, :], src_i[:, bass.ds(col, G)], 0.0, None, ALU.add).then_inc(s_stage, 1)
                    dve.wait_ge(s_stage, it * 2 + s + 1)
                    for h in range(2):
                        n = it * 4 + (2 * s + h)
                        dve.wait_ge(s_oh_used, n + 1)
                        v_.tensor_tensor(ohp[:, h, :, :], iota_f[:, :].unsqueeze(1).to_broadcast([P, 4, P]),
                                         dst_p[:, bass.ds(col + 4 * h, 4)].unsqueeze(2).to_broadcast([P, 4, P]),
                                         ALU.is_equal)
                        v_.tensor_tensor(ohj[:, h, :, :], iota_f[:, 0:NB].unsqueeze(1).to_broadcast([P, 4, NB]),
                                         dst_j[:, bass.ds(col + 4 * h, 4)].unsqueeze(2).to_broadcast([P, 4, NB]),
                                         ALU.is_equal).then_inc(s_oh, 1)
                        dve.wait_ge(s_srcb, n + 1)
                        srcb = banks[2 * s + h][:, :].rearrange("p (j e) -> p j e", j=4)
                        c1(v_.tensor_scalar(todummy[:, s, 4 * h:4 * h + 4], srcf[:, s, 4 * h:4 * h + 4], -1.0,
                                            dummy_row[:, 0:1], ALU.mult, ALU.add))
                        for j in range(4):
                            g = 4 * h + j
                            ins = v_.scalar_tensor_tensor(out=junk[:, :], in0=srcb[:, j, :],
                                                          scalar=srcf[:, s, g:g + 1], in1=tri[:, :], op0=ALU.is_equal,
                                                          op1=ALU.mult, accum_out=before[:, s, g:g + 1])
                            c1(ins)
                        dve.wait_ge(s_y, n + 1)
                        v_.tensor_tensor(same[:, h, :, :], srcb,
                                         srcf[:, s, 4 * h:4 * h + 4].unsqueeze(2).to_broadcast([P, 4, P]),
                                         ALU.is_equal).then_inc(s_same, 1)
                        dve.wait_ge(s_room, n + 1)
                        c1(v_.tensor_scalar(before[:, s, 4 * h:4 * h + 4], before[:, s, 4 * h:4 * h + 4], 1.0, None,
                                            ALU.min))
                        c1(v_.tensor_tensor(before[:, s, 4 * h:4 * h + 4], before[:, s, 4 * h:4 * h + 4],
                                            todummy[:, s, 4 * h:4 * h + 4], ALU.mult))
                        v_.tensor_tensor(idx[:, s, 4 * h:4 * h + 4], before[:, s, 4 * h:4 * h + 4],
                                         srcf[:, s, 4 * h:4 * h + 4], ALU.add).then_inc(s_idx, 1)

            dve.wait_ge(s_cnt, 1)
            ch(v_.tensor_copy(cnt_sb[:, 1, :], banks[6][:, 0:NB]))
            cat = y_sb.rearrange("p s w -> p (s w)")
            catT = big_a.rearrange("p g n -> p (g n)")
            dve.sem_inc(s_agg, 2)
            dve.wait_ge(s_ysb, 2 * NM + 2)
            for k in range(G):
                dve.wait_ge(s_tab[k], 16 * NM)
            with dve.Fori(0, NC // 2) as it:
                for s in range(2):
                    c = it * 2 + s
                    cc = Chain(dve, s_dve3, c * 2)
                    cols = cat[:, 0:CH * P].rearrange("p (b f) -> p b f", b=CH)
                    cc(v_.scalar_tensor_tensor(
                        out=cols[:, :, 0:D], in0=d_sb[:, bass.ds(c * CH, CH), :], scalar=0.0,
                        in1=rstd_sb[:, bass.ds(c * CH, CH)].unsqueeze(2).to_broadcast([P, CH, D]),
                        op0=ALU.max, op1=ALU.mult))
                    dve.wait_ge(s_acc[s], it * (16 * G) + 16 * G)
                    rows = work[:, s * G * CH * AW:(s + 1) * G * CH * AW].rearrange("p (k b c) -> p b c k", k=G, b=CH)
                    v_.tensor_reduce(cols[:, :, D:2 * D], rows[:, :, 0:D, :], X_AXIS, ALU.add).then_inc(s_cat, 1)
                    v_.tensor_reduce(cnt_sb[:, 0, bass.ds(c * CH, CH)], rows[:, :, D, :], X_AXIS, ALU.add
                                     ).then_inc(s_agg, 1)
                    dve.wait_ge(s_tr, c + 1)
                    v_.tensor_copy(catT[:, 0:512], banks[0][:, 0:512])
                    v_.tensor_copy(catT[:, 512:CH * P], banks[1][:, 0:CH * P - 512]).then_inc(s_trs, 1)
                    dve.wait_ge(s_o, c + 1)
                    xc = x_sb[:, bass.ds(c * CH, CH), :]
                    cc(v_.tensor_tensor(xc, xc, banks[4][:, 0:CH * D].rearrange("p (b d) -> p b d", b=CH), ALU.add))
            dve.wait_ge(s_agg, NC + 2)
            layernorm_stats(2, x_sb[:, :, :], work[:, 0:NB * D].rearrange("p (b d) -> p b d", d=D))
            with dve.Fori(0, NC) as c:
                v_.scalar_tensor_tensor(
                    out=cat[:, 0:CH * D].rearrange("p (b f) -> p b f", b=CH), in0=d_sb[:, bass.ds(c * CH, CH), :],
                    scalar=0.0, in1=rstd_sb[:, bass.ds(c * CH, CH)].unsqueeze(2).to_broadcast([P, CH, D]),
                    op0=ALU.max, op1=ALU.mult).then_inc(s_cat, 1)
                dve.wait_ge(s_zp, c + 1)
                v_.tensor_scalar(z_sb[:, bass.ds(c * CH, CH), :],
                                 banks[2][:, 0:CH * (D + 2)].rearrange("p (b f) -> p b f", b=CH), 0.0, None, ALU.add
                                 ).then_inc(s_z, 1)
            dve.wait_ge(s_z, NC)
            ch(v_.memset(src_i[:, NT:NT + 2 * G], 0))
            for s in range(2):
                v_.tensor_copy(idx[:, s, :], src_i[:, s * G:(s + 1) * G]).then_inc(s_zg_used, 1)
            w = work[:, 0:NB * D].rearrange("p (b d) -> p b d", d=D)
            z = z_sb[:, :, 0:D]
            for a in range(2):
                ch(v_.tensor_tensor(w, z, wide(cnt_sb[:, a, :], D), ALU.mult))
                ch(v_.tensor_reduce(sums[:, a, :], w.rearrange("p b d -> p d b"), X_AXIS, ALU.add))
            dve.sem_inc(s_part, 1)
            dve.wait_ge(s_psum, 1)
            ch(v_.tensor_scalar(sums.rearrange("p a d -> p (a d)"), banks[5][:, 0:2 * D], 1.0 / EDGES, None, ALU.mult))
            for a in range(2):
                mu = sums[:, a, :].unsqueeze(1).to_broadcast([P, NB, D])
                ch(v_.tensor_tensor(d_sb[:, :, :], z, mu, ALU.subtract))
                ch(v_.tensor_tensor(w, d_sb[:, :, :], d_sb[:, :, :], ALU.mult))
                ch(v_.tensor_tensor(w, w, wide(cnt_sb[:, a, :], D), ALU.mult))
                ch(v_.tensor_reduce(mom[:, a, :], w.rearrange("p b d -> p d b"), X_AXIS, ALU.add))
                ch(v_.tensor_tensor(w, w, d_sb[:, :, :], ALU.mult))
                ch(v_.tensor_reduce(mom[:, 2 + a, :], w.rearrange("p b d -> p d b"), X_AXIS, ALU.add))
            dve.sem_inc(s_part, 1)
            ch(v_.memset(work[:, 0:(NB + 1) * TW], 0.0))
            v_.memset(work[:, 0:(NB + 1) * TW].rearrange("p (b c) -> p b c", c=TW)[:, :, RW:TW], FLOOR).then_inc(s_tabi, 1)
            dve.wait_ge(s_psum, 2)
            flat = lambda a: a.rearrange("p a d -> p (a d)")
            ch(v_.tensor_scalar(flat(mom), banks[5][:, 0:4 * D], 1.0 / EDGES, None, ALU.mult))
            ch(v_.tensor_scalar(flat(mabs), flat(mom), -1.0, None, ALU.mult))
            ch(v_.tensor_tensor(flat(mabs), flat(mabs), flat(mom), ALU.max))
            ch(v_.tensor_scalar(flat(msign), flat(mom), 0.0, None, ALU.is_lt))
            ch(v_.scalar_tensor_tensor(out=flat(msign), in0=flat(mom), scalar=0.0, in1=flat(msign), op0=ALU.is_gt,
                                       op1=ALU.subtract))
            v_.tensor_scalar(flat(mabs), flat(mabs), 1e-37, None, ALU.max).then_inc(s_mom, 1)
            dve.wait_ge(s_root, 1)
            ch(v_.tensor_tensor(flat(mabs), flat(mabs), flat(msign), ALU.mult))
            ch(v_.tensor_tensor(flat(mabs), flat(mabs), flat(v_sb), ALU.mult))
            ch(v_.tensor_reduce(c_sb[:, :], flat(mabs), X_AXIS, ALU.add))
            v_.tensor_scalar(t_sb[:, :], z_sb[:, :, D + 1], c_sb[:, 0:1], None, ALU.add).then_inc(s_t, 1)
            dve.wait_ge(s_e2, 32)
            ch(v_.tensor_scalar(ee_sb[:, :], e2_sb[:, :, 0], q_sb[:, 0:1], None, ALU.mult))
            ch(v_.scalar_tensor_tensor(out=ee_sb[:, :], in0=e2_sb[:, :, 1], scalar=q_sb[:, 1:2], in1=ee_sb[:, :],
                                       op0=ALU.mult, op1=ALU.add))
            ch(v_.memset(ee_sb[0:DUP, (NM - 1) * G:NT], OFF))
            dve.wait_ge(s_range, 2)
            ch(v_.tensor_scalar(base_i[:, :], lo_all[:, :], -1.0, None, ALU.mult))
            ch(v_.tensor_tensor(tmp_i[:, :], hi_all[:, :], lo_all[:, :], ALU.add))
            ch(v_.tensor_scalar(tmp_i[:, :], tmp_i[:, :], P.bit_length() - 1, None, ALU.arith_shift_right))
            ch(v_.tensor_copy(tmp_m[:, :], tmp_i[:, :]))
            ch(v_.tensor_scalar(tmp_m[:, :], tmp_m[:, :], 1.0, None, ALU.add))
            ch(v_.memset(cum_f[:, 0:1], 0.0))
            ch(v_.tensor_tensor_scan(cum_f[:, 1:NM + 1], ones_f[:, 0:1].to_broadcast([P, NM]), tmp_m[:, :], 0.0, ALU.mult, ALU.add))
            v_.tensor_copy(cum_i[:, :], cum_f[:, :]).then_inc(s_win, 1)
            dve.wait_ge(s_win, 1)

            with dve.Fori(0, NM // 2) as it:
                for s in range(2):
                    m = it * 2 + s
                    col = it * (2 * G) + s * G
                    c0 = dve.snap(dve.value_load(cum_i[0:1, bass.ds(m, 1)], min_val=0, max_val=NM * NB))
                    c1 = dve.snap(dve.value_load(cum_i[0:1, bass.ds(m + 1, 1)], min_val=1, max_val=NM * NB))
                    cm = Chain(dve, s_dve4, m * 3)
                    dve.wait_ge(s_zg[s], it * (16 * G) + 16 * G)
                    cm(v_.tensor_tensor(s_sb[:, :], zg[:, s, :, D], ee_sb[:, bass.ds(col, G)], ALU.add))
                    cm(v_.tensor_scalar(zg[:, s, :, ZW + 1:RW], e2_sb[:, bass.ds(col, G), :], 0.0, None, ALU.add))
                    cm(v_.tensor_scalar(dloc[:, :], dst_f[:, bass.ds(col, G)], lo_all[:, bass.ds(m, 1)], None, ALU.add))
                    dve.sem_inc(s_held[2], 1)
                    with dve.Fori(c0, c1) as i:
                        cw = Chain(dve, s_dve5, i * 6)
                        cw(v_.tensor_tensor(big_a[:, :, :], iota_f[:, :].unsqueeze(1).to_broadcast([P, G, P]),
                                            dloc[:, :].unsqueeze(2).to_broadcast([P, G, P]), ALU.not_equal))
                        dve.wait_ge(s_rows, i * 32 + 32)
                        v_.scalar_tensor_tensor(out=big_a[:, :, :], in0=big_a[:, :, :], scalar=OFF,
                                                in1=trow[:, :].unsqueeze(1).to_broadcast([P, G, P]),
                                                op0=ALU.mult, op1=ALU.add).then_inc(s_mask, 1)
                        dve.wait_ge(s_lin, i + 1)
                        cw(v_.scalar_tensor_tensor(out=big_b[:, :, :], in0=big_b[:, :, :], scalar=SLOPE,
                                                   in1=big_b[:, :, :], op0=ALU.mult, op1=ALU.max))
                        v_.tensor_reduce(gmax[:, :], big_b.rearrange("p g n -> p n g"), X_AXIS, ALU.max
                                         ).then_inc(s_gmax, 1)
                        dve.wait_ge(s_gT, i + 1)
                        cw(v_.tensor_reduce(mloc[:, :], banks[0][:, 0:P], X_AXIS, ALU.max))
                        v_.tensor_tensor(mnew[:, :], mloc[:, :], tab[:, RW:TW], ALU.max).then_inc(s_mnew, 1)
                        dve.wait_ge(s_mnew, i + 1)
                        cw(v_.tensor_tensor(mloc[:, :], tab[:, RW:TW], mnew[:, :], ALU.subtract))
                        cw(v_.tensor_scalar(tab[:, RW:TW], mnew[:, :], 0.0, None, ALU.add))
                        dve.wait_ge(s_mrow, i + 1)
                        v_.tensor_tensor(big_b[:, :, :], big_b[:, :, :],
                                         banks[1][:, 0:P].unsqueeze(1).to_broadcast([P, G, P]), ALU.subtract
                                         ).then_inc(s_sub, 1)
                        cw(v_.tensor_scalar(dloc[:, :], dloc[:, :], -float(P), None, ALU.add))
                        dve.wait_ge(s_agg1, i + 1)
                        v_.scalar_tensor_tensor(out=tab[:, 0:RW], in0=tab[:, 0:RW], scalar=rescale[:, 0:1],
                                                in1=banks[2][:, 0:RW], op0=ALU.mult, op1=ALU.add).then_inc(s_tabn, 1)
                    v_.tensor_scalar(idx[:, s, :], src_i[:, bass.ds(col + 2 * G, G)], 0.0, None, ALU.add
                                     ).then_inc(s_zg_used, 1)

            dve.wait_ge(s_fin, 16)
            rows = work[:, 0:NB * TW].rearrange("p (b c) -> p b c", c=TW)
            ch(v_.tensor_scalar(mean_sb[:, :], rows[:, :, ZW], 1e-30, None, ALU.max))
            ch(v_.reciprocal(rstd_sb[:, :], mean_sb[:, :]))
            for j in range(2):
                ch(v_.tensor_tensor(d_sb[:, :, :], wide(rows[:, :, ZW + 1 + j], D),
                                    r_sb[:, j, :].unsqueeze(1).to_broadcast([P, NB, D]), ALU.mult))
                ch(v_.tensor_tensor(rows[:, :, 0:D], rows[:, :, 0:D], d_sb[:, :, :], ALU.add))
            ch(v_.tensor_tensor(rows[:, :, 0:D], rows[:, :, 0:D], wide(rstd_sb[:, :], D), ALU.mult))
            v_.tensor_tensor(x_sb[:, :, :], x_sb[:, :, :], rows[:, :, 0:D], ALU.add).then_inc(s_res, 1)


_INS = ['x', 'src', 'dst', 'edge_attr_2', 'edge_attr_64', 'L0_gnn_W1', 'L0_gnn_b1', 'L0_gnn_W2', 'L0_gnn_b2',
        'L1_gnn_W_fc', 'L1_gnn_W_attn', 'L1_gnn_W_edge', 'L1_gnn_W_e2n', 'L1_gnn_W_m1', 'L1_gnn_W_m2']


def kernel(**inputs):
    import numpy as _np
    import concourse.bacc as _bacc
    from concourse import mybir as _mybir
    from concourse.bass_utils import run_bass_kernel_spmd as _run

    nc = _bacc.Bacc("TRN2", target_bir_lowering=False, num_devices=1)
    arrays, args = {}, []
    for name in _INS:
        a = _np.ascontiguousarray(inputs[name])
        arrays[f"in_{name}_dram"] = a
        args.append(nc.dram_tensor(f"in_{name}_dram", a.shape, _mybir.dt.from_np(a.dtype), kind="ExternalInput").ap())
    args.append(nc.dram_tensor("out_0_dram", (NODES, D), _mybir.dt.float32, kind="ExternalOutput").ap())
    gnn_kernel(nc, *args)
    r = _run(nc, [arrays], core_ids=[0])
    return r.results[0]["out_0_dram"]
```

```python
import concourse.bass as bass
from concourse import mybir
from contextlib import ExitStack

ALU = mybir.AluOpType
ACT = mybir.ActivationFunctionType
X_AXIS = mybir.AxisListType.X
F32 = mybir.dt.float32
BF16 = mybir.dt.bfloat16
I32 = mybir.dt.int32

P = 128
NODES, EDGES, D, HID = 12500, 200000, 64, 128
G = 8
ME = P * G
NM = -(-EDGES // ME)
LAST0 = EDGES - ME
DUP = (NM * ME - EDGES) // G
NT = NM * G
NB = -(-NODES // P)
NPAD = P * NB
NROWS = NPAD + P
FULL = NODES // NB
REST = NODES - FULL * NB
AW = D + 1
ZW = D + 1
EW = D + 2
RW = D + 4
TW = RW + 1
CH = 7
NC = NB // CH
SL = 4
W = 80
EPS = 1e-5
SLOPE = 0.01
OFF = -1e30
FLOOR = -1e20
assert NM % 2 == 0 and (NM * ME - EDGES) % G == 0 and NB % CH == 0 and 0 < REST < NB


class Chain:

    def __init__(self, eng, sem, base=0):
        self.eng, self.sem, self.base, self.k = eng, sem, base, 0

    def __call__(self, ins):
        self.k += 1
        ins.then_inc(self.sem, 1)
        self.eng.wait_ge(self.sem, self.base + self.k)


def gnn_kernel(nc, x, src, dst, e2, e64, W1, b1, W2, b2, W_fc, W_attn, W_edge, W_e2n, W_m1, W_m2, out):
    with ExitStack() as ctx:
        def sb(name, shape, dt=F32):
            return ctx.enter_context(nc.sbuf_tensor(name, shape, dt))

        def pb(name, shape, dt=F32):
            return ctx.enter_context(nc.psum_tensor(name, shape, dt))

        def sem(name):
            return ctx.enter_context(nc.semaphore(name))

        acc_dram = [nc.dram_tensor(f"acc_dram{k}", (NROWS, AW), F32, kind="Internal").ap() for k in range(G)]
        z_dram = nc.dram_tensor("z_dram", (NPAD, ZW), F32, kind="Internal").ap()
        t_dram = nc.dram_tensor("t_dram", (1, NROWS), F32, kind="Internal").ap()
        tab_dram = nc.dram_tensor("tab_dram", (NROWS, TW), F32, kind="Internal").ap()

        ident = sb("ident", [P, P])
        iota_f = sb("iota_f", [P, P])
        ones_f = sb("ones_f", [P, P])
        zeros_b = sb("zeros_b", [P, P], BF16)
        bits = sb("bits", [P, 2], I32)
        dummy_row = sb("dummy_row", [P, 1])
        w1_sb = sb("w1_sb", [P, HID])
        b1_sb = sb("b1_sb", [P, 1])
        w2_sb = sb("w2_sb", [P, D])
        b2_sb = sb("b2_sb", [P, D])
        wfc_sb = sb("wfc_sb", [D, D])
        blk_sb = sb("blk_sb", [D, 6])
        we_sb = sb("we_sb", [2, 1])
        wedge_sb = sb("wedge_sb", [2, 2])
        we2nT_sb = sb("we2nT_sb", [2, D])
        wm_sb = sb("wm_sb", [D, 2, D])
        wz_sb = sb("wz_sb", [D, D + 2])
        q_sb = sb("q_sb", [P, 2])
        r_sb = sb("r_sb", [P, 2, D])
        v_sb = sb("v_sb", [P, 4, D])
        src_i = sb("src_i", [P, NT + SL * G], I32)
        dst_i = sb("dst_i", [P, NT], I32)
        dst_f = sb("dst_f", [P, NT])
        dst_p = sb("dst_p", [P, NT + G], BF16)
        dst_j = sb("dst_j", [P, NT + G], BF16)
        e2_sb = sb("e2_sb", [P, NT, 2])
        ee_sb = sb("ee_sb", [P, NT])
        x_sb = sb("x_sb", [P, NB, D])
        d_sb = sb("d_sb", [P, NB, D])
        z_sb = sb("z_sb", [P, NB, D + 2])
        work = sb("work", [P, max((NB + 1) * TW, 2 * G * CH * AW)])
        cnt_sb = sb("cnt_sb", [P, 2, NB])
        mean_sb = sb("mean_sb", [P, NB])
        var_sb = sb("var_sb", [P, NB])
        rstd_sb = sb("rstd_sb", [P, NB])
        t_sb = sb("t_sb", [P, NB])
        ea_sb = sb("ea_sb", [P, 2, G, EW])
        threshold = sb("threshold", [P, 1])
        srcf = sb("srcf", [P, 2, G])
        src_hi = sb("src_hi", [P, 2, G], BF16)
        src_lo = sb("src_lo", [P, 2, G], BF16)
        srchi_all = sb("srchi_all", [P, NT + G], BF16)
        srclo_all = sb("srclo_all", [P, NT + G], BF16)
        ident_b = sb("ident_b", [P, P], BF16)
        ohp = sb("ohp", [P, 2, 4, P], BF16)
        ohj = sb("ohj", [P, 2, 4, NB], BF16)
        same = sb("same", [P, 2, 4, P])
        todummy = sb("todummy", [P, 2, G])
        idx = sb("idx", [P, SL, G], I32)
        y_sb = sb("y_sb", [P, 2, G * EW])
        zg = sb("zg", [P, SL, G, RW])
        s_sb = sb("s_sb", [P, G])
        dloc = sb("dloc", [P, G])
        big_a = sb("big_a", [P, G, P])
        big_b = sb("big_b", [P, G, P])
        gmax = sb("gmax", [P, P])
        trow = sb("trow", [P, P])
        tab = sb("tab", [P, TW])
        mloc = sb("mloc", [P, 1])
        mnew = sb("mnew", [P, 1])
        rescale = sb("rescale", [P, 1])
        lo_all = sb("lo_all", [P, NM])
        hi_all = sb("hi_all", [P, NM])
        cum_f = sb("cum_f", [P, NM + 1])
        cum_i = sb("cum_i", [P, NM + 1], I32)
        base_i = sb("base_i", [P, NM], I32)
        tmp_m = sb("tmp_m", [P, NM])
        tmp_i = sb("tmp_i", [P, NM], I32)
        tmp_m2 = sb("tmp_m2", [P, NM])
        sums = sb("sums", [P, 2, D])
        mom = sb("mom", [P, 4, D])
        mabs = sb("mabs", [P, 4, D])
        msign = sb("msign", [P, 4, D])
        c_sb = sb("c_sb", [P, 1])
        far_f = sb("far_f", [P, 1])
        far_i = sb("far_i", [P, 1], I32)
        def f_big(k):
            return work[:, k * 2 * G * W:(k + 1) * 2 * G * W].rearrange("p (s g n) -> p s g n", s=2, g=G)

        f_masks, f_scores, f_probs = f_big(0), f_big(1), f_big(2)
        f_s = sb("f_s", [P, 2, G])
        f_dloc = sb("f_dloc", [P, G])
        f_t = sb("f_t", [P, 2, W])
        f_top = sb("f_top", [P, W])
        f_max = sb("f_max", [P, SL])
        f_new = sb("f_new", [P, 1])
        f_ratio = sb("f_ratio", [P, 2])
        f_fact = sb("f_fact", [P, 2])

        banks = [pb(f"bank{i}", [P, 512]) for i in range(8)]

        s_const = sem("s_const")
        s_work = sem("s_work")
        s_tab = [sem(f"s_tab{k}") for k in range(G)]
        s_zero = [sem(f"s_zero{k}") for k in range(G)]
        s_room = sem("s_room")
        s_w = sem("s_w")
        s_src = sem("s_src")
        s_dst = sem("s_dst")
        s_e2 = sem("s_e2")
        s_x = sem("s_x")
        s_ea = [sem(f"s_ea{k}") for k in range(2)]
        s_pad = sem("s_pad")
        s_stage = sem("s_stage")
        s_srcb = sem("s_srcb")
        s_oh = sem("s_oh")
        s_oh_used = sem("s_oh_used")
        s_same = sem("s_same")
        s_y = sem("s_y")
        s_ysb = sem("s_ysb")
        s_idx = sem("s_idx")
        s_held = [sem(f"s_held{k}") for k in range(4)]
        s_pool = sem("s_pool")
        s_dve = sem("s_dve")
        s_dve1 = sem("s_dve1")
        s_dve2 = sem("s_dve2")
        s_dve3 = sem("s_dve3")
        s_dve4 = sem("s_dve4")
        s_dve5 = sem("s_dve5")
        s_act = sem("s_act")
        s_prep = sem("s_prep")
        s_prep_sb = sem("s_prep_sb")
        s_cnt = sem("s_cnt")
        s_dsub = sem("s_dsub")
        s_sq = sem("s_sq")
        s_std = sem("s_std")
        s_vv = sem("s_vv")
        s_rstd = sem("s_rstd")
        s_acc = [sem(f"s_acc{k}") for k in range(2)]
        s_cat = sem("s_cat")
        s_agg = sem("s_agg")
        s_tr = sem("s_tr")
        s_trs = sem("s_trs")
        s_hid = sem("s_hid")
        s_hids = sem("s_hids")
        s_o = sem("s_o")
        s_x1 = sem("s_x1")
        s_zp = sem("s_zp")
        s_z = sem("s_z")
        s_zst = sem("s_zst")
        s_part = sem("s_part")
        s_psum = sem("s_psum")
        s_mom = sem("s_mom")
        s_root = sem("s_root")
        s_t = sem("s_t")
        s_tst = sem("s_tst")
        s_tabi = sem("s_tabi")
        s_neg = sem("s_neg")
        s_range = sem("s_range")
        s_win = sem("s_win")
        s_bits = sem("s_bits")
        s_pos = sem("s_pos")
        s_zg = [sem(f"s_zg{k}") for k in range(SL)]
        s_zg_used = sem("s_zg_used")
        s_rows = sem("s_rows")
        s_row_free = sem("s_row_free")
        s_mask = sem("s_mask")
        s_lin = sem("s_lin")
        s_gmax = sem("s_gmax")
        s_gT = sem("s_gT")
        s_mnew = sem("s_mnew")
        s_mrow = sem("s_mrow")
        s_sub = sem("s_sub")
        s_exp = sem("s_exp")
        s_agg1 = sem("s_agg1")
        s_tabn = sem("s_tabn")
        s_tabs = sem("s_tabs")
        s_fin = sem("s_fin")
        s_zfree = sem("s_zfree")
        f_trow = [sem(f"f_trow{k}") for k in range(2)]
        f_mask = sem("f_mask")
        f_lin = sem("f_lin")
        f_gmax = sem("f_gmax")
        f_gT = sem("f_gT")
        f_mloc = sem("f_mloc")
        f_mrow = sem("f_mrow")
        f_sub = sem("f_sub")
        f_exp = sem("f_exp")
        f_rows = sem("f_rows")
        f_diff = sem("f_diff")
        f_resc = sem("f_resc")
        f_tabn = sem("f_tabn")
        f_tabs = sem("f_tabs")
        f_link = [sem(f"f_link{k}") for k in range(4)]
        s_res = sem("s_res")
        s_out = sem("s_out")

        NEDGE_MAIN = (NM - 1) * ME
        NPARTS = 4
        zero_w = (NB + 1) * AW // 3

        def nodes_dma(eng, tile, dram, load, s):
            pairs = [(tile[0:FULL, :, :], dram[0:FULL * NB, :].rearrange("(p b) w -> p b w", p=FULL)),
                     (tile[FULL:FULL + 1, 0:REST, :], dram[FULL * NB:NODES, :].rearrange("(p b) w -> p b w", p=1))]
            for a, b in pairs:
                eng.dma_start(*((a, b) if load else (b, a))).then_inc(s, 16)

        block = ctx.enter_context(nc.Block())

        @block.sync
        def _(sp):
            nc_ = nc.sync
            sp.dma_start(src_i[:, 0:(NM - 1) * G].rearrange("p (m g) -> p m g", g=G),
                         src[0:NEDGE_MAIN].rearrange("(m p g) -> p m g", p=P, g=G)).then_inc(s_src, 16)
            sp.dma_start(src_i[:, (NM - 1) * G:NT], src[LAST0:EDGES].rearrange("(p g) -> p g", g=G)).then_inc(s_src, 16)
            sp.wait_ge(s_work, 1)
            for k in range(G):
                for h in range(3):
                    view = acc_dram[k].rearrange("(p r) c -> p (r c)", p=P)
                    sp.dma_start(view[:, h * zero_w:(h + 1) * zero_w], work[:, 0:zero_w]).then_inc(s_zero[k], 16)
                if k == 1:
                    sp.wait_ge(s_work, 2)
                    nodes_dma(sp, x_sb, x, True, s_x)
                    sp.dma_start(dst_i[:, 0:(NM - 1) * G].rearrange("p (m g) -> p m g", g=G),
                                 dst[0:NEDGE_MAIN].rearrange("(m p g) -> p m g", p=P, g=G)).then_inc(s_dst, 16)
                    sp.dma_start(dst_i[:, (NM - 1) * G:NT],
                                 dst[LAST0:EDGES].rearrange("(p g) -> p g", g=G)).then_inc(s_dst, 16)
            wa = W_attn.rearrange("a n -> n a")
            with nc.allow_non_contiguous_dma(reason="small transposed weights"):
                sp.dma_start(blk_sb[:, :], W_attn[0:1, 0:6 * D].rearrange("a (k d) -> d (a k)", k=6)).then_inc(s_w, 16)
                sp.dma_start(we_sb[:, :], wa[6 * D:6 * D + 2, :]).then_inc(s_w, 16)
                sp.dma_start(we2nT_sb[:, :], W_e2n.rearrange("f i -> i f")).then_inc(s_w, 16)
                sp.dma_start(b1_sb[:, :], b1.rearrange("(p a) -> p a", a=1)).then_inc(s_w, 16)
            sp.dma_start(w1_sb[:, :], W1).then_inc(s_w, 16)
            sp.dma_start(w2_sb[:, :], W2).then_inc(s_w, 16)
            sp.dma_start(b2_sb[:, :], b2.rearrange("(a d) -> a d", a=1).to_broadcast([P, D])).then_inc(s_w, 16)
            sp.dma_start(wfc_sb[:, :], W_fc).then_inc(s_w, 16)
            sp.dma_start(wedge_sb[:, :], W_edge).then_inc(s_w, 16)
            sp.dma_start(wm_sb[:, 0, :], W_m1).then_inc(s_w, 16)
            sp.dma_start(wm_sb[:, 1, :], W_m2).then_inc(s_w, 16)
            sp.dma_start(e2_sb[:, 0:(NM - 1) * G, :].rearrange("p (m g) c -> p m (g c)", g=G),
                         e2[0:NEDGE_MAIN, :].rearrange("(m p g) c -> p m (g c)", p=P, g=G)).then_inc(s_e2, 16)
            sp.dma_start(e2_sb[:, (NM - 1) * G:NT, :],
                         e2[LAST0:EDGES, :].rearrange("(p g) c -> p g c", g=G)).then_inc(s_e2, 16)

            def load_ea(s, m):
                rows = e64[bass.ds(m * ME, ME), :] if not isinstance(m, int) else e64[m * ME:(m + 1) * ME, :]
                sp.dma_start(ea_sb[:, s, :, 0:D], rows.rearrange("(p g) c -> p g c", g=G)).then_inc(s_ea[s], 16)

            sp.wait_ge(s_const, 1)
            load_ea(0, 0)
            load_ea(1, 1)
            with sp.Fori(1, NM // 2 - 1) as it:
                for s in range(2):
                    sp.wait_ge(s_y, it * 4 + 2 * s)
                    load_ea(s, it * 2 + s)
            sp.wait_ge(s_y, 2 * (NM - 2))
            load_ea(0, NM - 2)
            sp.wait_ge(s_y, 2 * (NM - 1))
            sp.dma_start(ea_sb[0:DUP, 1, :, 0:AW], work[0:DUP, 0:G * AW].rearrange("p (g c) -> p g c", g=G)
                         ).then_inc(s_pad, 16)
            sp.wait_ge(s_pad, 16)
            sp.dma_start(ea_sb[DUP:P, 1, :, 0:D],
                         e64[LAST0 + DUP * G:EDGES, :].rearrange("(p g) c -> p g c", g=G)).then_inc(s_ea[1], 16)

            for k in range(G):
                sp.wait_ge(s_tab[k], 16 * NM)
            with sp.Fori(0, NC // 2) as it:
                for s in range(2):
                    sp.wait_ge(s_agg, it * 2 + s + 1)
                    for k in range(G):
                        view = acc_dram[k][0:NPAD, :].rearrange("(p b) c -> p b c", p=P)
                        sp.dma_start(
                            work[:, s * G * CH * AW:(s + 1) * G * CH * AW].rearrange(
                                "p (k b c) -> p k b c", k=G, b=CH)[:, k, :, :],
                            view[:, bass.ds((it * 2 + s) * CH, CH), :]).then_inc(s_acc[s], 16)
            sp.wait_ge(s_z, NC)
            sp.dma_start(z_dram.rearrange("(p b) c -> p b c", p=P), z_sb[:, :, 0:ZW]).then_inc(s_zst, 16)
            sp.wait_ge(s_tabi, 1)
            sp.dma_start(tab_dram.rearrange("(p b) c -> p (b c)", p=P), work[:, 0:(NB + 1) * TW]).then_inc(s_tst, 16)
            sp.wait_ge(s_t, 1)
            sp.dma_start(t_dram[0:1, 0:NPAD].rearrange("a (p b) -> (a p) b", p=P), t_sb[:, :]).then_inc(s_tst, 16)
            sp.dma_start(t_dram[0:1, NPAD:NROWS].rearrange("a (p b) -> (a p) b", p=P), t_sb[:, 0:1]).then_inc(s_tst, 16)
            sp.wait_ge(s_tst, 48)
            sp.wait_ge(s_win, 1)
            far = sp.snap(sp.value_load(far_i[0:1, 0:1], min_val=0, max_val=1))

            def row_of(m):
                at = slice(m, m + 1) if isinstance(m, int) else bass.ds(m, 1)
                return sp.snap(sp.value_load(base_i[0:1, at], min_val=0, max_val=NODES - 1))

            def load_t(it, q):
                m = it * SL + q
                if isinstance(m, int) and m < 2:
                    pass
                else:
                    sp.wait_ge(f_mask, m - 1)
                sp.dma_start(f_t[:, q % 2, :], t_dram[0:1, bass.ds(row_of(m), W)].to_broadcast([P, W])
                             ).then_inc(f_trow[q % 2], 16)

            def update_rows(it, q):
                m = it * SL + q
                row = row_of(m)
                sp.dma_start(tab[0:W, :], tab_dram[bass.ds(row, W), :]).then_inc(f_rows, 16)
                sp.wait_ge(f_tabn, m + 1)
                sp.dma_start(tab_dram[bass.ds(row, W), :], tab[0:W, :]).then_inc(f_tabs, 16)
                sp.wait_ge(f_tabs, m * 16 + 16)
                sp.sem_inc(s_held[1], 1)

            with sp.If(far == 0):
                for q in range(SL):
                    load_t(0, q)
                    if q >= 3:
                        update_rows(0, q - 3)
                with sp.Fori(1, NM // SL) as it:
                    for q in range(SL):
                        load_t(it, q)
                        update_rows(it, q - 3)
                for q in range(3):
                    update_rows(NM // SL, q - 3)
            with sp.If(far == 1):
                with sp.Fori(0, NM) as m:
                    c0 = sp.snap(sp.value_load(cum_i[0:1, bass.ds(m, 1)], min_val=0, max_val=NM * NB))
                    c1 = sp.snap(sp.value_load(cum_i[0:1, bass.ds(m + 1, 1)], min_val=1, max_val=NM * NB))
                    first = sp.snap(sp.value_load(base_i[0:1, bass.ds(m, 1)], min_val=0, max_val=NODES - 1))
                    with sp.Fori(c0, c1) as i:
                        row = sp.snap(nc.s_assert_within(
                            first + (i - c0) * P, 0, NROWS - P,
                            skip_runtime_bounds_check_because="a window starts at or below the last destination"))
                        sp.dma_start(tab[:, :], tab_dram[bass.ds(row, P), :]).then_inc(s_rows, 16)
                        sp.dma_start(trow[:, :], t_dram[0:1, bass.ds(row, P)].to_broadcast([P, P])
                                     ).then_inc(s_rows, 16)
                        sp.wait_ge(s_tabn, i + 1)
                        sp.dma_start(tab_dram[bass.ds(row, P), :], tab[:, :]).then_inc(s_tabs, 16)
                        sp.wait_ge(s_tabs, i * 16 + 16)
                        sp.sem_inc(s_held[1], 1)
            sp.dma_start(work[:, 0:NB * TW], tab_dram[0:NPAD, :].rearrange("(p b) c -> p (b c)", p=P)).then_inc(s_fin, 16)
            sp.wait_ge(s_res, 1)
            nodes_dma(sp, x_sb, out, False, s_out)
            sp.wait_ge(s_out, 32)

        @block.gpsimd
        def _(pool):
            g_ = nc.gpsimd
            chain = Chain(pool, s_pool)
            chain(g_.memset(ones_f[:, :], 1.0))
            chain(g_.memset(ident[:, :], 0.0))
            chain(g_.affine_select(out=ident[:, :], in_=ident[:, :], compare_op=ALU.not_equal, fill=1.0, base=0,
                                   pattern=[[-1, P]], channel_multiplier=1))
            chain(g_.iota(src_iota := idx[:, 0, 0:1], pattern=[[0, 1]], base=NPAD, channel_multiplier=1))
            chain(g_.tensor_copy(dummy_row[:, :], src_iota))
            chain(g_.iota(cum_i[:, 0:P], pattern=[[1, P]], base=0, channel_multiplier=0))
            chain(g_.tensor_copy(iota_f[:, :], cum_i[:, 0:P]))
            chain(g_.tensor_copy(ident_b[:, :], ident[:, :]))
            chain(g_.iota(bits[:, 0:1], pattern=[[0, 1]], base=190, channel_multiplier=-1))
            g_.iota(bits[:, 1:2], pattern=[[0, 1]], base=191, channel_multiplier=-1).then_inc(s_bits, 1)
            chain(g_.memset(zeros_b[:, :], 0.0))
            for s in range(2):
                chain(g_.memset(ea_sb[:, s, :, D:AW], 1.0))
            for s in range(SL):
                chain(g_.memset(zg[:, s, :, ZW:ZW + 1], 1.0))
            g_.sem_inc(s_const, 1)
            def scatter_half(s, h, n, before):
                pool.wait_ge(s_ysb, n + 3)
                pool.wait_ge(s_idx, n + 2)
                for g in range(4 * h, 4 * h + 4):
                    if before is None:
                        pool.wait_ge(s_zero[g], 48)
                    else:
                        pool.wait_ge(s_tab[g], before)
                g_.sem_inc(s_room, 1)
                for g in range(4 * h, 4 * h + 4):
                    g_.indirect_dma_start(
                        out=acc_dram[g][:, :],
                        out_offset=bass.IndirectOffsetOnAxis(ap=idx[:, s, g:g + 1], axis=0),
                        in_=y_sb[:, s, g * EW:g * EW + AW], in_offset=None,
                        compute_op=ALU.add).then_inc(s_tab[g], 16)

            for n in range(4):
                scatter_half(n // 2, n % 2, n, 16 if n >= 2 else None)
            with pool.Fori(1, NM // 2) as it:
                for s in range(2):
                    for h in range(2):
                        scatter_half(s, h, it * 4 + (2 * s + h), it * 32 + 16 * s)
            pool.wait_ge(s_neg, 1)
            g_.partition_all_reduce(lo_all[:, :], lo_all[:, :], P, bass.bass_isa.ReduceOp.max).then_inc(s_range, 1)
            g_.partition_all_reduce(hi_all[:, :], hi_all[:, :], P, bass.bass_isa.ReduceOp.max).then_inc(s_range, 1)
            pool.wait_ge(s_zst, 16)
            with pool.Fori(0, NM // SL) as it:
                for s in range(SL):
                    pool.wait_ge(s_zg_used, it * SL + s + 1)
                    pool.wait_ge(s_zfree, it * SL + s + 1)
                    g_.sem_inc(s_held[0], 1)
                    for g in range(G):
                        g_.indirect_dma_start(
                            out=zg[:, s, g, 0:ZW], out_offset=None, in_=z_dram[:, :],
                            in_offset=bass.IndirectOffsetOnAxis(ap=idx[:, s, g:g + 1], axis=0)).then_inc(s_zg[s], 16)

        @block.scalar
        def _(act):
            a_ = nc.scalar
            act.wait_ge(s_dsub, 1)
            a_.activation(z_sb[:, :, 0:D], d_sb[:, :, :], ACT.Square).then_inc(s_sq, 1)
            act.wait_ge(s_vv, 1)
            a_.activation(var_sb[:, :], var_sb[:, :], ACT.Sqrt).then_inc(s_std, 1)
            with act.Fori(0, NM // 2) as it:
                for s in range(2):
                    for h in range(2):
                        act.wait_ge(s_y, it * 4 + 2 * s + h + 3)
                        act.wait_ge(s_room, it * 4 + 2 * s + h + 1)
                        a_.activation(y_sb[:, s, 4 * h * EW:4 * (h + 1) * EW], banks[4 + h][:, 0:4 * EW],
                                      ACT.Copy).then_inc(s_ysb, 1)
            with act.Fori(0, NC) as c:
                act.wait_ge(s_hid, c + 1)
                for h in range(2):
                    w = 512 if h == 0 else CH * P - 512
                    ins = a_.activation(big_b.rearrange("p g n -> p (g n)")[:, h * 512:h * 512 + w], banks[2 + h][:, 0:w],
                                        ACT.Relu, bias=b1_sb[:, 0:1])
                ins.then_inc(s_hids, 1)
            act.wait_ge(s_dsub, 2)
            a_.activation(work[:, 0:NB * D], d_sb.rearrange("p b d -> p (b d)"), ACT.Square).then_inc(s_sq, 1)
            act.wait_ge(s_vv, 2)
            a_.activation(var_sb[:, :], var_sb[:, :], ACT.Sqrt).then_inc(s_std, 1)
            with act.Fori(0, NC) as c:
                act.wait_ge(s_tr, c + (NC + 1))
                for h in range(2):
                    w = 512 if h == 0 else CH * P - 512
                    ins = a_.activation(big_b.rearrange("p g n -> p (g n)")[0:D, h * 512:h * 512 + w], banks[h][0:D, 0:w],
                                        ACT.Copy)
                ins.then_inc(s_trs, 1)
            act.wait_ge(s_mom, 1)
            ch = Chain(act, s_act)
            ch(a_.activation(mabs[:, :, :], mabs[:, :, :], ACT.Ln))
            ch(a_.activation(mabs[:, 0:2, :], mabs[:, 0:2, :], ACT.Exp, scale=0.5))
            a_.activation(mabs[:, 2:4, :], mabs[:, 2:4, :], ACT.Exp, scale=1.0 / 3.0).then_inc(s_root, 1)
            act.wait_ge(s_win, 1)
            far = act.snap(act.value_load(far_i[0:1, 0:1], min_val=0, max_val=1))

            def add_s(it, q):
                m = it * SL + q
                act.wait_ge(f_mask, m + 1)
                if not (isinstance(m, int) and m < 2):
                    act.wait_ge(f_exp, m - 1)
                for g in range(G):
                    ins = a_.activation(f_scores[:, q % 2, g, :], f_masks[:, q % 2, g, :], ACT.Identity,
                                        bias=f_s[:, q % 2, g:g + 1])
                ins.then_inc(f_lin, 1)

            def factors(it, q):
                act.wait_ge(f_diff, it * SL + q + 1)
                a_.activation(f_fact[0:W, :], f_ratio[0:W, :], ACT.Exp).then_inc(f_resc, 1)

            def exps(it, q):
                act.wait_ge(f_sub, it * SL + q + 1)
                a_.activation(f_probs[:, q % 2, :, :], f_scores[:, q % 2, :, :], ACT.Exp).then_inc(f_exp, 1)

            def act_step(it, q, first=False):
                add_s(it, q)
                if not first or q >= 2:
                    factors(it, q - 2)
                if not first or q >= 1:
                    exps(it, q - 1)

            with act.If(far == 0):
                for q in range(SL):
                    act_step(0, q, first=True)
                with act.Fori(1, NM // SL) as it:
                    for q in range(SL):
                        act_step(it, q)
                factors(NM // SL, -2)
                exps(NM // SL, -1)
                factors(NM // SL, -1)
            with act.If(far == 1):
                with act.Fori(0, NM) as m:
                    c0 = act.snap(act.value_load(cum_i[0:1, bass.ds(m, 1)], min_val=0, max_val=NM * NB))
                    c1 = act.snap(act.value_load(cum_i[0:1, bass.ds(m + 1, 1)], min_val=1, max_val=NM * NB))
                    with act.Fori(c0, c1) as i:
                        act.wait_ge(s_mask, i + 1)
                        for g in range(G):
                            ins = a_.activation(big_b[:, g, :], big_a[:, g, :], ACT.Identity, bias=s_sb[:, g:g + 1])
                        ins.then_inc(s_lin, 1)
                        act.wait_ge(s_sub, i + 1)
                        a_.activation(rescale[:, :], mloc[:, :], ACT.Exp)
                        a_.activation(big_a[:, :, :], big_b[:, :, :], ACT.Exp).then_inc(s_exp, 1)

        @block.tensor
        def _(pe):
            t_ = nc.tensor
            pe.wait_ge(s_const, 1)
            pe.wait_ge(s_w, 16 * 11)
            t_.transpose(banks[0][0:D, 0:D], wfc_sb[:, :], ident[0:D, 0:D])
            t_.matmul(banks[0][0:D, D:D + 1], wfc_sb[:, :], blk_sb[:, 0:1], start=True, stop=True)
            t_.matmul(banks[0][0:D, D + 1:D + 2], wfc_sb[:, :], blk_sb[:, 3:4], start=True, stop=True)
            t_.matmul(banks[1][:, 0:2], we_sb[:, 0:1].to_broadcast([2, P]), wedge_sb[:, :], start=True, stop=True)
            for j in range(2):
                t_.matmul(banks[2][:, j * D:(j + 1) * D], wedge_sb[:, j:j + 1].to_broadcast([2, P]), we2nT_sb[:, :],
                          start=True, stop=True)
            for k, b in enumerate((1, 4, 2, 5)):
                ins = t_.matmul(banks[3][:, k * D:(k + 1) * D], blk_sb[:, b:b + 1].to_broadcast([D, P]),
                                wm_sb[:, k // 2, :], start=True, stop=True)
            ins.then_inc(s_prep, 1)
            t_.matmul(banks[6][:, 0:NB], zeros_b[:, :], zeros_b[:, 0:NB], start=True, stop=False)
            pe.wait_ge(s_prep_sb, 1)
            pe.wait_ge(s_pos, 2)
            def spread_sources(bank, s, h, n, m):
                pe.wait_ge(s_stage, m + 1)
                pe.wait_ge(s_same, n + 1)
                for j in range(4):
                    for part, half in enumerate((src_hi, src_lo)):
                        ins = t_.matmul(banks[bank][:, j * P:(j + 1) * P],
                                        half[:, s, 4 * h + j:4 * h + j + 1].to_broadcast([P, P]), ident_b[:, :],
                                        start=(part == 0), stop=(part == 1))
                ins.then_inc(s_srcb, 1)

            spread_sources(0, 0, 0, 0, 0)
            with pe.Fori(0, NM // 2) as it:
                for q in range(4):
                    s, h = divmod(q, 2)
                    n = it * 4 + q
                    r = (q + 1) % 4
                    spread_sources(r, r // 2, r % 2, n + 1, it * 2 + (q + 1) // 2)
                    pe.wait_ge(s_oh, n + 1)
                    for j in range(4):
                        ins = t_.matmul(banks[6][:, 0:NB], ohp[:, h, j, :], ohj[:, h, j, :], start=False, stop=False)
                    ins.then_inc(s_oh_used, 1)
                    pe.wait_ge(s_same, n + 5)
                    if h == 0:
                        pe.wait_ge(s_ea[s], it * 16 + 16)
                    pe.wait_ge(s_ysb, n + 1)
                    for j in range(4):
                        ins = t_.matmul(banks[4 + h][:, j * EW:(j + 1) * EW], same[:, h, j, :],
                                        ea_sb[:, s, 4 * h + j, :], start=True, stop=True)
                    ins.then_inc(s_y, 1)
            t_.matmul(banks[6][:, 0:NB], zeros_b[:, :], zeros_b[:, 0:NB], start=False, stop=True).then_inc(s_cnt, 1)
            catT = big_a.rearrange("p g n -> p (g n)")
            hidT = big_b.rearrange("p g n -> p (g n)")
            cat = y_sb.rearrange("p s w -> p (s w)")
            with pe.Fori(0, NC) as c:
                pe.wait_ge(s_cat, c + 1)
                for b in range(CH):
                    ins = t_.transpose(banks[b // 4][:, (b % 4) * P:(b % 4 + 1) * P], cat[:, b * P:(b + 1) * P], ident[:, :])
                ins.then_inc(s_tr, 1)
                pe.wait_ge(s_trs, c + 1)
                t_.matmul(banks[2][:, 0:512], w1_sb[:, :], catT[:, 0:512], start=True, stop=True)
                t_.matmul(banks[3][:, 0:CH * P - 512], w1_sb[:, :], catT[:, 512:CH * P], start=True, stop=True
                          ).then_inc(s_hid, 1)
                pe.wait_ge(s_hids, c + 1)
                for b in range(CH):
                    ins = t_.matmul(banks[4][:, b * D:(b + 1) * D], hidT[:, b * P:(b + 1) * P], w2_sb[:, :],
                                    start=True, stop=True)
                ins.then_inc(s_o, 1)
            with pe.Fori(0, NC) as c:
                pe.wait_ge(s_cat, c + (NC + 1))
                pe.sem_inc(s_held[3], 1)
                for b in range(CH):
                    ins = t_.transpose(banks[b // 4][0:D, (b % 4) * P:(b % 4 + 1) * P], cat[:, b * D:(b + 1) * D],
                                       ident[:, :])
                ins.then_inc(s_tr, 1)
                pe.wait_ge(s_trs, c + (NC + 1))
                for b in range(CH):
                    ins = t_.matmul(banks[2][:, b * (D + 2):(b + 1) * (D + 2)], hidT[0:D, b * P:(b + 1) * P], wz_sb[:, :],
                                    start=True, stop=True)
                ins.then_inc(s_zp, 1)
            pe.wait_ge(s_part, 1)
            t_.matmul(banks[5][:, 0:2 * D], ones_f[:, :], sums.rearrange("p a d -> p (a d)"), start=True, stop=True
                      ).then_inc(s_psum, 1)
            pe.wait_ge(s_part, 2)
            t_.matmul(banks[5][:, 0:4 * D], ones_f[:, :], mom.rearrange("p a d -> p (a d)"), start=True, stop=True
                      ).then_inc(s_psum, 1)
            pe.wait_ge(s_win, 1)
            far = pe.snap(pe.value_load(far_i[0:1, 0:1], min_val=0, max_val=1))

            def maxima(it, q):
                m = it * SL + q
                pe.wait_ge(f_gmax, m + 1)
                t_.transpose(banks[0][0:W, 0:P], f_top[:, :], ident[:, :]).then_inc(f_gT, 1)
                pe.wait_ge(f_mloc, m + 1)
                t_.matmul(banks[1][:, 0:W], f_max[0:W, q:q + 1].to_broadcast([W, P]), ident[0:W, 0:W],
                          start=True, stop=True).then_inc(f_mrow, 1)

            def weighted_sums(it, q):
                pe.wait_ge(f_exp, it * SL + q + 1)
                for g in range(G):
                    ins = t_.matmul(banks[2 + q % 2][0:W, 0:RW], f_probs[:, q % 2, g, :], zg[:, q % SL, g, :],
                                    start=(g == 0), stop=(g == G - 1))
                ins.then_inc(s_zfree, 1)

            with pe.If(far == 0):
                for q in range(SL):
                    maxima(0, q)
                    if q >= 1:
                        weighted_sums(0, q - 1)
                with pe.Fori(1, NM // SL) as it:
                    for q in range(SL):
                        maxima(it, q)
                        weighted_sums(it, q - 1)
                weighted_sums(NM // SL, -1)
            with pe.If(far == 1):
                with pe.Fori(0, NM // SL) as it:
                    for s in range(SL):
                        c0 = pe.snap(pe.value_load(cum_i[0:1, bass.ds(it * SL + s, 1)], min_val=0, max_val=NM * NB))
                        c1 = pe.snap(pe.value_load(cum_i[0:1, bass.ds(it * SL + s + 1, 1)], min_val=1, max_val=NM * NB))
                        with pe.Fori(c0, c1) as i:
                            pe.wait_ge(s_gmax, i + 1)
                            t_.transpose(banks[0][:, 0:P], gmax[:, :], ident[:, :]).then_inc(s_gT, 1)
                            pe.wait_ge(s_mnew, i + 1)
                            t_.matmul(banks[1][:, 0:P], mnew[:, 0:1].to_broadcast([P, P]), ident[:, :], start=True, stop=True
                                      ).then_inc(s_mrow, 1)
                            pe.wait_ge(s_exp, i + 1)
                            for g in range(G):
                                ins = t_.matmul(banks[2][:, 0:RW], big_a[:, g, :], zg[:, s, g, :], start=(g == 0),
                                                stop=(g == G - 1))
                            ins.then_inc(s_agg1, 1)

        @block.vector
        def _(dve):
            v_ = nc.vector
            ch = Chain(dve, s_dve)
            v_.memset(work[:, :], 0.0).then_inc(s_work, 1)
            v_.memset(x_sb[:, :, :], 0.0).then_inc(s_work, 1)
            dve.sem_inc(s_same, 4)
            dve.sem_inc(s_ysb, 2)
            dve.sem_inc(s_idx, 1)
            dve.sem_inc(s_room, 2)
            dve.sem_inc(s_y, 2)
            dve.sem_inc(s_oh_used, 2)
            dve.wait_ge(s_prep, 1)
            v_.tensor_copy(wz_sb[:, :], banks[0][0:D, 0:D + 2])
            v_.tensor_copy(q_sb[:, :], banks[1][:, 0:2])
            v_.tensor_copy(r_sb.rearrange("p a d -> p (a d)"), banks[2][:, 0:2 * D])
            v_.tensor_copy(v_sb.rearrange("p a d -> p (a d)"), banks[3][:, 0:4 * D]).then_inc(s_prep_sb, 1)
            dve.wait_ge(s_prep_sb, 1)

            def wide(a, n):
                return a.unsqueeze(2).to_broadcast([P, NB, n])

            def layernorm_stats(n, xs, sq):
                ch(v_.tensor_reduce(mean_sb[:, :], xs, X_AXIS, ALU.add))
                ch(v_.tensor_scalar(mean_sb[:, :], mean_sb[:, :], 1.0 / D, None, ALU.mult))
                v_.tensor_tensor(d_sb[:, :, :], xs, wide(mean_sb[:, :], D), ALU.subtract).then_inc(s_dsub, 1)
                dve.wait_ge(s_sq, n)
                ch(v_.tensor_reduce(var_sb[:, :], sq, X_AXIS, ALU.add))
                v_.tensor_scalar(var_sb[:, :], var_sb[:, :], 1.0 / D, EPS, ALU.mult, ALU.add).then_inc(s_vv, 1)
                dve.wait_ge(s_std, n)
                v_.reciprocal(rstd_sb[:, :], var_sb[:, :]).then_inc(s_rstd, 1)
                dve.wait_ge(s_rstd, n)
                dve.wait_ge(s_dsub, n)

            dve.wait_ge(s_dst, 32)
            ch(v_.tensor_copy(dst_f[:, :], dst_i[:, :]))
            ch(v_.tensor_scalar(dst_i[:, :], dst_f[:, :], 1.0 / NB, None, ALU.mult))
            ch(v_.tensor_copy(dst_p[:, 0:NT], dst_i[:, :]))
            ch(v_.scalar_tensor_tensor(out=dst_j[:, 0:NT], in0=dst_p[:, 0:NT], scalar=-float(NB), in1=dst_f[:, :],
                                       op0=ALU.mult, op1=ALU.add))
            ch(v_.tensor_scalar(ee_sb[:, :], dst_j[:, 0:NT], 0.0, None, ALU.is_lt))
            ch(v_.tensor_tensor(dst_p[:, 0:NT], dst_p[:, 0:NT], ee_sb[:, :], ALU.subtract))
            ch(v_.scalar_tensor_tensor(out=dst_j[:, 0:NT], in0=ee_sb[:, :], scalar=float(NB), in1=dst_j[:, 0:NT],
                                       op0=ALU.mult, op1=ALU.add))
            ch(v_.memset(dst_p[0:DUP, (NM - 1) * G:NT], -1.0))
            ch(v_.memset(dst_p[:, NT:NT + G], -1.0))
            ch(v_.memset(dst_j[:, NT:NT + G], -1.0))
            ch(v_.tensor_reduce(hi_all[:, :], dst_f.rearrange("p (m g) -> p m g", g=G), X_AXIS, ALU.max))
            ch(v_.tensor_reduce(lo_all[:, :], dst_f.rearrange("p (m g) -> p m g", g=G), X_AXIS, ALU.min))
            v_.tensor_scalar(lo_all[:, :], lo_all[:, :], -1.0, None, ALU.mult).then_inc(s_neg, 1)
            dve.wait_ge(s_x, 32)
            layernorm_stats(1, x_sb[:, :, :], z_sb[:, :, 0:D])
            ch(v_.tensor_tensor(x_sb[:, :, :], x_sb[:, :, :], b2_sb[:, :].unsqueeze(1).to_broadcast([P, NB, D]), ALU.add))
            dve.wait_ge(s_src, 32)

            ch(v_.tensor_scalar(dst_i[:, :], src_i[:, 0:NT], P - 1, None, ALU.bitwise_and))
            ch(v_.memset(srclo_all[:, NT:NT + G], 0.0))
            ch(v_.memset(srchi_all[:, NT:NT + G], 0.0))
            ch(v_.tensor_copy(srclo_all[:, 0:NT], dst_i[:, :]))
            ch(v_.tensor_copy(ee_sb[:, :], src_i[:, 0:NT]))
            ch(v_.tensor_tensor(srchi_all[:, 0:NT], ee_sb[:, :], srclo_all[:, 0:NT], ALU.subtract))
            dve.wait_ge(s_bits, 1)
            ch(v_.tensor_scalar(bits[:, :], bits[:, :], 23, None, ALU.logical_shift_left))
            for s in range(2):
                v_.tensor_copy(ea_sb[:, s, :, AW:EW], bits[:, 0:1].bitcast(F32).unsqueeze(1).to_broadcast([P, G, 1])
                               ).then_inc(s_pos, 1)
            ch(v_.tensor_scalar(threshold[:, :], bits[:, 1:2].bitcast(F32), 1.5, None, ALU.mult))

            def stage(s, m, col):
                v_.tensor_scalar(src_lo[:, s, :], srclo_all[:, bass.ds(col, G)], 0.0, None, ALU.add)
                v_.tensor_scalar(src_hi[:, s, :], srchi_all[:, bass.ds(col, G)], 0.0, None, ALU.add)
                v_.tensor_tensor(srcf[:, s, :], srclo_all[:, bass.ds(col, G)], srchi_all[:, bass.ds(col, G)], ALU.add
                                 ).then_inc(s_stage, 1)
                dve.wait_ge(s_stage, m + 1)

            def onehots(h, n, col):
                dve.wait_ge(s_oh_used, n + 1)
                v_.tensor_tensor(ohp[:, h, :, :], iota_f[:, :].unsqueeze(1).to_broadcast([P, 4, P]),
                                 dst_p[:, bass.ds(col, 4)].unsqueeze(2).to_broadcast([P, 4, P]), ALU.is_equal)
                v_.tensor_tensor(ohj[:, h, :, :], iota_f[:, 0:NB].unsqueeze(1).to_broadcast([P, 4, NB]),
                                 dst_j[:, bass.ds(col, 4)].unsqueeze(2).to_broadcast([P, 4, NB]),
                                 ALU.is_equal).then_inc(s_oh, 1)

            stage(0, 0, 0)
            onehots(0, 0, 0)
            with dve.Fori(0, NM // 2) as it:
                c1 = Chain(dve, s_dve1, it * 8)
                for q in range(4):
                    s, h = divmod(q, 2)
                    n = it * 4 + q
                    half = srcf[:, s, 4 * h:4 * h + 4]
                    dve.wait_ge(s_srcb, n + 1)
                    dve.wait_ge(s_y, n + 1)
                    v_.tensor_tensor(same[:, h, :, :], banks[q][:, :].rearrange("p (j e) -> p j e", j=4),
                                     half.unsqueeze(2).to_broadcast([P, 4, P]), ALU.is_equal).then_inc(s_same, 1)
                    if h == 0:
                        dve.wait_ge(s_idx, n + 1)
                        stage((s + 1) % 2, it * 2 + s + 1, it * (2 * G) + (s + 1) * G)
                    onehots((h + 1) % 2, n + 1, it * (2 * G) + 4 * (q + 1))
                    c1(v_.tensor_scalar(todummy[:, s, 4 * h:4 * h + 4], half, -1.0, dummy_row[:, 0:1],
                                        ALU.mult, ALU.add))
                    dve.wait_ge(s_ysb, n + 3)
                    weight = y_sb[:, s, 4 * h * EW:4 * (h + 1) * EW].rearrange("p (j c) -> p j c", j=4)[:, :, AW]
                    c1(v_.scalar_tensor_tensor(out=todummy[:, s, 4 * h:4 * h + 4], in0=weight,
                                               scalar=threshold[:, 0:1], in1=todummy[:, s, 4 * h:4 * h + 4],
                                               op0=ALU.is_ge, op1=ALU.mult))
                    dve.wait_ge(s_room, n + 1)
                    v_.tensor_tensor(idx[:, s, 4 * h:4 * h + 4], todummy[:, s, 4 * h:4 * h + 4], half, ALU.add
                                     ).then_inc(s_idx, 1)

            dve.wait_ge(s_cnt, 1)
            ch(v_.tensor_copy(cnt_sb[:, 1, :], banks[6][:, 0:NB]))
            cat = y_sb.rearrange("p s w -> p (s w)")
            catT = big_a.rearrange("p g n -> p (g n)")
            dve.sem_inc(s_agg, 2)
            dve.wait_ge(s_ysb, 2 * NM + 2)
            for k in range(G):
                dve.wait_ge(s_tab[k], 16 * NM)
            with dve.Fori(0, NC // 2) as it:
                for s in range(2):
                    c = it * 2 + s
                    cc = Chain(dve, s_dve3, c * 2)
                    cols = cat[:, 0:CH * P].rearrange("p (b f) -> p b f", b=CH)
                    cc(v_.scalar_tensor_tensor(
                        out=cols[:, :, 0:D], in0=d_sb[:, bass.ds(c * CH, CH), :], scalar=0.0,
                        in1=rstd_sb[:, bass.ds(c * CH, CH)].unsqueeze(2).to_broadcast([P, CH, D]),
                        op0=ALU.max, op1=ALU.mult))
                    dve.wait_ge(s_acc[s], it * (16 * G) + 16 * G)
                    rows = work[:, s * G * CH * AW:(s + 1) * G * CH * AW].rearrange("p (k b c) -> p b c k", k=G, b=CH)
                    v_.tensor_reduce(cols[:, :, D:2 * D], rows[:, :, 0:D, :], X_AXIS, ALU.add).then_inc(s_cat, 1)
                    v_.tensor_reduce(cnt_sb[:, 0, bass.ds(c * CH, CH)], rows[:, :, D, :], X_AXIS, ALU.add
                                     ).then_inc(s_agg, 1)
                    dve.wait_ge(s_tr, c + 1)
                    v_.tensor_copy(catT[:, 0:512], banks[0][:, 0:512])
                    v_.tensor_copy(catT[:, 512:CH * P], banks[1][:, 0:CH * P - 512]).then_inc(s_trs, 1)
                    dve.wait_ge(s_o, c + 1)
                    xc = x_sb[:, bass.ds(c * CH, CH), :]
                    cc(v_.tensor_tensor(xc, xc, banks[4][:, 0:CH * D].rearrange("p (b d) -> p b d", b=CH), ALU.add))
            dve.wait_ge(s_agg, NC + 2)
            layernorm_stats(2, x_sb[:, :, :], work[:, 0:NB * D].rearrange("p (b d) -> p b d", d=D))
            with dve.Fori(0, NC) as c:
                v_.scalar_tensor_tensor(
                    out=cat[:, 0:CH * D].rearrange("p (b f) -> p b f", b=CH), in0=d_sb[:, bass.ds(c * CH, CH), :],
                    scalar=0.0, in1=rstd_sb[:, bass.ds(c * CH, CH)].unsqueeze(2).to_broadcast([P, CH, D]),
                    op0=ALU.max, op1=ALU.mult).then_inc(s_cat, 1)
                dve.wait_ge(s_zp, c + 1)
                v_.tensor_scalar(z_sb[:, bass.ds(c * CH, CH), :],
                                 banks[2][:, 0:CH * (D + 2)].rearrange("p (b f) -> p b f", b=CH), 0.0, None, ALU.add
                                 ).then_inc(s_z, 1)
            dve.wait_ge(s_z, NC)
            ch(v_.memset(src_i[:, NT:NT + SL * G], 0))
            for s in range(SL):
                v_.tensor_copy(idx[:, s, :], src_i[:, s * G:(s + 1) * G]).then_inc(s_zg_used, 1)
            w = work[:, 0:NB * D].rearrange("p (b d) -> p b d", d=D)
            z = z_sb[:, :, 0:D]
            for a in range(2):
                ch(v_.tensor_tensor(w, z, wide(cnt_sb[:, a, :], D), ALU.mult))
                ch(v_.tensor_reduce(sums[:, a, :], w.rearrange("p b d -> p d b"), X_AXIS, ALU.add))
            dve.sem_inc(s_part, 1)
            dve.wait_ge(s_psum, 1)
            ch(v_.tensor_scalar(sums.rearrange("p a d -> p (a d)"), banks[5][:, 0:2 * D], 1.0 / EDGES, None, ALU.mult))
            for a in range(2):
                mu = sums[:, a, :].unsqueeze(1).to_broadcast([P, NB, D])
                ch(v_.tensor_tensor(d_sb[:, :, :], z, mu, ALU.subtract))
                ch(v_.tensor_tensor(w, d_sb[:, :, :], d_sb[:, :, :], ALU.mult))
                ch(v_.tensor_tensor(w, w, wide(cnt_sb[:, a, :], D), ALU.mult))
                ch(v_.tensor_reduce(mom[:, a, :], w.rearrange("p b d -> p d b"), X_AXIS, ALU.add))
                ch(v_.tensor_tensor(w, w, d_sb[:, :, :], ALU.mult))
                ch(v_.tensor_reduce(mom[:, 2 + a, :], w.rearrange("p b d -> p d b"), X_AXIS, ALU.add))
            dve.sem_inc(s_part, 1)
            ch(v_.memset(work[:, 0:(NB + 1) * TW], 0.0))
            v_.memset(work[:, 0:(NB + 1) * TW].rearrange("p (b c) -> p b c", c=TW)[:, :, RW:TW], FLOOR).then_inc(s_tabi, 1)
            dve.wait_ge(s_psum, 2)
            flat = lambda a: a.rearrange("p a d -> p (a d)")
            ch(v_.tensor_scalar(flat(mom), banks[5][:, 0:4 * D], 1.0 / EDGES, None, ALU.mult))
            ch(v_.tensor_scalar(flat(mabs), flat(mom), -1.0, None, ALU.mult))
            ch(v_.tensor_tensor(flat(mabs), flat(mabs), flat(mom), ALU.max))
            ch(v_.tensor_scalar(flat(msign), flat(mom), 0.0, None, ALU.is_lt))
            ch(v_.scalar_tensor_tensor(out=flat(msign), in0=flat(mom), scalar=0.0, in1=flat(msign), op0=ALU.is_gt,
                                       op1=ALU.subtract))
            v_.tensor_scalar(flat(mabs), flat(mabs), 1e-37, None, ALU.max).then_inc(s_mom, 1)
            dve.wait_ge(s_root, 1)
            ch(v_.tensor_tensor(flat(mabs), flat(mabs), flat(msign), ALU.mult))
            ch(v_.tensor_tensor(flat(mabs), flat(mabs), flat(v_sb), ALU.mult))
            ch(v_.tensor_reduce(c_sb[:, :], flat(mabs), X_AXIS, ALU.add))
            v_.tensor_scalar(t_sb[:, :], z_sb[:, :, D + 1], c_sb[:, 0:1], None, ALU.add).then_inc(s_t, 1)
            dve.wait_ge(s_e2, 32)
            ch(v_.tensor_scalar(ee_sb[:, :], e2_sb[:, :, 0], q_sb[:, 0:1], None, ALU.mult))
            ch(v_.scalar_tensor_tensor(out=ee_sb[:, :], in0=e2_sb[:, :, 1], scalar=q_sb[:, 1:2], in1=ee_sb[:, :],
                                       op0=ALU.mult, op1=ALU.add))
            ch(v_.memset(ee_sb[0:DUP, (NM - 1) * G:NT], OFF))
            dve.wait_ge(s_range, 2)
            ch(v_.tensor_scalar(base_i[:, :], lo_all[:, :], -1.0, None, ALU.mult))
            ch(v_.tensor_tensor(tmp_i[:, :], hi_all[:, :], lo_all[:, :], ALU.add))
            ch(v_.tensor_scalar(tmp_i[:, :], tmp_i[:, :], P.bit_length() - 1, None, ALU.arith_shift_right))
            ch(v_.tensor_copy(tmp_m[:, :], tmp_i[:, :]))
            ch(v_.tensor_scalar(tmp_m[:, :], tmp_m[:, :], 1.0, None, ALU.add))
            ch(v_.tensor_tensor(tmp_m2[:, :], hi_all[:, :], lo_all[:, :], ALU.add))
            ch(v_.tensor_reduce(far_f[:, :], tmp_m2[:, :], X_AXIS, ALU.max))
            ch(v_.tensor_scalar(far_i[:, :], far_f[:, :], float(W), None, ALU.is_ge))
            ch(v_.memset(cum_f[:, 0:1], 0.0))
            ch(v_.tensor_tensor_scan(cum_f[:, 1:NM + 1], ones_f[:, 0:1].to_broadcast([P, NM]), tmp_m[:, :], 0.0, ALU.mult, ALU.add))
            v_.tensor_copy(cum_i[:, :], cum_f[:, :]).then_inc(s_win, 1)
            dve.wait_ge(s_win, 1)

            dve.sem_inc(s_zfree, SL)
            dve.wait_ge(s_tst, 48)
            far = dve.snap(dve.value_load(far_i[0:1, 0:1], min_val=0, max_val=1))

            def masks(it, q):
                m, col = it * SL + q, (it * SL + q) * G
                link = Chain(dve, f_link[0], m * 2)
                dve.wait_ge(s_zg[q], it * (16 * G) + 16 * G)
                v_.tensor_scalar(idx[:, q, :], src_i[:, bass.ds(col + SL * G, G)], 0.0, None, ALU.add
                                 ).then_inc(s_zg_used, 1)
                v_.tensor_tensor(f_s[:, q % 2, :], zg[:, q, :, D], ee_sb[:, bass.ds(col, G)], ALU.add)
                v_.tensor_scalar(zg[:, q, :, ZW + 1:RW], e2_sb[:, bass.ds(col, G), :], 0.0, None, ALU.add)
                link(v_.tensor_scalar(f_dloc[:, :], dst_f[:, bass.ds(col, G)], lo_all[:, bass.ds(m, 1)], None, ALU.add))
                mask = f_masks[:, q % 2, :, :]
                link(v_.tensor_tensor(mask, iota_f[:, 0:W].unsqueeze(1).to_broadcast([P, G, W]),
                                      f_dloc[:, :].unsqueeze(2).to_broadcast([P, G, W]), ALU.not_equal))
                dve.wait_ge(f_trow[q % 2], it * (8 * SL) + (q // 2 + 1) * 16)
                v_.scalar_tensor_tensor(out=mask, in0=mask, scalar=OFF,
                                        in1=f_t[:, q % 2, :].unsqueeze(1).to_broadcast([P, G, W]),
                                        op0=ALU.mult, op1=ALU.add).then_inc(f_mask, 1)

            def new_maxima(it, q):
                m, k = it * SL + q, q % SL
                link = Chain(dve, f_link[1], m * 3)
                dve.wait_ge(f_rows, m * 16 + 16)
                link(v_.tensor_tensor(f_new[0:W, :], f_max[0:W, k:k + 1], tab[0:W, RW:TW], ALU.max))
                v_.tensor_tensor(f_ratio[0:W, 0:1], tab[0:W, RW:TW], f_new[0:W, :], ALU.subtract)
                v_.tensor_tensor(f_ratio[0:W, 1:2], f_max[0:W, k:k + 1], f_new[0:W, :], ALU.subtract
                                 ).then_inc(f_diff, 1)
                dve.wait_ge(f_diff, m + 1)
                link(v_.tensor_scalar(tab[0:W, RW:TW], f_new[0:W, :], 0.0, None, ALU.add))
                dve.wait_ge(f_resc, m + 1)
                link(v_.tensor_scalar(tab[0:W, 0:RW], tab[0:W, 0:RW], f_fact[0:W, 0:1], None, ALU.mult))

            def less_maxima(it, q):
                m = it * SL + q
                dve.wait_ge(f_mrow, m + 1)
                scores = f_scores[:, q % 2, :, :]
                v_.tensor_tensor(scores, scores, banks[1][:, 0:W].unsqueeze(1).to_broadcast([P, G, W]), ALU.subtract
                                 ).then_inc(f_sub, 1)

            def scores_top(it, q):
                m = it * SL + q
                link = Chain(dve, f_link[2], m)
                dve.wait_ge(f_lin, m + 1)
                scores = f_scores[:, q % 2, :, :]
                link(v_.scalar_tensor_tensor(out=scores, in0=scores, scalar=SLOPE, in1=scores, op0=ALU.mult,
                                             op1=ALU.max))
                v_.tensor_reduce(f_top[:, :], scores.rearrange("p g n -> p n g"), X_AXIS, ALU.max).then_inc(f_gmax, 1)

            def merge(it, q):
                dve.wait_ge(s_zfree, it * SL + q + SL + 1)
                v_.scalar_tensor_tensor(out=tab[0:W, 0:RW], in0=banks[2 + q % 2][0:W, 0:RW], scalar=f_fact[0:W, 1:2],
                                        in1=tab[0:W, 0:RW], op0=ALU.mult, op1=ALU.add).then_inc(f_tabn, 1)

            def segment_maxima(it, q):
                m = it * SL + q
                link = Chain(dve, f_link[3], m)
                dve.wait_ge(f_gT, m + 1)
                link(v_.tensor_reduce(f_max[0:W, q:q + 1], banks[0][0:W, 0:P], X_AXIS, ALU.max))
                v_.tensor_scalar(f_max[0:W, q:q + 1], f_max[0:W, q:q + 1], FLOOR, None, ALU.max).then_inc(f_mloc, 1)

            def dve_step(it, q, first=False):
                masks(it, q)
                if not first or q >= 1:
                    less_maxima(it, q - 1)
                scores_top(it, q)
                if not first or q >= 2:
                    new_maxima(it, q - 2)
                    merge(it, q - 2)
                segment_maxima(it, q)

            with dve.If(far == 0):
                for q in range(SL):
                    dve_step(0, q, first=True)
                with dve.Fori(1, NM // SL) as it:
                    for q in range(SL):
                        dve_step(it, q)
                last = NM // SL
                less_maxima(last, -1)
                for q in (-2, -1):
                    new_maxima(last, q)
                    merge(last, q)
            with dve.If(far == 1):
                with dve.Fori(0, NM // SL) as it:
                    for s in range(SL):
                        m = it * SL + s
                        col = it * (SL * G) + s * G
                        c0 = dve.snap(dve.value_load(cum_i[0:1, bass.ds(m, 1)], min_val=0, max_val=NM * NB))
                        c1 = dve.snap(dve.value_load(cum_i[0:1, bass.ds(m + 1, 1)], min_val=1, max_val=NM * NB))
                        cm = Chain(dve, s_dve4, m * 3)
                        dve.wait_ge(s_zg[s], it * (16 * G) + 16 * G)
                        cm(v_.tensor_tensor(s_sb[:, :], zg[:, s, :, D], ee_sb[:, bass.ds(col, G)], ALU.add))
                        cm(v_.tensor_scalar(zg[:, s, :, ZW + 1:RW], e2_sb[:, bass.ds(col, G), :], 0.0, None, ALU.add))
                        cm(v_.tensor_scalar(dloc[:, :], dst_f[:, bass.ds(col, G)], lo_all[:, bass.ds(m, 1)], None, ALU.add))
                        dve.sem_inc(s_held[2], 1)
                        with dve.Fori(c0, c1) as i:
                            cw = Chain(dve, s_dve5, i * 6)
                            cw(v_.tensor_tensor(big_a[:, :, :], iota_f[:, :].unsqueeze(1).to_broadcast([P, G, P]),
                                                dloc[:, :].unsqueeze(2).to_broadcast([P, G, P]), ALU.not_equal))
                            dve.wait_ge(s_rows, i * 32 + 32)
                            v_.scalar_tensor_tensor(out=big_a[:, :, :], in0=big_a[:, :, :], scalar=OFF,
                                                    in1=trow[:, :].unsqueeze(1).to_broadcast([P, G, P]),
                                                    op0=ALU.mult, op1=ALU.add).then_inc(s_mask, 1)
                            dve.wait_ge(s_lin, i + 1)
                            cw(v_.scalar_tensor_tensor(out=big_b[:, :, :], in0=big_b[:, :, :], scalar=SLOPE,
                                                       in1=big_b[:, :, :], op0=ALU.mult, op1=ALU.max))
                            v_.tensor_reduce(gmax[:, :], big_b.rearrange("p g n -> p n g"), X_AXIS, ALU.max
                                             ).then_inc(s_gmax, 1)
                            dve.wait_ge(s_gT, i + 1)
                            cw(v_.tensor_reduce(mloc[:, :], banks[0][:, 0:P], X_AXIS, ALU.max))
                            v_.tensor_tensor(mnew[:, :], mloc[:, :], tab[:, RW:TW], ALU.max).then_inc(s_mnew, 1)
                            dve.wait_ge(s_mnew, i + 1)
                            cw(v_.tensor_tensor(mloc[:, :], tab[:, RW:TW], mnew[:, :], ALU.subtract))
                            cw(v_.tensor_scalar(tab[:, RW:TW], mnew[:, :], 0.0, None, ALU.add))
                            dve.wait_ge(s_mrow, i + 1)
                            v_.tensor_tensor(big_b[:, :, :], big_b[:, :, :],
                                             banks[1][:, 0:P].unsqueeze(1).to_broadcast([P, G, P]), ALU.subtract
                                             ).then_inc(s_sub, 1)
                            cw(v_.tensor_scalar(dloc[:, :], dloc[:, :], -float(P), None, ALU.add))
                            dve.wait_ge(s_agg1, i + 1)
                            v_.scalar_tensor_tensor(out=tab[:, 0:RW], in0=tab[:, 0:RW], scalar=rescale[:, 0:1],
                                                    in1=banks[2][:, 0:RW], op0=ALU.mult, op1=ALU.add).then_inc(s_tabn, 1)
                        v_.tensor_scalar(idx[:, s, :], src_i[:, bass.ds(col + SL * G, G)], 0.0, None, ALU.add
                                         ).then_inc(s_zg_used, 1)
                        dve.sem_inc(s_zfree, 1)

            dve.wait_ge(s_fin, 16)
            rows = work[:, 0:NB * TW].rearrange("p (b c) -> p b c", c=TW)
            ch(v_.tensor_scalar(mean_sb[:, :], rows[:, :, ZW], 1e-30, None, ALU.max))
            ch(v_.reciprocal(rstd_sb[:, :], mean_sb[:, :]))
            for j in range(2):
                ch(v_.tensor_tensor(d_sb[:, :, :], wide(rows[:, :, ZW + 1 + j], D),
                                    r_sb[:, j, :].unsqueeze(1).to_broadcast([P, NB, D]), ALU.mult))
                ch(v_.tensor_tensor(rows[:, :, 0:D], rows[:, :, 0:D], d_sb[:, :, :], ALU.add))
            ch(v_.tensor_tensor(rows[:, :, 0:D], rows[:, :, 0:D], wide(rstd_sb[:, :], D), ALU.mult))
            v_.tensor_tensor(x_sb[:, :, :], x_sb[:, :, :], rows[:, :, 0:D], ALU.add).then_inc(s_res, 1)


_INS = ['x', 'src', 'dst', 'edge_attr_2', 'edge_attr_64', 'L0_gnn_W1', 'L0_gnn_b1', 'L0_gnn_W2', 'L0_gnn_b2',
        'L1_gnn_W_fc', 'L1_gnn_W_attn', 'L1_gnn_W_edge', 'L1_gnn_W_e2n', 'L1_gnn_W_m1', 'L1_gnn_W_m2']


def kernel(**inputs):
    import numpy as _np
    import concourse.bacc as _bacc
    from concourse import mybir as _mybir
    from concourse.bass_utils import run_bass_kernel_spmd as _run

    nc = _bacc.Bacc("TRN2", target_bir_lowering=False, num_devices=1)
    arrays, args = {}, []
    for name in _INS:
        a = _np.ascontiguousarray(inputs[name])
        arrays[f"in_{name}_dram"] = a
        args.append(nc.dram_tensor(f"in_{name}_dram", a.shape, _mybir.dt.from_np(a.dtype), kind="ExternalInput").ap())
    args.append(nc.dram_tensor("out_0_dram", (NODES, D), _mybir.dt.float32, kind="ExternalOutput").ap())
    gnn_kernel(nc, *args)
    r = _run(nc, [arrays], core_ids=[0])
    return r.results[0]["out_0_dram"]
```

```python
import concourse.bass as bass
from concourse import mybir
from contextlib import ExitStack

ALU = mybir.AluOpType
ACT = mybir.ActivationFunctionType
X_AXIS = mybir.AxisListType.X
F32 = mybir.dt.float32
BF16 = mybir.dt.bfloat16
I32 = mybir.dt.int32

P = 128
NODES, EDGES, D, HID = 12500, 200000, 64, 128
G = 8
ME = P * G
NM = -(-EDGES // ME)
LAST0 = EDGES - ME
DUP = (NM * ME - EDGES) // G
NT = NM * G
NB = -(-NODES // P)
NPAD = P * NB
NROWS = NPAD + P
FULL = NODES // NB
REST = NODES - FULL * NB
ZP = 2 * (D + 2)
AW = D + 1
ZW = D + 1
EW = D + 2
RW = D + 4
TW = ZW + 2
CH = 7
NC = NB // CH
CZ = 2 * CH
SL = 7
U = 2 * SL
W = 80
EPS = 1e-5
SLOPE = 0.01
OFF = -1e30
FLOOR = -1e20
assert NM % U == 0 and (NM * ME - EDGES) % G == 0 and NB % CH == 0 and 0 < REST < NB


class Chain:

    def __init__(self, eng, sem, base=0):
        self.eng, self.sem, self.base, self.k = eng, sem, base, 0

    def __call__(self, ins):
        self.k += 1
        ins.then_inc(self.sem, 1)
        self.eng.wait_ge(self.sem, self.base + self.k)


def gnn_kernel(nc, x, src, dst, e2, e64, W1, b1, W2, b2, W_fc, W_attn, W_edge, W_e2n, W_m1, W_m2, out):
    with ExitStack() as ctx:
        def sb(name, shape, dt=F32):
            return ctx.enter_context(nc.sbuf_tensor(name, shape, dt))

        def pb(name, shape, dt=F32):
            return ctx.enter_context(nc.psum_tensor(name, shape, dt))

        def sem(name):
            return ctx.enter_context(nc.semaphore(name))

        acc_dram = [nc.dram_tensor(f"acc_dram{k}", (NROWS, AW), F32, kind="Internal").ap() for k in range(G)]
        z_dram = nc.dram_tensor("z_dram", (NPAD, ZW), F32, kind="Internal").ap()
        t_dram = nc.dram_tensor("t_dram", (1, NROWS), F32, kind="Internal").ap()
        tab_dram = nc.dram_tensor("tab_dram", (NROWS, TW), F32, kind="Internal").ap()

        ident = sb("ident", [P, P])
        iota_f = sb("iota_f", [P, P])
        ones_f = sb("ones_f", [P, P])
        zero_row = sb("zero_row", [P, AW])
        zeros_b = sb("zeros_b", [P, P], BF16)
        bits = sb("bits", [P, 2], I32)
        dummy_row = sb("dummy_row", [P, 1])
        w1_sb = sb("w1_sb", [P, HID])
        b1_sb = sb("b1_sb", [P, 1])
        w2_sb = sb("w2_sb", [P, D])
        b2_sb = sb("b2_sb", [P, D])
        wfc_sb = sb("wfc_sb", [D, D])
        blk_sb = sb("blk_sb", [D, 6])
        we_sb = sb("we_sb", [2, 1])
        wedge_sb = sb("wedge_sb", [2, 2])
        we2nT_sb = sb("we2nT_sb", [2, D])
        wm_sb = sb("wm_sb", [D, 2, D])
        wz2_sb = sb("wz2_sb", [P, 2 * (D + 2)])
        q_sb = sb("q_sb", [P, 2])
        r_sb = sb("r_sb", [P, 2, D])
        v_sb = sb("v_sb", [P, 4, D])
        src_i = sb("src_i", [P, NT + SL * G], I32)
        dst_f = sb("dst_f", [P, NT])
        zg = sb("zg", [P, SL, G, RW])
        zg_flat = zg.rearrange("p s g c -> p (s g c)")
        n_bf = (NT + G) // 2
        dst_i = zg_flat[:, 0:NT].bitcast(I32)
        dst_p = zg_flat[:, NT:NT + n_bf].bitcast(BF16)
        dst_j = zg_flat[:, NT + n_bf:NT + 2 * n_bf].bitcast(BF16)
        e2_sb = sb("e2_sb", [P, NT, 2])
        ee_sb = sb("ee_sb", [P, NT])
        x_sb = sb("x_sb", [P, NB, D])
        d_sb = sb("d_sb", [P, NB, D])
        z_sb = sb("z_sb", [P, NB, D + 2])
        work = sb("work", [P, max((NB + 1) * TW, 2 * G * CH * AW)])
        cnt_sb = sb("cnt_sb", [P, 2, NB])
        mean_sb = sb("mean_sb", [P, NB])
        var_sb = sb("var_sb", [P, NB])
        rstd_sb = sb("rstd_sb", [P, NB])
        t_sb = sb("t_sb", [P, NB])
        src_rest = z_sb.rearrange("p b d -> p (b d)")[:, 0:NT].bitcast(I32)
        ea_sb = sb("ea_sb", [P, 2, G, EW])
        threshold = sb("threshold", [P, 1])
        srcf = sb("srcf", [P, 2, G])
        src_hi = sb("src_hi", [P, 2, G], BF16)
        src_lo = sb("src_lo", [P, 2, G], BF16)
        srchi_all = sb("srchi_all", [P, NT + G], BF16)
        srclo_all = sb("srclo_all", [P, NT + G], BF16)
        ident_b = sb("ident_b", [P, P], BF16)
        ohp = sb("ohp", [P, 2, 4, P], BF16)
        ohj = sb("ohj", [P, 2, 4, NB], BF16)
        same = sb("same", [P, 2, 4, P])
        todummy = sb("todummy", [P, 2, G])
        idx = sb("idx", [P, SL, G], I32)
        y_sb = sb("y_sb", [P, 2, G * EW])
        s_sb = sb("s_sb", [P, G])
        dloc = sb("dloc", [P, G])
        big_a = sb("big_a", [P, G, P])
        big_b = sb("big_b", [P, G, P])
        gmax = sb("gmax", [P, P])
        trow = sb("trow", [P, P])
        tab = sb("tab", [P, TW])
        mloc = sb("mloc", [P, 1])
        mnew = sb("mnew", [P, 1])
        rescale = sb("rescale", [P, 1])
        lo_all = sb("lo_all", [P, NM])
        hi_all = sb("hi_all", [P, NM])
        cum_f = sb("cum_f", [P, NM + 1])
        cum_i = sb("cum_i", [P, NM + 1], I32)
        base_i = sb("base_i", [P, NM], I32)
        tmp_m = sb("tmp_m", [P, NM])
        tmp_i = sb("tmp_i", [P, NM], I32)
        tmp_m2 = sb("tmp_m2", [P, NM])
        sums = sb("sums", [P, 2, D])
        mom = sb("mom", [P, 4, D])
        mabs = sb("mabs", [P, 4, D])
        msign = sb("msign", [P, 4, D])
        c_sb = sb("c_sb", [P, 1])
        cats = [y_sb.rearrange("p s w -> p (s w)")[:, 0:CH * P],
                same.rearrange("p h j e -> p (h j e)")[:, 0:CH * P]]
        catTs = [b.rearrange("p g n -> p (g n)")[:, 0:CH * P] for b in (big_a, big_b)]
        hids = [ea_sb.rearrange("p s g c -> p (s g c)")[:, 0:CH * P], 
                z_sb.rearrange("p b d -> p (b d)")[:, 0:CH * P]]
        h2s, h2Ts = [catTs[1], cats[0]], [catTs[0], cats[1]]
        sq_buf = ohp.rearrange("p h j e -> p (h j e)").bitcast(F32)[:, 0:CH * D].rearrange("p (b d) -> p b d", b=CH)
        n_half = NB // 2
        pows = [buf[:, 0:NB * D].rearrange("p (b k d) -> p b k d", k=2, d=D)
                for buf in (d_sb.rearrange("p b d -> p (b d)"), work)]

        def chunk(c):
            return slice(c * CH, (c + 1) * CH) if isinstance(c, int) else bass.ds(c * CH, CH)

        far_f = sb("far_f", [P, 1])
        far_i = sb("far_i", [P, 1], I32)
        def f_big(k):
            return work[:, k * 2 * G * W:(k + 1) * 2 * G * W].rearrange("p (s g n) -> p s g n", s=2, g=G)

        f_masks, f_scores, f_probs = f_big(0), f_big(1), f_big(2)
        f_s = sb("f_s", [P, 2, G])
        f_dloc = sb("f_dloc", [P, G])
        f_t = sb("f_t", [P, 2, W])
        f_top = sb("f_top", [P, W])
        f_max = sb("f_max", [P, SL])
        f_new = sb("f_new", [P, 1])
        f_ratio = sb("f_ratio", [P, 2])
        f_fact = sb("f_fact", [P, 2])
        f_e = sb("f_e", [P, 2])
        f_v = sb("f_v", [P, TW - 1])

        banks = [pb(f"bank{i}", [P, 512]) for i in range(8)]

        s_const = sem("s_const")
        s_work = sem("s_work")
        s_tab = [sem(f"s_tab{k}") for k in range(G)]
        s_zero = [sem(f"s_zero{k}") for k in range(G)]
        s_room = sem("s_room")
        s_w = sem("s_w")
        s_src = sem("s_src")
        s_dst = sem("s_dst")
        s_e2 = sem("s_e2")
        s_rowf = sem("s_rowf")
        s_turn = sem("s_turn")
        s_turned = sem("s_turned")
        s_x = sem("s_x")
        s_ea = [sem(f"s_ea{k}") for k in range(2)]
        s_pad = sem("s_pad")
        s_stage = sem("s_stage")
        s_srcb = sem("s_srcb")
        s_oh = sem("s_oh")
        s_oh_used = sem("s_oh_used")
        s_same = sem("s_same")
        s_y = sem("s_y")
        s_ysb = sem("s_ysb")
        s_idx = sem("s_idx")
        s_held = [sem(f"s_held{k}") for k in range(4)]
        s_pool = sem("s_pool")
        s_dve = sem("s_dve")
        s_dve1 = sem("s_dve1")
        s_dve3 = sem("s_dve3")
        s_dve4 = sem("s_dve4")
        s_dve5 = sem("s_dve5")
        s_act = sem("s_act")
        s_prep = sem("s_prep")
        s_prep_sb = sem("s_prep_sb")
        s_cnt = sem("s_cnt")
        s_dsub = sem("s_dsub")
        s_sq = sem("s_sq")
        s_std = sem("s_std")
        s_vv = sem("s_vv")
        s_rstd = sem("s_rstd")
        s_acc = [sem(f"s_acc{k}") for k in range(2)]
        s_cat = sem("s_cat")
        s_agg = sem("s_agg")
        s_tr = sem("s_tr")
        s_trs = sem("s_trs")
        s_hid = sem("s_hid")
        s_hids = sem("s_hids")
        s_o = sem("s_o")
        s_x1 = sem("s_x1")
        s_zp = sem("s_zp")
        s_z = sem("s_z")
        s_zst = sem("s_zst")
        s_part = sem("s_part")
        s_psum = sem("s_psum")
        s_mom = sem("s_mom")
        s_root = sem("s_root")
        s_t = sem("s_t")
        s_tst = sem("s_tst")
        s_tabi = sem("s_tabi")
        s_neg = sem("s_neg")
        s_range = sem("s_range")
        s_win = sem("s_win")
        s_bits = sem("s_bits")
        s_csum = sem("s_csum")
        s_cw3 = sem("s_cw3")
        s_csq = sem("s_csq")
        s_cd = sem("s_cd")
        s_h2 = sem("s_h2")
        s_trs2 = sem("s_trs2")
        s_tr2 = sem("s_tr2")
        s_sq2 = sem("s_sq2")
        s_var = sem("s_var")
        s_d2 = sem("s_d2")
        s_cath = sem("s_cath")
        s_h = sem("s_h")
        s_pos = sem("s_pos")
        s_zg = [sem(f"s_zg{k}") for k in range(SL)]
        s_zg_used = sem("s_zg_used")
        s_rows = sem("s_rows")
        s_mask = sem("s_mask")
        s_lin = sem("s_lin")
        s_gmax = sem("s_gmax")
        s_gT = sem("s_gT")
        s_mnew = sem("s_mnew")
        s_mrow = sem("s_mrow")
        s_sub = sem("s_sub")
        s_exp = sem("s_exp")
        s_agg1 = sem("s_agg1")
        s_tabn = sem("s_tabn")
        s_tabs = sem("s_tabs")
        s_fin = [sem(f"s_fin{c}") for c in range(NB // CZ)]
        s_zfree = sem("s_zfree")
        f_trow = [sem(f"f_trow{k}") for k in range(2)]
        f_mask = sem("f_mask")
        f_lin = sem("f_lin")
        f_gmax = sem("f_gmax")
        f_gT = sem("f_gT")
        f_mloc = sem("f_mloc")
        f_mrow = sem("f_mrow")
        f_sub = sem("f_sub")
        f_exp = sem("f_exp")
        f_rows = sem("f_rows")
        f_diff = sem("f_diff")
        f_resc = sem("f_resc")
        f_tabn = sem("f_tabn")
        f_tabs = sem("f_tabs")
        f_link = [sem(f"f_link{k}") for k in range(5)]
        s_res = sem("s_res")
        s_out = sem("s_out")

        q_at = D + 2
        r_at = q_at + 2
        v_at = r_at + 2 * D
        NEDGE_MAIN = (NM - 1) * ME
        NPARTS = 4
        zero_w = (NB + 1) * AW // 3
        floor_w = (NB + 1) * TW // 3
        n_stores = NB // CZ + -(-REST // CZ)

        MH = NM // 2
        row_buf = z_sb.rearrange("p b d -> p (b d)")[:, NT:NT + 4 * ME].rearrange("p (k h e) -> p k h e", k=2, h=2
                                                                                ).bitcast(I32)
        row_f = d_sb.rearrange("p b d -> p (b d)")[:, 0:4 * ME].rearrange("p (k h e) -> p k h e", k=2, h=2)

        def load_rows(eng, values, k, s):
            eng.dma_start(row_buf[0:MH, k, 0, :], values[0:MH * ME].rearrange("(m e) -> m e", e=ME)).then_inc(s, 16)
            eng.dma_start(row_buf[0:MH - 1, k, 1, :], values[MH * ME:NEDGE_MAIN].rearrange("(m e) -> m e", e=ME)
                          ).then_inc(s, 16)
            eng.dma_start(row_buf[MH - 1:MH, k, 1, :], values[LAST0:EDGES].rearrange("(a e) -> a e", a=1)
                          ).then_inc(s, 16)

        block = ctx.enter_context(nc.Block())

        @block.sync
        def _(sp):
            load_rows(sp, src, 0, s_src)

            def load_ea(s, m):
                rows = e64[bass.ds(m * ME, ME), :] if not isinstance(m, int) else e64[m * ME:(m + 1) * ME, :]
                sp.dma_start(ea_sb[:, s, :, 0:D], rows.rearrange("(p g) c -> p g c", g=G)).then_inc(s_ea[s], 16)

            def load_e2(it):
                sp.dma_start(e2_sb[:, bass.ds(it * (2 * G), 2 * G), :].rearrange("p (m g) c -> p m (g c)", g=G),
                             e2[bass.ds(it * (2 * ME), 2 * ME), :].rearrange("(m p g) c -> p m (g c)", p=P, g=G)
                             ).then_inc(s_e2, 16)

            load_ea(0, 0)
            load_ea(1, 1)
            sp.wait_ge(s_work, 2)
            sp.dma_start(x_sb[0:FULL, :, :], x[0:FULL * NB, :].rearrange("(p b) w -> p b w", p=FULL)).then_inc(s_x, 16)
            sp.dma_start(x_sb[FULL:FULL + 1, 0:REST, :], x[FULL * NB:NODES, :].rearrange("(p b) w -> p b w", p=1)
                         ).then_inc(s_x, 16)
            for k in range(G):
                view = acc_dram[k].rearrange("(p r) c -> p (r c)", p=P)
                for h in range(3):
                    sp.dma_start(view[:, h * zero_w:(h + 1) * zero_w], work[:, 0:zero_w]).then_inc(s_zero[k], 16)
            with sp.Fori(1, NM // 2 - 1) as it:
                for s in range(2):
                    sp.wait_ge(s_y, it * 4 + 2 * s)
                    load_ea(s, it * 2 + s)
                load_e2(it - 1)
            load_e2(NM // 2 - 2)
            for m, e0 in ((NM - 2, (NM - 2) * ME), (NM - 1, LAST0)):
                sp.dma_start(e2_sb[:, m * G:(m + 1) * G, :], e2[e0:e0 + ME, :].rearrange("(p g) c -> p g c", g=G)
                             ).then_inc(s_e2, 16)
            sp.wait_ge(s_y, 2 * (NM - 2))
            load_ea(0, NM - 2)
            sp.wait_ge(s_y, 2 * (NM - 1))
            sp.dma_start(ea_sb[0:DUP, 1, :, 0:AW], zero_row[0:DUP, :].unsqueeze(1).to_broadcast([DUP, G, AW])
                         ).then_inc(s_pad, 16)
            sp.wait_ge(s_pad, 16)
            sp.dma_start(ea_sb[DUP:P, 1, :, 0:D],
                         e64[LAST0 + DUP * G:EDGES, :].rearrange("(p g) c -> p g c", g=G)).then_inc(s_ea[1], 16)

            for k in range(G):
                sp.wait_ge(s_tab[k], 16 * NM)
            sp.wait_ge(s_tst, 48)
            with sp.Fori(0, NC // 2) as it:
                for s in range(2):
                    sp.wait_ge(s_agg, it * 2 + s + 1)
                    for k in range(G):
                        view = acc_dram[k][0:NPAD, :].rearrange("(p b) c -> p b c", p=P)
                        sp.dma_start(
                            work[:, s * G * CH * AW:(s + 1) * G * CH * AW].rearrange(
                                "p (k b c) -> p k b c", k=G, b=CH)[:, k, :, :],
                            view[:, bass.ds((it * 2 + s) * CH, CH), :]).then_inc(s_acc[s], 16)
            for c in range(NB // CZ):
                sp.wait_ge(s_z, c + 1)
                sp.dma_start(z_dram.rearrange("(p b) c -> p b c", p=P)[:, c * CZ:(c + 1) * CZ, :],
                             z_sb[:, c * CZ:(c + 1) * CZ, 0:ZW]).then_inc(s_zst, 16)
            sp.wait_ge(s_t, 1)
            sp.dma_start(t_dram[0:1, 0:NPAD].rearrange("a (p b) -> (a p) b", p=P), t_sb[:, :]).then_inc(s_tst, 16)
            sp.dma_start(t_dram[0:1, NPAD:NROWS].rearrange("a (p b) -> (a p) b", p=P), t_sb[:, 0:1]).then_inc(s_tst, 16)
            sp.wait_ge(s_tst, 80)
            sp.wait_ge(s_win, 1)
            far = sp.snap(sp.value_load(far_i[0:1, 0:1], min_val=0, max_val=1))

            def row_of(m):
                at = slice(m, m + 1) if isinstance(m, int) else bass.ds(m, 1)
                return sp.snap(sp.value_load(base_i[0:1, at], min_val=0, max_val=NODES - 1))

            def load_t(it, q):
                m = it * U + q
                if isinstance(m, int) and m < 2:
                    pass
                else:
                    sp.wait_ge(f_mask, m - 1)
                sp.dma_start(f_t[:, q % 2, :], t_dram[0:1, bass.ds(row_of(m), W)].to_broadcast([P, W])
                             ).then_inc(f_trow[q % 2], 16)

            def update_rows(it, q):
                m = it * U + q
                row = row_of(m)
                sp.dma_start(tab[0:W, :], tab_dram[bass.ds(row, W), :]).then_inc(f_rows, 16)
                sp.wait_ge(f_tabn, m + 1)
                sp.dma_start(tab_dram[bass.ds(row, W), :], tab[0:W, :]).then_inc(f_tabs, 16)
                sp.wait_ge(f_tabs, m * 16 + 16)
                sp.sem_inc(s_held[1], 1)

            with sp.If(far == 0):
                for q in range(U):
                    load_t(0, q)
                    if q >= 3:
                        update_rows(0, q - 3)
                with sp.Fori(1, NM // U) as it:
                    for q in range(U):
                        load_t(it, q)
                        update_rows(it, q - 3)
                for q in range(3):
                    update_rows(NM // U, q - 3)
            with sp.If(far == 1):
                with sp.Fori(0, NM) as m:
                    c0 = sp.snap(sp.value_load(cum_i[0:1, bass.ds(m, 1)], min_val=0, max_val=NM * NB))
                    c1 = sp.snap(sp.value_load(cum_i[0:1, bass.ds(m + 1, 1)], min_val=1, max_val=NM * NB))
                    first = sp.snap(sp.value_load(base_i[0:1, bass.ds(m, 1)], min_val=0, max_val=NODES - 1))
                    with sp.Fori(c0, c1) as i:
                        row = sp.snap(nc.s_assert_within(
                            first + (i - c0) * P, 0, NROWS - P,
                            skip_runtime_bounds_check_because="a window starts at or below the last destination"))
                        sp.dma_start(tab[:, :], tab_dram[bass.ds(row, P), :]).then_inc(s_rows, 16)
                        sp.dma_start(trow[:, :], t_dram[0:1, bass.ds(row, P)].to_broadcast([P, P])
                                     ).then_inc(s_rows, 16)
                        sp.wait_ge(s_tabn, i + 1)
                        sp.dma_start(tab_dram[bass.ds(row, P), :], tab[:, :]).then_inc(s_tabs, 16)
                        sp.wait_ge(s_tabs, i * 16 + 16)
                        sp.sem_inc(s_held[1], 1)
            for c in range(NB // CZ):
                w = CZ * TW
                sp.dma_start(work[:, c * w:(c + 1) * w], tab_dram[0:NPAD, :].rearrange("(p b) c -> p (b c)", p=P)[
                    :, c * w:(c + 1) * w]).then_inc(s_fin[c], 16)
            sp.wait_ge(s_out, 16 * n_stores)

        @block.gpsimd
        def _(pool):
            g_ = nc.gpsimd
            chain = Chain(pool, s_pool)
            chain(g_.memset(work[:, zero_w:zero_w + floor_w], 0.0))
            g_.memset(work[:, zero_w:zero_w + floor_w].rearrange("p (r c) -> p r c", c=TW)[:, :, TW - 1:TW], FLOOR
                      ).then_inc(s_tabi, 1)
            chain(g_.memset(zero_row[:, :], 0.0))
            chain(g_.memset(ones_f[:, :], 1.0))
            chain(g_.memset(ident[:, :], 0.0))
            chain(g_.affine_select(out=ident[:, :], in_=ident[:, :], compare_op=ALU.not_equal, fill=1.0, base=0,
                                   pattern=[[-1, P]], channel_multiplier=1))
            chain(g_.iota(src_iota := idx[:, 0, 0:1], pattern=[[0, 1]], base=NPAD, channel_multiplier=1))
            chain(g_.tensor_copy(dummy_row[:, :], src_iota))
            chain(g_.iota(cum_i[:, 0:P], pattern=[[1, P]], base=0, channel_multiplier=0))
            chain(g_.tensor_copy(iota_f[:, :], cum_i[:, 0:P]))
            chain(g_.tensor_copy(ident_b[:, :], ident[:, :]))
            chain(g_.iota(bits[:, 0:1], pattern=[[0, 1]], base=190, channel_multiplier=-1))
            g_.iota(bits[:, 1:2], pattern=[[0, 1]], base=191, channel_multiplier=-1).then_inc(s_bits, 1)
            chain(g_.memset(zeros_b[:, :], 0.0))
            for s in range(2):
                chain(g_.memset(ea_sb[:, s, :, D:AW], 1.0))
            g_.sem_inc(s_const, 1)
            def scatter_half(s, h, n, before):
                pool.wait_ge(s_ysb, n + 3)
                pool.wait_ge(s_idx, n + 2)
                for g in range(4 * h, 4 * h + 4):
                    if before is None:
                        pool.wait_ge(s_zero[g], 48)
                    else:
                        pool.wait_ge(s_tab[g], before)
                g_.sem_inc(s_room, 1)
                for g in range(4 * h, 4 * h + 4):
                    g_.indirect_dma_start(
                        out=acc_dram[g][:, :],
                        out_offset=bass.IndirectOffsetOnAxis(ap=idx[:, s, g:g + 1], axis=0),
                        in_=y_sb[:, s, g * EW:g * EW + AW], in_offset=None,
                        compute_op=ALU.add).then_inc(s_tab[g], 16)

            for n in range(4):
                scatter_half(n // 2, n % 2, n, 16 if n >= 2 else None)
            with pool.Fori(1, NM // 2) as it:
                for s in range(2):
                    for h in range(2):
                        scatter_half(s, h, it * 4 + (2 * s + h), it * 32 + 16 * s)
            pool.wait_ge(s_neg, 1)
            g_.partition_all_reduce(lo_all[:, :], lo_all[:, :], P, bass.bass_isa.ReduceOp.max).then_inc(s_range, 1)
            g_.partition_all_reduce(hi_all[:, :], hi_all[:, :], P, bass.bass_isa.ReduceOp.max).then_inc(s_range, 1)
            for s in range(SL):
                chain(g_.memset(zg[:, s, :, ZW:ZW + 1], 1.0))
            pool.wait_ge(s_zst, 16 * (NB // CZ))
            with pool.Fori(0, NM // SL) as it:
                for s in range(SL):
                    pool.wait_ge(s_zg_used, it * SL + s + 1)
                    pool.wait_ge(s_zfree, it * SL + s + 1)
                    g_.sem_inc(s_held[0], 1)
                    for g in range(G):
                        g_.indirect_dma_start(
                            out=zg[:, s, g, 0:ZW], out_offset=None, in_=z_dram[:, :],
                            in_offset=bass.IndirectOffsetOnAxis(ap=idx[:, s, g:g + 1], axis=0)).then_inc(s_zg[s], 16)

        @block.scalar
        def _(act):
            a_ = nc.scalar
            load_rows(act, dst, 1, s_dst)
            with nc.allow_non_contiguous_dma(reason="small transposed weights"):
                act.dma_start(blk_sb[:, :], W_attn[0:1, 0:6 * D].rearrange("a (k d) -> d (a k)", k=6)).then_inc(s_w, 16)
                act.dma_start(we_sb[:, :], W_attn.rearrange("a n -> n a")[6 * D:6 * D + 2, :]).then_inc(s_w, 16)
                act.dma_start(we2nT_sb[:, :], W_e2n.rearrange("f i -> i f")).then_inc(s_w, 16)
                act.dma_start(b1_sb[:, :], b1.rearrange("(p a) -> p a", a=1)).then_inc(s_w, 16)
            act.dma_start(w1_sb[:, :], W1).then_inc(s_w, 16)
            act.dma_start(w2_sb[:, :], W2).then_inc(s_w, 16)
            act.dma_start(b2_sb[:, :], b2.rearrange("(a d) -> a d", a=1).to_broadcast([P, D])).then_inc(s_w, 16)
            act.dma_start(wfc_sb[:, :], W_fc).then_inc(s_w, 16)
            act.dma_start(wedge_sb[:, :], W_edge).then_inc(s_w, 16)
            act.dma_start(wm_sb[:, 0, :], W_m1).then_inc(s_w, 16)
            act.dma_start(wm_sb[:, 1, :], W_m2).then_inc(s_w, 16)
            act.wait_ge(s_dsub, 1)
            a_.activation(z_sb[:, :, 0:D], d_sb[:, :, :], ACT.Square).then_inc(s_sq, 1)
            act.wait_ge(s_vv, 1)
            a_.activation(var_sb[:, :], var_sb[:, :], ACT.Sqrt).then_inc(s_std, 1)
            act.wait_ge(s_zero[G - 1], 48)
            act.wait_ge(s_tabi, 1)
            view = tab_dram.rearrange("(p r) c -> p (r c)", p=P)
            for h in range(3):
                act.dma_start(view[:, h * floor_w:(h + 1) * floor_w], work[:, zero_w:zero_w + floor_w]
                              ).then_inc(s_tst, 16)
            with act.Fori(0, NM // 2) as it:
                for s in range(2):
                    for h in range(2):
                        act.wait_ge(s_y, it * 4 + 2 * s + h + 3)
                        act.wait_ge(s_room, it * 4 + 2 * s + h + 1)
                        a_.activation(y_sb[:, s, 4 * h * EW:4 * (h + 1) * EW], banks[4 + h][:, 0:4 * EW],
                                      ACT.Copy).then_inc(s_ysb, 1)
            act.wait_ge(s_cnt, 1)
            act.wait_ge(s_h, 1)

            def copy_h(c, p):
                a_.activation(cats[p].rearrange("p (b f) -> p b f", b=CH)[:, :, 0:D], d_sb[:, chunk(c), :], ACT.Copy
                              ).then_inc(s_cath, 1)

            def copy_transposes(c, p):
                act.wait_ge(s_tr, c + 1)
                a_.activation(catTs[p][:, 0:512], banks[0][:, 0:512], ACT.Copy)
                a_.activation(catTs[p][:, 512:CH * P], banks[1][:, 0:CH * P - 512], ACT.Copy).then_inc(s_trs, 1)

            def hidden(c, p):
                act.wait_ge(s_hid, c + 1)
                a_.activation(hids[p][:, 0:512], banks[2][:, 0:512], ACT.Relu, bias=b1_sb[:, 0:1])
                a_.activation(hids[p][:, 512:CH * P], banks[3][:, 0:CH * P - 512], ACT.Relu, bias=b1_sb[:, 0:1]
                              ).then_inc(s_hids, 1)

            def squares(c):
                act.wait_ge(s_d2, c + 1)
                act.wait_ge(s_var, c + 1)
                a_.activation(sq_buf[:, :, :], d_sb[:, chunk(c), :], ACT.Square).then_inc(s_sq2, 1)

            copy_h(0, 0)
            copy_h(1, 1)
            copy_transposes(0, 0)
            hidden(0, 0)
            copy_transposes(1, 1)
            copy_h(2, 0)
            with act.Fori(0, NC // 2 - 2) as it:
                for k in (1, 2):
                    c = it * 2 + k
                    hidden(c, k % 2)
                    copy_transposes(c + 1, (k + 1) % 2)
                    copy_h(c + 2, k % 2)
                    squares(c - 1)
            for c in range(NC - 3, NC):
                hidden(c, c % 2)
                if c + 1 < NC:
                    copy_transposes(c + 1, (c + 1) % 2)
                if c + 2 < NC:
                    copy_h(c + 2, c % 2)
                squares(c - 1)
            squares(NC - 1)
            act.wait_ge(s_vv, 2)
            a_.activation(var_sb[:, :], var_sb[:, :], ACT.Sqrt).then_inc(s_std, 1)
            for c in range(NB // CZ):
                act.wait_ge(s_tr2, c + 1)
                if c >= 2:
                    act.wait_ge(s_zp, c)
                a_.activation(h2Ts[c % 2][:, 0:512], banks[0][:, 0:512], ACT.Copy)
                a_.activation(h2Ts[c % 2][:, 512:CH * P], banks[1][:, 0:CH * P - 512], ACT.Copy).then_inc(s_trs2, 1)
            for u in range(4):
                act.wait_ge(s_cd, u + 1)
                a_.activation(pows[u % 2][:, :, 0, :], pows[u % 2][:, :, 1, :], ACT.Square).then_inc(s_csq, 1)
            act.wait_ge(s_mom, 1)
            ch = Chain(act, s_act)
            ch(a_.activation(mabs[:, :, :], mabs[:, :, :], ACT.Ln))
            ch(a_.activation(mabs[:, 0:2, :], mabs[:, 0:2, :], ACT.Exp, scale=0.5))
            a_.activation(mabs[:, 2:4, :], mabs[:, 2:4, :], ACT.Exp, scale=1.0 / 3.0).then_inc(s_root, 1)
            act.wait_ge(s_win, 1)
            far = act.snap(act.value_load(far_i[0:1, 0:1], min_val=0, max_val=1))

            def add_s(it, q):
                m = it * U + q
                act.wait_ge(f_mask, m + 1)
                if not (isinstance(m, int) and m < 2):
                    act.wait_ge(f_exp, m - 1)
                for g in range(G):
                    ins = a_.activation(f_scores[:, q % 2, g, :], f_masks[:, q % 2, g, :], ACT.Identity,
                                        bias=f_s[:, q % 2, g:g + 1])
                ins.then_inc(f_lin, 1)

            def factors(it, q):
                act.wait_ge(f_diff, it * U + q + 1)
                a_.activation(f_fact[0:W, :], f_ratio[0:W, :], ACT.Exp).then_inc(f_resc, 1)

            def exps(it, q):
                act.wait_ge(f_sub, it * U + q + 1)
                a_.activation(f_probs[:, q % 2, :, :], f_scores[:, q % 2, :, :], ACT.Exp).then_inc(f_exp, 1)

            def act_step(it, q, first=False):
                add_s(it, q)
                if not first or q >= 2:
                    factors(it, q - 2)
                if not first or q >= 1:
                    exps(it, q - 1)

            with act.If(far == 0):
                for q in range(U):
                    act_step(0, q, first=True)
                with act.Fori(1, NM // U) as it:
                    for q in range(U):
                        act_step(it, q)
                factors(NM // U, -2)
                exps(NM // U, -1)
                factors(NM // U, -1)
            with act.If(far == 1):
                with act.Fori(0, NM) as m:
                    c0 = act.snap(act.value_load(cum_i[0:1, bass.ds(m, 1)], min_val=0, max_val=NM * NB))
                    c1 = act.snap(act.value_load(cum_i[0:1, bass.ds(m + 1, 1)], min_val=1, max_val=NM * NB))
                    with act.Fori(c0, c1) as i:
                        act.wait_ge(s_mask, i + 1)
                        for g in range(G):
                            ins = a_.activation(big_b[:, g, :], big_a[:, g, :], ACT.Identity, bias=s_sb[:, g:g + 1])
                        ins.then_inc(s_lin, 1)
                        act.wait_ge(s_sub, i + 1)
                        a_.activation(rescale[:, :], mloc[:, :], ACT.Exp)
                        a_.activation(big_a[:, :, :], big_b[:, :, :], ACT.Exp).then_inc(s_exp, 1)

            for c in range(NB // CZ):
                b0, b1_ = c * CZ, (c + 1) * CZ
                act.wait_ge(s_res, c + 1)
                act.dma_start(out[0:FULL * NB, :].rearrange("(p b) w -> p b w", p=FULL)[:, b0:b1_, :],
                              x_sb[0:FULL, b0:b1_, :]).then_inc(s_out, 16)
                if b0 < REST:
                    b1_ = min(b1_, REST)
                    act.dma_start(out[FULL * NB + b0:FULL * NB + b1_, :].rearrange("(p b) w -> p b w", p=1),
                                  x_sb[FULL:FULL + 1, b0:b1_, :]).then_inc(s_out, 16)

        @block.tensor
        def _(pe):
            t_ = nc.tensor
            pe.wait_ge(s_const, 1)
            for k in range(2):
                pe.wait_ge(s_rowf, k + 1)
                if k == 1:
                    pe.wait_ge(s_turned, 1)
                for h in range(2):
                    for g in range(G):
                        ins = t_.transpose(
                            banks[h * 2 + g // 4][:, g % 4 * MH:(g % 4 + 1) * MH],
                            row_f[0:MH, k, h, :].rearrange("m (p g) -> m g p", g=G)[:, g, :], ident[0:MH, 0:MH])
                ins.then_inc(s_turn, 1)
            pe.wait_ge(s_w, 16 * 11)
            t_.transpose(banks[7][0:D, 0:D], wfc_sb[:, :], ident[0:D, 0:D])
            t_.matmul(banks[7][0:D, D:D + 1], wfc_sb[:, :], blk_sb[:, 0:1], start=True, stop=True)
            t_.matmul(banks[7][0:D, D + 1:D + 2], wfc_sb[:, :], blk_sb[:, 3:4], start=True, stop=True)
            t_.matmul(banks[7][:, q_at:q_at + 2], we_sb[:, 0:1].to_broadcast([2, P]), wedge_sb[:, :], start=True, stop=True)
            for j in range(2):
                t_.matmul(banks[7][:, r_at + j * D:r_at + (j + 1) * D], wedge_sb[:, j:j + 1].to_broadcast([2, P]), we2nT_sb[:, :],
                          start=True, stop=True)
            for k, b in enumerate((1, 4, 2, 5)):
                ins = t_.matmul(banks[7][:, v_at + k * D:v_at + (k + 1) * D], blk_sb[:, b:b + 1].to_broadcast([D, P]),
                                wm_sb[:, k // 2, :], start=True, stop=True)
            ins.then_inc(s_prep, 1)
            t_.matmul(banks[6][:, 0:NB], zeros_b[:, :], zeros_b[:, 0:NB], start=True, stop=False)
            pe.wait_ge(s_pos, 2)
            pe.wait_ge(s_turned, 2)
            def spread_sources(bank, s, h, n, m):
                pe.wait_ge(s_stage, m + 1)
                pe.wait_ge(s_same, n + 1)
                for j in range(4):
                    for part, half in enumerate((src_hi, src_lo)):
                        ins = t_.matmul(banks[bank][:, j * P:(j + 1) * P],
                                        half[:, s, 4 * h + j:4 * h + j + 1].to_broadcast([P, P]), ident_b[:, :],
                                        start=(part == 0), stop=(part == 1))
                ins.then_inc(s_srcb, 1)

            spread_sources(0, 0, 0, 0, 0)
            with pe.Fori(0, NM // 2) as it:
                for q in range(4):
                    s, h = divmod(q, 2)
                    n = it * 4 + q
                    r = (q + 1) % 4
                    spread_sources(r, r // 2, r % 2, n + 1, it * 2 + (q + 1) // 2)
                    pe.wait_ge(s_oh, n + 1)
                    for j in range(4):
                        ins = t_.matmul(banks[6][:, 0:NB], ohp[:, h, j, :], ohj[:, h, j, :], start=False, stop=False)
                    ins.then_inc(s_oh_used, 1)
                    pe.wait_ge(s_same, n + 5)
                    if h == 0:
                        pe.wait_ge(s_ea[s], it * 16 + 16)
                    pe.wait_ge(s_ysb, n + 1)
                    for j in range(4):
                        ins = t_.matmul(banks[4 + h][:, j * EW:(j + 1) * EW], same[:, h, j, :],
                                        ea_sb[:, s, 4 * h + j, :], start=True, stop=True)
                    ins.then_inc(s_y, 1)
            t_.matmul(banks[6][:, 0:NB], zeros_b[:, :], zeros_b[:, 0:NB], start=False, stop=True).then_inc(s_cnt, 1)
            def transposes(c, p):
                pe.wait_ge(s_cath, c + 1)
                pe.wait_ge(s_cat, c + 1)
                pe.wait_ge(s_trs, c + 1)
                for b in range(CH):
                    ins = t_.transpose(banks[b // 4][:, (b % 4) * P:(b % 4 + 1) * P], cats[p][:, b * P:(b + 1) * P],
                                       ident[:, :])
                ins.then_inc(s_tr, 1)

            def layer1(c, p):
                pe.wait_ge(s_trs, c + 2)
                pe.wait_ge(s_hids, c + 1)
                t_.matmul(banks[2][:, 0:512], w1_sb[:, :], catTs[p][:, 0:512], start=True, stop=True)
                t_.matmul(banks[3][:, 0:CH * P - 512], w1_sb[:, :], catTs[p][:, 512:CH * P], start=True, stop=True
                          ).then_inc(s_hid, 1)

            def layer2(c, p):
                pe.wait_ge(s_hids, c + 2)
                pe.wait_ge(s_x1, c + 1)
                for b in range(CH):
                    ins = t_.matmul(banks[4][:, b * D:(b + 1) * D], hids[p][:, b * P:(b + 1) * P], w2_sb[:, :],
                                    start=True, stop=True)
                ins.then_inc(s_o, 1)

            transposes(0, 0)
            with pe.Fori(0, NC // 2 - 1) as it:
                for k in range(2):
                    c = it * 2 + k
                    layer1(c, k)
                    transposes(c + 1, 1 - k)
                    layer2(c, k)
            for c in (NC - 2, NC - 1):
                layer1(c, c % 2)
                if c + 1 < NC:
                    transposes(c + 1, 1)
                layer2(c, c % 2)

            def transposes2(c):
                pe.wait_ge(s_h2, c + 1)
                pe.wait_ge(s_trs2, c + 1)
                for b in range(CH):
                    ins = t_.transpose(banks[b // 4][:, (b % 4) * P:(b % 4 + 1) * P], h2s[c % 2][:, b * P:(b + 1) * P],
                                       ident[:, :])
                ins.then_inc(s_tr2, 1)

            def zs(c):
                pe.wait_ge(s_trs2, c + 2)
                if c >= 1:
                    pe.wait_ge(s_z, c)
                for b in range(CH):
                    bank, col = 2 + b // 3, b % 3 * ZP
                    ins = t_.matmul(banks[bank][:, col:col + ZP], h2Ts[c % 2][:, b * P:(b + 1) * P], wz2_sb[:, :],
                                    start=True, stop=True)
                ins.then_inc(s_zp, 1)

            def z_sums(c):
                pe.wait_ge(s_z, c + 1)
                for b in range(c * CZ, (c + 1) * CZ):
                    ins = t_.matmul(banks[6][0:2, 0:D], cnt_sb[:, :, b], z_sb[:, b, 0:D], start=(b == 0),
                                    stop=(b == NB - 1))
                return ins

            transposes2(0)
            transposes2(1)
            for c in range(NB // CZ):
                zs(c)
                if c >= 1:
                    z_sums(c - 1)
                if c + 2 < NB // CZ:
                    transposes2(c + 2)
            z_sums(NB // CZ - 1).then_inc(s_psum, 1)
            pe.wait_ge(s_part, 1)
            for a in range(2):
                ins = t_.matmul(banks[5][:, a * D:(a + 1) * D], ident[0:2, a:a + 1].to_broadcast([2, P]),
                                mabs[0:2, 0, :], start=True, stop=True)
            ins.then_inc(s_psum, 1)
            for u in range(4):
                pe.wait_ge(s_csq, u + 1)
                pe.wait_ge(s_cw3, u + 1)
                a, h = u // 2, u % 2
                for b in range(n_half):
                    at = h * n_half + b
                    ins = t_.matmul(banks[5 + 2 * a][:, 0:2 * D], cnt_sb[:, a, at:at + 1].to_broadcast([P, P]),
                                    pows[h][:, b, :, :].rearrange("p k d -> p (k d)"),
                                    start=(at == 0), stop=(at == NB - 1))
                ins.then_inc(s_csum, 1)
            pe.wait_ge(s_win, 1)
            far = pe.snap(pe.value_load(far_i[0:1, 0:1], min_val=0, max_val=1))

            def maxima(it, q):
                m = it * U + q
                pe.wait_ge(f_gmax, m + 1)
                t_.transpose(banks[0][0:W, 0:P], f_top[:, :], ident[:, :]).then_inc(f_gT, 1)
                pe.wait_ge(f_mloc, m + 1)
                t_.matmul(banks[1][:, 0:W], f_max[0:W, q % SL:q % SL + 1].to_broadcast([W, P]), ident[0:W, 0:W],
                          start=True, stop=True).then_inc(f_mrow, 1)

            def weighted_sums(it, q):
                pe.wait_ge(f_exp, it * U + q + 1)
                for g in range(G):
                    ins = t_.matmul(banks[2 + q % 2][0:W, 0:RW], f_probs[:, q % 2, g, :], zg[:, q % SL, g, :],
                                    start=(g == 0), stop=(g == G - 1))
                ins.then_inc(s_zfree, 1)

            with pe.If(far == 0):
                for q in range(U):
                    maxima(0, q)
                    if q >= 1:
                        weighted_sums(0, q - 1)
                with pe.Fori(1, NM // U) as it:
                    for q in range(U):
                        maxima(it, q)
                        weighted_sums(it, q - 1)
                weighted_sums(NM // U, -1)
            with pe.If(far == 1):
                with pe.Fori(0, NM // SL) as it:
                    for s in range(SL):
                        c0 = pe.snap(pe.value_load(cum_i[0:1, bass.ds(it * SL + s, 1)], min_val=0, max_val=NM * NB))
                        c1 = pe.snap(pe.value_load(cum_i[0:1, bass.ds(it * SL + s + 1, 1)], min_val=1, max_val=NM * NB))
                        with pe.Fori(c0, c1) as i:
                            pe.wait_ge(s_gmax, i + 1)
                            t_.transpose(banks[0][:, 0:P], gmax[:, :], ident[:, :]).then_inc(s_gT, 1)
                            pe.wait_ge(s_mnew, i + 1)
                            t_.matmul(banks[1][:, 0:P], mnew[:, 0:1].to_broadcast([P, P]), ident[:, :], start=True, stop=True
                                      ).then_inc(s_mrow, 1)
                            pe.wait_ge(s_exp, i + 1)
                            for g in range(G):
                                ins = t_.matmul(banks[2][:, 0:RW], big_a[:, g, :], zg[:, s, g, :], start=(g == 0),
                                                stop=(g == G - 1))
                            ins.then_inc(s_agg1, 1)

        @block.vector
        def _(dve):
            v_ = nc.vector
            ch = Chain(dve, s_dve)
            v_.memset(work[:, 0:zero_w], 0.0).then_inc(s_work, 1)
            v_.memset(x_sb[P - 32:P, REST:NB, :], 0.0).then_inc(s_work, 1)
            dve.sem_inc(s_same, 4)
            dve.sem_inc(s_ysb, 2)
            dve.sem_inc(s_idx, 1)
            dve.sem_inc(s_room, 2)
            dve.sem_inc(s_y, 2)
            dve.sem_inc(s_oh_used, 2)
            def wide(a, n):
                return a.unsqueeze(2).to_broadcast([P, NB, n])

            def layernorm_stats(n, xs, sq):
                ch(v_.tensor_reduce(mean_sb[:, :], xs, X_AXIS, ALU.add))
                ch(v_.tensor_scalar(mean_sb[:, :], mean_sb[:, :], 1.0 / D, None, ALU.mult))
                v_.tensor_tensor(d_sb[:, :, :], xs, wide(mean_sb[:, :], D), ALU.subtract).then_inc(s_dsub, 1)
                dve.wait_ge(s_sq, n)
                ch(v_.tensor_reduce(var_sb[:, :], sq, X_AXIS, ALU.add))
                v_.tensor_scalar(var_sb[:, :], var_sb[:, :], 1.0 / D, EPS, ALU.mult, ALU.add).then_inc(s_vv, 1)
                dve.wait_ge(s_std, n)
                v_.reciprocal(rstd_sb[:, :], var_sb[:, :]).then_inc(s_rstd, 1)
                dve.wait_ge(s_rstd, n)
                dve.wait_ge(s_dsub, n)

            for k, s in ((0, s_src), (1, s_dst)):
                dve.wait_ge(s, 48)
                v_.tensor_copy(row_f[0:MH, k, :, :], row_buf[0:MH, k, :, :]).then_inc(s_rowf, 1)

            def turned(k, to):
                dve.wait_ge(s_turn, k + 1)
                for b in range(4):
                    h, g = b // 2, b % 2 * 4
                    ins = v_.tensor_copy(
                        to[:, h * MH * G:(h + 1) * MH * G].rearrange("p (m g) -> p g m", g=G)[:, g:g + 4, :],
                        banks[b][:, 0:4 * MH].rearrange("p (g m) -> p g m", g=4))
                ins.then_inc(s_turned, 1)
                dve.wait_ge(s_turned, k + 1)

            turned(0, ee_sb)
            ch(v_.tensor_copy(src_i[:, 0:NT], ee_sb[:, :]))
            ch(v_.tensor_scalar(src_rest[:, :], src_i[:, 0:NT], P - 1, None, ALU.bitwise_and))
            ch(v_.memset(srclo_all[:, NT:NT + G], 0.0))
            ch(v_.memset(srchi_all[:, NT:NT + G], 0.0))
            ch(v_.tensor_copy(srclo_all[:, 0:NT], src_rest[:, :]))
            ch(v_.tensor_tensor(srchi_all[:, 0:NT], ee_sb[:, :], srclo_all[:, 0:NT], ALU.subtract))
            dve.wait_ge(s_bits, 1)
            ch(v_.tensor_scalar(bits[:, :], bits[:, :], 23, None, ALU.logical_shift_left))
            for s in range(2):
                v_.tensor_copy(ea_sb[:, s, :, AW:EW], bits[:, 0:1].bitcast(F32).unsqueeze(1).to_broadcast([P, G, 1])
                               ).then_inc(s_pos, 1)
            ch(v_.tensor_scalar(threshold[:, :], bits[:, 1:2].bitcast(F32), 1.5, None, ALU.mult))

            turned(1, dst_f)
            ch(v_.tensor_scalar(dst_i[:, :], dst_f[:, :], 1.0 / NB, None, ALU.mult))
            ch(v_.tensor_copy(dst_p[:, 0:NT], dst_i[:, :]))
            ch(v_.scalar_tensor_tensor(out=dst_j[:, 0:NT], in0=dst_p[:, 0:NT], scalar=-float(NB), in1=dst_f[:, :],
                                       op0=ALU.mult, op1=ALU.add))
            ch(v_.tensor_scalar(ee_sb[:, :], dst_j[:, 0:NT], 0.0, None, ALU.is_lt))
            ch(v_.tensor_tensor(dst_p[:, 0:NT], dst_p[:, 0:NT], ee_sb[:, :], ALU.subtract))
            ch(v_.scalar_tensor_tensor(out=dst_j[:, 0:NT], in0=ee_sb[:, :], scalar=float(NB), in1=dst_j[:, 0:NT],
                                       op0=ALU.mult, op1=ALU.add))
            ch(v_.memset(dst_p[0:DUP, (NM - 1) * G:NT], -1.0))
            ch(v_.memset(dst_p[:, NT:NT + G], -1.0))
            ch(v_.memset(dst_j[:, NT:NT + G], -1.0))
            dve.wait_ge(s_x, 32)
            layernorm_stats(1, x_sb[:, :, :], z_sb[:, :, 0:D])
            dve.wait_ge(s_w, 16 * 11)
            def stage(s, m, col):
                v_.tensor_scalar(src_lo[:, s, :], srclo_all[:, bass.ds(col, G)], 0.0, None, ALU.add)
                v_.tensor_scalar(src_hi[:, s, :], srchi_all[:, bass.ds(col, G)], 0.0, None, ALU.add)
                v_.tensor_tensor(srcf[:, s, :], srclo_all[:, bass.ds(col, G)], srchi_all[:, bass.ds(col, G)], ALU.add
                                 ).then_inc(s_stage, 1)
                dve.wait_ge(s_stage, m + 1)

            def onehots(h, n, col):
                dve.wait_ge(s_oh_used, n + 1)
                v_.tensor_tensor(ohp[:, h, :, :], iota_f[:, :].unsqueeze(1).to_broadcast([P, 4, P]),
                                 dst_p[:, bass.ds(col, 4)].unsqueeze(2).to_broadcast([P, 4, P]), ALU.is_equal)
                v_.tensor_tensor(ohj[:, h, :, :], iota_f[:, 0:NB].unsqueeze(1).to_broadcast([P, 4, NB]),
                                 dst_j[:, bass.ds(col, 4)].unsqueeze(2).to_broadcast([P, 4, NB]),
                                 ALU.is_equal).then_inc(s_oh, 1)

            stage(0, 0, 0)
            onehots(0, 0, 0)
            with dve.Fori(0, NM // 2) as it:
                c1 = Chain(dve, s_dve1, it * 9)
                for q in range(4):
                    s, h = divmod(q, 2)
                    n = it * 4 + q
                    half = srcf[:, s, 4 * h:4 * h + 4]
                    dve.wait_ge(s_srcb, n + 1)
                    dve.wait_ge(s_y, n + 1)
                    v_.tensor_tensor(same[:, h, :, :], banks[q][:, :].rearrange("p (j e) -> p j e", j=4),
                                     half.unsqueeze(2).to_broadcast([P, 4, P]), ALU.is_equal).then_inc(s_same, 1)
                    if h == 0:
                        dve.wait_ge(s_idx, n + 1)
                        stage((s + 1) % 2, it * 2 + s + 1, it * (2 * G) + (s + 1) * G)
                    onehots((h + 1) % 2, n + 1, it * (2 * G) + 4 * (q + 1))
                    c1(v_.tensor_scalar(todummy[:, s, 4 * h:4 * h + 4], half, -1.0, dummy_row[:, 0:1],
                                        ALU.mult, ALU.add))
                    dve.wait_ge(s_ysb, n + 3)
                    weight = y_sb[:, s, 4 * h * EW:4 * (h + 1) * EW].rearrange("p (j c) -> p j c", j=4)[:, :, AW]
                    c1(v_.scalar_tensor_tensor(out=todummy[:, s, 4 * h:4 * h + 4], in0=weight,
                                               scalar=threshold[:, 0:1], in1=todummy[:, s, 4 * h:4 * h + 4],
                                               op0=ALU.is_ge, op1=ALU.mult))
                    dve.wait_ge(s_room, n + 1)
                    v_.tensor_tensor(idx[:, s, 4 * h:4 * h + 4], todummy[:, s, 4 * h:4 * h + 4], half, ALU.add
                                     ).then_inc(s_idx, 1)
                cols = bass.ds(it * (2 * G), 2 * G)
                v_.scalar_tensor_tensor(out=d_sb[:, bass.ds(it, 1), :], in0=d_sb[:, bass.ds(it, 1), :], scalar=0.0,
                                        in1=rstd_sb[:, bass.ds(it, 1)].unsqueeze(2).to_broadcast([P, 1, D]),
                                        op0=ALU.max, op1=ALU.mult)
                v_.tensor_tensor(x_sb[:, bass.ds(it, 1), :], x_sb[:, bass.ds(it, 1), :], b2_sb[:, :].unsqueeze(1),
                                 ALU.add)
                v_.tensor_reduce(hi_all[:, bass.ds(it * 2, 2)], dst_f[:, cols].rearrange("p (m g) -> p m g", g=G),
                                 X_AXIS, ALU.max)
                c1(v_.tensor_reduce(lo_all[:, bass.ds(it * 2, 2)], dst_f[:, cols].rearrange("p (m g) -> p m g", g=G),
                                    X_AXIS, ALU.min))

            v_.tensor_scalar(lo_all[:, :], lo_all[:, :], -1.0, None, ALU.mult).then_inc(s_neg, 1)
            dve.wait_ge(s_prep, 1)
            ch(v_.memset(wz2_sb[:, :], 0.0))
            v_.tensor_copy(wz2_sb[0:D, 0:D + 2], banks[7][0:D, 0:D + 2])
            v_.tensor_copy(wz2_sb[D:P, D + 2:ZP], banks[7][0:D, 0:D + 2])
            v_.tensor_copy(q_sb[:, :], banks[7][:, q_at:r_at])
            v_.tensor_copy(r_sb.rearrange("p a d -> p (a d)"), banks[7][:, r_at:v_at])
            v_.tensor_copy(v_sb.rearrange("p a d -> p (a d)"), banks[7][:, v_at:v_at + 4 * D]).then_inc(s_prep_sb, 1)
            dve.wait_ge(s_prep_sb, 1)
            dve.wait_ge(s_e2, 16 * (NM // 2 + 1))
            ch(v_.tensor_scalar(ee_sb[:, :], e2_sb[:, :, 0], q_sb[:, 0:1], None, ALU.mult))
            ch(v_.scalar_tensor_tensor(out=ee_sb[:, :], in0=e2_sb[:, :, 1], scalar=q_sb[:, 1:2], in1=ee_sb[:, :],
                                       op0=ALU.mult, op1=ALU.add))
            ch(v_.memset(ee_sb[0:DUP, (NM - 1) * G:NT], OFF))

            dve.wait_ge(s_cnt, 1)
            ch(v_.tensor_copy(cnt_sb[:, 1, :], banks[6][:, 0:NB]))
            dve.wait_ge(s_ysb, 2 * NM + 2)
            for k in range(G):
                dve.wait_ge(s_tab[k], 16 * NM)
            dve.sem_inc(s_h, 1)
            dve.sem_inc(s_agg, 2)
            for free in (s_trs, s_hids, s_x1, s_var, s_trs2, s_zp):
                dve.sem_inc(free, 1)

            def table_sums(c, it, p):
                rows = work[:, p * G * CH * AW:(p + 1) * G * CH * AW].rearrange("p (k b c) -> p b c k", k=G, b=CH)
                dve.wait_ge(s_acc[p], it * (16 * G) + 16 * G)
                if not (isinstance(c, int) and c < 2):
                    dve.wait_ge(s_tr, c - 1)
                v_.tensor_reduce(cats[p].rearrange("p (b f) -> p b f", b=CH)[:, :, D:2 * D], rows[:, :, 0:D, :],
                                 X_AXIS, ALU.add).then_inc(s_cat, 1)
                v_.tensor_reduce(cnt_sb[:, 0, chunk(c)], rows[:, :, D, :], X_AXIS, ALU.add).then_inc(s_agg, 1)

            def new_x(c):
                link = Chain(dve, s_dve3, c)
                xc, mean = x_sb[:, chunk(c), :], mean_sb[:, chunk(c)]
                dve.wait_ge(s_o, c + 1)
                v_.tensor_tensor(xc, xc, banks[4][:, 0:CH * D].rearrange("p (b d) -> p b d", b=CH), ALU.add
                                 ).then_inc(s_x1, 1)
                dve.wait_ge(s_x1, c + 2)
                link(v_.tensor_reduce(mean, xc, X_AXIS, ALU.add))
                dve.wait_ge(s_cath, c + 1)
                v_.scalar_tensor_tensor(out=d_sb[:, chunk(c), :], in0=mean.unsqueeze(2).to_broadcast([P, CH, D]),
                                        scalar=-1.0 / D, in1=xc, op0=ALU.mult, op1=ALU.add).then_inc(s_d2, 1)

            def variance(c):
                dve.wait_ge(s_sq2, c + 1)
                v_.tensor_reduce(var_sb[:, chunk(c)], sq_buf[:, :, :], X_AXIS, ALU.add).then_inc(s_var, 1)

            table_sums(0, 0, 0)
            table_sums(1, 0, 1)
            table_sums(2, 1, 0)
            new_x(0)
            with dve.Fori(0, NC // 2 - 2) as it:
                table_sums(it * 2 + 3, it + 1, 1)
                new_x(it * 2 + 1)
                variance(it * 2)
                table_sums(it * 2 + 4, it + 2, 0)
                new_x(it * 2 + 2)
                variance(it * 2 + 1)
            for c in range(NC - 3, NC):
                if c + 2 < NC:
                    table_sums(c + 2, (c + 2) // 2, c % 2)
                new_x(c)
                variance(c - 1)
            variance(NC - 1)
            dve.wait_ge(s_var, NC + 1)
            v_.tensor_scalar(var_sb[:, :], var_sb[:, :], 1.0 / D, EPS, ALU.mult, ALU.add).then_inc(s_vv, 1)
            dve.wait_ge(s_std, 2)
            ch(v_.reciprocal(rstd_sb[:, :], var_sb[:, :]))
            dve.wait_ge(s_d2, NC)

            def h2(c):
                at = slice(c * CZ, (c + 1) * CZ)
                if c >= 2:
                    dve.wait_ge(s_tr2, c - 1)
                v_.scalar_tensor_tensor(out=h2s[c % 2].rearrange("p (b f) -> p b f", b=CZ), in0=d_sb[:, at, :],
                                        scalar=0.0, in1=rstd_sb[:, at].unsqueeze(2).to_broadcast([P, CZ, D]),
                                        op0=ALU.max, op1=ALU.mult).then_inc(s_h2, 1)

            def z_out(c):
                dve.wait_ge(s_zp, c + 2)
                for k in range(3):
                    n = min(3, CH - 3 * k) * 2
                    at = c * CZ + 6 * k
                    ins = v_.tensor_copy(z_sb[:, at:at + n, :],
                                         banks[2 + k][:, 0:n * (D + 2)].rearrange("p (b f) -> p b f", b=n))
                ins.then_inc(s_z, 1)

            dve.wait_ge(s_agg, NC + 2)
            h2(0)
            h2(1)
            for c in range(NB // CZ):
                if c + 2 < NB // CZ:
                    h2(c + 2)
                z_out(c)
            ch(v_.memset(src_i[:, NT:NT + SL * G], 0))
            for s in range(SL):
                v_.tensor_copy(idx[:, s, :], src_i[:, s * G:(s + 1) * G]).then_inc(s_zg_used, 1)
            dve.sem_inc(s_zfree, SL)
            dve.wait_ge(s_psum, 1)
            v_.tensor_scalar(mabs[0:2, 0, :], banks[6][0:2, 0:D], 1.0 / EDGES, None, ALU.mult).then_inc(s_part, 1)
            dve.wait_ge(s_psum, 2)
            ch(v_.tensor_copy(sums.rearrange("p a d -> p (a d)"), banks[5][:, 0:2 * D]))

            def differences(u):
                a, at = u // 2, slice(u % 2 * n_half, (u % 2 + 1) * n_half)
                if u >= 2:
                    dve.wait_ge(s_csum, u - 1)
                v_.tensor_tensor(pows[u % 2][:, :, 1, :], z_sb[:, at, 0:D],
                                 sums[:, a, :].unsqueeze(1).to_broadcast([P, n_half, D]), ALU.subtract
                                 ).then_inc(s_cd, 1)

            def cubes(u):
                buf = pows[u % 2]
                dve.wait_ge(s_csq, u + 1)
                v_.tensor_tensor(buf[:, :, 1, :], buf[:, :, 1, :], buf[:, :, 0, :], ALU.mult).then_inc(s_cw3, 1)

            differences(0)
            differences(1)
            cubes(0)
            cubes(1)
            for u in (2, 3):
                differences(u)
                cubes(u)
            dve.wait_ge(s_range, 2)
            ch(v_.tensor_scalar(base_i[:, :], lo_all[:, :], -1.0, None, ALU.mult))
            ch(v_.tensor_tensor(tmp_i[:, :], hi_all[:, :], lo_all[:, :], ALU.add))
            ch(v_.tensor_scalar(tmp_i[:, :], tmp_i[:, :], P.bit_length() - 1, None, ALU.arith_shift_right))
            ch(v_.tensor_copy(tmp_m[:, :], tmp_i[:, :]))
            ch(v_.tensor_scalar(tmp_m[:, :], tmp_m[:, :], 1.0, None, ALU.add))
            ch(v_.tensor_tensor(tmp_m2[:, :], hi_all[:, :], lo_all[:, :], ALU.add))
            ch(v_.tensor_reduce(far_f[:, :], tmp_m2[:, :], X_AXIS, ALU.max))
            ch(v_.tensor_scalar(far_i[:, :], far_f[:, :], float(W), None, ALU.is_ge))
            ch(v_.memset(cum_f[:, 0:1], 0.0))
            ch(v_.tensor_tensor_scan(cum_f[:, 1:NM + 1], ones_f[:, 0:1].to_broadcast([P, NM]), tmp_m[:, :], 0.0, ALU.mult, ALU.add))
            v_.tensor_copy(cum_i[:, :], cum_f[:, :]).then_inc(s_win, 1)
            dve.wait_ge(s_win, 1)

            for a in range(2):
                dve.wait_ge(s_csum, 2 * a + 2)
                ch(v_.tensor_scalar(mom[:, a::2, :], banks[5 + 2 * a][:, 0:2 * D].rearrange("p (k d) -> p k d", k=2),
                                    1.0 / EDGES, None, ALU.mult))

            def flat(a):
                return a.rearrange("p a d -> p (a d)")

            ch(v_.tensor_scalar(flat(mabs), flat(mom), -1.0, None, ALU.mult))
            ch(v_.tensor_tensor(flat(mabs), flat(mabs), flat(mom), ALU.max))
            ch(v_.tensor_scalar(flat(msign), flat(mom), 0.0, None, ALU.is_lt))
            ch(v_.scalar_tensor_tensor(out=flat(msign), in0=flat(mom), scalar=0.0, in1=flat(msign), op0=ALU.is_gt,
                                       op1=ALU.subtract))
            v_.tensor_scalar(flat(mabs), flat(mabs), 1e-37, None, ALU.max).then_inc(s_mom, 1)
            dve.wait_ge(s_root, 1)
            ch(v_.tensor_tensor(flat(mabs), flat(mabs), flat(msign), ALU.mult))
            ch(v_.tensor_tensor(flat(mabs), flat(mabs), flat(v_sb), ALU.mult))
            ch(v_.tensor_reduce(c_sb[:, :], flat(mabs), X_AXIS, ALU.add))
            v_.tensor_scalar(t_sb[:, :], z_sb[:, :, D + 1], c_sb[:, 0:1], None, ALU.add).then_inc(s_t, 1)
            far = dve.snap(dve.value_load(far_i[0:1, 0:1], min_val=0, max_val=1))

            def masks(it, q):
                m, col = it * U + q, (it * U + q) * G
                link = Chain(dve, f_link[0], m * 2)
                dve.wait_ge(s_zg[q % SL], (it * 2 + q // SL) * (16 * G) + 16 * G)
                v_.tensor_scalar(idx[:, q % SL, :], src_i[:, bass.ds(col + SL * G, G)], 0.0, None, ALU.add
                                 ).then_inc(s_zg_used, 1)
                v_.tensor_tensor(f_s[:, q % 2, :], zg[:, q % SL, :, D], ee_sb[:, bass.ds(col, G)], ALU.add)
                v_.tensor_scalar(zg[:, q % SL, :, ZW + 1:RW], e2_sb[:, bass.ds(col, G), :], 0.0, None, ALU.add)
                link(v_.tensor_scalar(f_dloc[:, :], dst_f[:, bass.ds(col, G)], lo_all[:, bass.ds(m, 1)], None, ALU.add))
                mask = f_masks[:, q % 2, :, :]
                link(v_.tensor_tensor(mask, iota_f[:, 0:W].unsqueeze(1).to_broadcast([P, G, W]),
                                      f_dloc[:, :].unsqueeze(2).to_broadcast([P, G, W]), ALU.not_equal))
                dve.wait_ge(f_trow[q % 2], it * (8 * U) + (q // 2 + 1) * 16)
                v_.scalar_tensor_tensor(out=mask, in0=mask, scalar=OFF,
                                        in1=f_t[:, q % 2, :].unsqueeze(1).to_broadcast([P, G, W]),
                                        op0=ALU.mult, op1=ALU.add).then_inc(f_mask, 1)

            def new_maxima(it, q):
                m, k = it * U + q, q % SL
                link = Chain(dve, f_link[1], m * 3)
                dve.wait_ge(f_rows, m * 16 + 16)
                link(v_.tensor_tensor(f_new[0:W, :], f_max[0:W, k:k + 1], tab[0:W, TW - 1:TW], ALU.max))
                v_.tensor_tensor(f_ratio[0:W, 0:1], tab[0:W, TW - 1:TW], f_new[0:W, :], ALU.subtract)
                v_.tensor_tensor(f_ratio[0:W, 1:2], f_max[0:W, k:k + 1], f_new[0:W, :], ALU.subtract
                                 ).then_inc(f_diff, 1)
                dve.wait_ge(f_diff, m + 1)
                link(v_.tensor_scalar(tab[0:W, TW - 1:TW], f_new[0:W, :], 0.0, None, ALU.add))
                dve.wait_ge(f_resc, m + 1)
                link(v_.tensor_scalar(tab[0:W, 0:TW - 1], tab[0:W, 0:TW - 1], f_fact[0:W, 0:1], None, ALU.mult))

            def less_maxima(it, q):
                m = it * U + q
                dve.wait_ge(f_mrow, m + 1)
                scores = f_scores[:, q % 2, :, :]
                v_.tensor_tensor(scores, scores, banks[1][:, 0:W].unsqueeze(1).to_broadcast([P, G, W]), ALU.subtract
                                 ).then_inc(f_sub, 1)

            def scores_top(it, q):
                m = it * U + q
                link = Chain(dve, f_link[2], m)
                dve.wait_ge(f_lin, m + 1)
                scores = f_scores[:, q % 2, :, :]
                link(v_.scalar_tensor_tensor(out=scores, in0=scores, scalar=SLOPE, in1=scores, op0=ALU.mult,
                                             op1=ALU.max))
                v_.tensor_reduce(f_top[:, :], scores.rearrange("p g n -> p n g"), X_AXIS, ALU.max).then_inc(f_gmax, 1)

            def window_sums(it, q):
                m = it * U + q
                link = Chain(dve, f_link[4], m * 2)
                window = banks[2 + q % 2]
                dve.wait_ge(s_zfree, m + SL + 1)
                link(v_.scalar_tensor_tensor(out=f_v[0:W, 0:D], in0=r_sb[0:W, 0, :], scalar=window[0:W, ZW + 1:ZW + 2],
                                             in1=window[0:W, 0:D], op0=ALU.mult, op1=ALU.add))
                v_.tensor_scalar(f_v[0:W, D:TW - 1], window[0:W, D:TW - 1], 0.0, None, ALU.add)
                link(v_.scalar_tensor_tensor(out=f_v[0:W, 0:D], in0=r_sb[0:W, 1, :], scalar=window[0:W, ZW + 2:RW],
                                             in1=f_v[0:W, 0:D], op0=ALU.mult, op1=ALU.add))

            def merge(it, q):
                v_.scalar_tensor_tensor(out=tab[0:W, 0:TW - 1], in0=f_v[0:W, :], scalar=f_fact[0:W, 1:2],
                                        in1=tab[0:W, 0:TW - 1], op0=ALU.mult, op1=ALU.add).then_inc(f_tabn, 1)

            def segment_maxima(it, q):
                m = it * U + q
                link = Chain(dve, f_link[3], m)
                dve.wait_ge(f_gT, m + 1)
                link(v_.tensor_reduce(f_max[0:W, q % SL:q % SL + 1], banks[0][0:W, 0:P], X_AXIS, ALU.max))
                v_.tensor_scalar(f_max[0:W, q % SL:q % SL + 1], f_max[0:W, q % SL:q % SL + 1], FLOOR, None, ALU.max).then_inc(f_mloc, 1)

            def dve_step(it, q, first=False):
                masks(it, q)
                if not first or q >= 1:
                    less_maxima(it, q - 1)
                if not first or q >= 2:
                    window_sums(it, q - 2)
                scores_top(it, q)
                if not first or q >= 2:
                    new_maxima(it, q - 2)
                    merge(it, q - 2)
                segment_maxima(it, q)

            with dve.If(far == 0):
                for q in range(U):
                    dve_step(0, q, first=True)
                with dve.Fori(1, NM // U) as it:
                    for q in range(U):
                        dve_step(it, q)
                last = NM // U
                less_maxima(last, -1)
                for q in (-2, -1):
                    dve.wait_ge(f_tabn, NM + q)
                    window_sums(last, q)
                    new_maxima(last, q)
                    merge(last, q)
            with dve.If(far == 1):
                with dve.Fori(0, NM // SL) as it:
                    for s in range(SL):
                        m = it * SL + s
                        col = it * (SL * G) + s * G
                        c0 = dve.snap(dve.value_load(cum_i[0:1, bass.ds(m, 1)], min_val=0, max_val=NM * NB))
                        c1 = dve.snap(dve.value_load(cum_i[0:1, bass.ds(m + 1, 1)], min_val=1, max_val=NM * NB))
                        cm = Chain(dve, s_dve4, m * 3)
                        dve.wait_ge(s_zg[s], it * (16 * G) + 16 * G)
                        cm(v_.tensor_tensor(s_sb[:, :], zg[:, s, :, D], ee_sb[:, bass.ds(col, G)], ALU.add))
                        cm(v_.tensor_scalar(zg[:, s, :, ZW + 1:RW], e2_sb[:, bass.ds(col, G), :], 0.0, None, ALU.add))
                        cm(v_.tensor_scalar(dloc[:, :], dst_f[:, bass.ds(col, G)], lo_all[:, bass.ds(m, 1)], None, ALU.add))
                        dve.sem_inc(s_held[2], 1)
                        with dve.Fori(c0, c1) as i:
                            cw = Chain(dve, s_dve5, i * 9)
                            cw(v_.tensor_tensor(big_a[:, :, :], iota_f[:, :].unsqueeze(1).to_broadcast([P, G, P]),
                                                dloc[:, :].unsqueeze(2).to_broadcast([P, G, P]), ALU.not_equal))
                            dve.wait_ge(s_rows, i * 32 + 32)
                            v_.scalar_tensor_tensor(out=big_a[:, :, :], in0=big_a[:, :, :], scalar=OFF,
                                                    in1=trow[:, :].unsqueeze(1).to_broadcast([P, G, P]),
                                                    op0=ALU.mult, op1=ALU.add).then_inc(s_mask, 1)
                            dve.wait_ge(s_lin, i + 1)
                            cw(v_.scalar_tensor_tensor(out=big_b[:, :, :], in0=big_b[:, :, :], scalar=SLOPE,
                                                       in1=big_b[:, :, :], op0=ALU.mult, op1=ALU.max))
                            v_.tensor_reduce(gmax[:, :], big_b.rearrange("p g n -> p n g"), X_AXIS, ALU.max
                                             ).then_inc(s_gmax, 1)
                            dve.wait_ge(s_gT, i + 1)
                            cw(v_.tensor_reduce(mloc[:, :], banks[0][:, 0:P], X_AXIS, ALU.max))
                            v_.tensor_tensor(mnew[:, :], mloc[:, :], tab[:, TW - 1:TW], ALU.max).then_inc(s_mnew, 1)
                            dve.wait_ge(s_mnew, i + 1)
                            cw(v_.tensor_tensor(mloc[:, :], tab[:, TW - 1:TW], mnew[:, :], ALU.subtract))
                            cw(v_.tensor_scalar(tab[:, TW - 1:TW], mnew[:, :], 0.0, None, ALU.add))
                            dve.wait_ge(s_mrow, i + 1)
                            v_.tensor_tensor(big_b[:, :, :], big_b[:, :, :],
                                             banks[1][:, 0:P].unsqueeze(1).to_broadcast([P, G, P]), ALU.subtract
                                             ).then_inc(s_sub, 1)
                            cw(v_.tensor_scalar(dloc[:, :], dloc[:, :], -float(P), None, ALU.add))
                            dve.wait_ge(s_agg1, i + 1)
                            cw(v_.tensor_scalar(f_e[:, :], banks[2][:, ZW + 1:RW], 0.0, None, ALU.add))
                            cw(v_.scalar_tensor_tensor(out=tab[:, 0:TW - 1], in0=tab[:, 0:TW - 1],
                                                       scalar=rescale[:, 0:1], in1=banks[2][:, 0:TW - 1],
                                                       op0=ALU.mult, op1=ALU.add))
                            cw(v_.scalar_tensor_tensor(out=tab[:, 0:D], in0=r_sb[:, 0, :], scalar=f_e[:, 0:1],
                                                       in1=tab[:, 0:D], op0=ALU.mult, op1=ALU.add))
                            v_.scalar_tensor_tensor(out=tab[:, 0:D], in0=r_sb[:, 1, :], scalar=f_e[:, 1:2],
                                                    in1=tab[:, 0:D], op0=ALU.mult, op1=ALU.add).then_inc(s_tabn, 1)
                        v_.tensor_scalar(idx[:, s, :], src_i[:, bass.ds(col + SL * G, G)], 0.0, None, ALU.add
                                         ).then_inc(s_zg_used, 1)
                        dve.sem_inc(s_zfree, 1)

            rows = work[:, 0:NB * TW].rearrange("p (b c) -> p b c", c=TW)
            for c in range(NB // CZ):
                at = slice(c * CZ, (c + 1) * CZ)
                dve.wait_ge(s_fin[c], 16)
                ch(v_.tensor_scalar(mean_sb[:, at], rows[:, at, ZW], 1e-30, None, ALU.max))
                ch(v_.reciprocal(rstd_sb[:, at], mean_sb[:, at]))
                ch(v_.tensor_tensor(rows[:, at, 0:D], rows[:, at, 0:D],
                                    rstd_sb[:, at].unsqueeze(2).to_broadcast([P, CZ, D]), ALU.mult))
                v_.tensor_tensor(x_sb[:, at, :], x_sb[:, at, :], rows[:, at, 0:D], ALU.add).then_inc(s_res, 1)


_INS = ['x', 'src', 'dst', 'edge_attr_2', 'edge_attr_64', 'L0_gnn_W1', 'L0_gnn_b1', 'L0_gnn_W2', 'L0_gnn_b2',
        'L1_gnn_W_fc', 'L1_gnn_W_attn', 'L1_gnn_W_edge', 'L1_gnn_W_e2n', 'L1_gnn_W_m1', 'L1_gnn_W_m2']


def kernel(**inputs):
    import numpy as _np
    import concourse.bacc as _bacc
    from concourse import mybir as _mybir
    from concourse.bass_utils import run_bass_kernel_spmd as _run

    nc = _bacc.Bacc("TRN2", target_bir_lowering=False, num_devices=1)
    arrays, args = {}, []
    for name in _INS:
        a = _np.ascontiguousarray(inputs[name])
        arrays[f"in_{name}_dram"] = a
        args.append(nc.dram_tensor(f"in_{name}_dram", a.shape, _mybir.dt.from_np(a.dtype), kind="ExternalInput").ap())
    args.append(nc.dram_tensor("out_0_dram", (NODES, D), _mybir.dt.float32, kind="ExternalOutput").ap())
    gnn_kernel(nc, *args)
    r = _run(nc, [arrays], core_ids=[0])
    return r.results[0]["out_0_dram"]
```
